# Optimizing a Trainium2 kernel written in Bass

```python
import numpy as np
import jax
import jax.numpy as jnp

def _softmax(x, axis=-1):
    return jax.nn.softmax(x, axis=axis)

def _gelu(x):
    return jax.nn.gelu(x, approximate=True)

def _silu(x):
    return jax.nn.silu(x)

def _sigmoid(x):
    return jax.nn.sigmoid(x)

def _layernorm(x, axis=-1, eps=1e-05):
    m = jnp.mean(x, axis=axis, keepdims=True)
    v = jnp.var(x, axis=axis, keepdims=True)
    return (x - m) / jnp.sqrt(v + eps)

def _scatter_add(tgt, idx, src, axis=0):
    return tgt.at[idx].add(src)

def _segment_sum(src, seg, n):
    return jax.ops.segment_sum(src, seg, n)
kernel_name = 'mk_lm_tower_d1_tok_ids1024_r4_c0cdb6'

def setup_inputs(seed: int=0):
    np.random.seed(seed)
    _w = jnp.asarray

    def _rec_inputs():
        import jax
        import jax.numpy as jnp
        _rk = jax.random.key(seed)
        x = jax.random.randint(jax.random.fold_in(_rk, 1), (4, 1024), 0, 12564, jnp.int32)
        return x
    x = _rec_inputs()

    def _L0_tok_setup():
        import jax, jax.numpy as jnp
        import numpy as np
        VOCAB = 50257
        D_MODEL = 256
        N_BASES = 4
        B, S = (8, 2048)
        key = jax.random.key(seed)
        k1, k2, k3, k4 = jax.random.split(key, 4)
        x = jax.random.randint(k1, (B, S), 0, VOCAB, dtype=jnp.int32).astype(jnp.int64)
        coeff_weight = jax.random.normal(k2, (VOCAB, N_BASES), dtype=jnp.float32)
        base_embed_weight = jax.random.normal(k3, (N_BASES, D_MODEL), dtype=jnp.float32)
        lang_bias = jax.random.normal(k4, (N_BASES, D_MODEL), dtype=jnp.float32)
        return {'x': x, 'lang_id': 2, 'coeff_weight': coeff_weight, 'base_embed_weight': base_embed_weight, 'lang_bias': lang_bias}
    _L0_tok_all = _L0_tok_setup()
    _L0_tok_in = {k: v for k, v in _L0_tok_all.items() if k in ('coeff_weight', 'base_embed_weight', 'lang_bias')}
    del _L0_tok_all

    def _L0_attn_setup():
        import jax, jax.numpy as jnp
        import numpy as np
        import math
        B, S, D, H = (4, 512, 256, 16)
        DK = D // H
        key = jax.random.key(seed)
        ks = jax.random.split(key, 5)
        scale = 1.0 / math.sqrt(D)
        return {'x': jax.random.normal(ks[0], (B, S, D), dtype=jnp.float32), 'Wv': jax.random.normal(ks[1], (D, D), dtype=jnp.float32) * scale, 'bv': jax.random.normal(ks[2], (D,), dtype=jnp.float32) * scale, 'Wo': jax.random.normal(ks[3], (D, D), dtype=jnp.float32) * scale, 'bo': jax.random.normal(ks[4], (D,), dtype=jnp.float32) * scale}
    _L0_attn_all = _L0_attn_setup()
    _L0_attn_in = {k: v for k, v in _L0_attn_all.items() if k in ('Wv', 'bv', 'Wo', 'bo')}
    del _L0_attn_all

    def _L0_ffn_setup():
        import jax, jax.numpy as jnp
        import numpy as np
        NUM_EXPERTS = 8
        TOP_K = 2
        MOE_DIM = 512

        def _moe_forward(x, moe_router, moe_w13, moe_w2):
            b, s, d = x.shape
            x_flat = x.reshape(b * s, d)
            router_logits = jnp.einsum('td,de->te', x_flat, moe_router)
            topk_logits, topk_idx = jax.lax.top_k(router_logits, TOP_K)
            topk_weights = jax.nn.softmax(topk_logits, axis=-1).astype(x.dtype)
            tokens = x_flat.shape[0]
            expert_ids = topk_idx.reshape(tokens * TOP_K)
            dispatch_weights = topk_weights.reshape(tokens * TOP_K)
            sort_idx = jnp.argsort(expert_ids, axis=0)
            token_ids = jnp.arange(tokens * TOP_K, dtype=jnp.int32) // TOP_K
            token_ids_sort = token_ids[sort_idx]
            x_sort = x_flat[token_ids_sort]
            w_sort = dispatch_weights[sort_idx].astype(x_flat.dtype)
            group_sizes = jnp.bincount(expert_ids, length=NUM_EXPERTS).astype(jnp.int32)
            w13_out = jax.lax.ragged_dot(x_sort, moe_w13, group_sizes)
            gate, up = jnp.split(w13_out, [MOE_DIM], axis=-1)
            hidden = jax.nn.silu(gate) * up
            out_dispatch = jax.lax.ragged_dot(hidden, moe_w2, group_sizes)
            out_flat = jnp.zeros_like(x_flat).at[token_ids_sort].add(out_dispatch * w_sort[:, None], mode='drop')
            return out_flat.reshape(b, s, d)
        key = jax.random.key(seed)
        k1, k2, k3, k4 = jax.random.split(key, 4)
        B, S, D = (4, 512, 256)
        x = jax.random.normal(k1, (B, S, D), dtype=jnp.float32)
        moe_router = jax.random.normal(k2, (D, NUM_EXPERTS), dtype=jnp.float32) * 0.02
        moe_w13 = jax.random.normal(k3, (NUM_EXPERTS, D, 2 * MOE_DIM), dtype=jnp.float32) * 0.02
        moe_w2 = jax.random.normal(k4, (NUM_EXPERTS, MOE_DIM, D), dtype=jnp.float32) * 0.02
        return {'x': x, 'moe_router': moe_router, 'moe_w13': moe_w13, 'moe_w2': moe_w2}
    _L0_ffn_all = _L0_ffn_setup()
    _L0_ffn_in = {k: v for k, v in _L0_ffn_all.items() if k in ('moe_router', 'moe_w13', 'moe_w2')}
    del _L0_ffn_all
    return {'x': x, 'L0_tok_coeff_weight': _L0_tok_in['coeff_weight'], 'L0_tok_base_embed_weight': _L0_tok_in['base_embed_weight'], 'L0_tok_lang_bias': _L0_tok_in['lang_bias'], 'L0_attn_Wv': _L0_attn_in['Wv'], 'L0_attn_bv': _L0_attn_in['bv'], 'L0_attn_Wo': _L0_attn_in['Wo'], 'L0_attn_bo': _L0_attn_in['bo'], 'L0_ffn_moe_router': _L0_ffn_in['moe_router'], 'L0_ffn_moe_w13': _L0_ffn_in['moe_w13'], 'L0_ffn_moe_w2': _L0_ffn_in['moe_w2']}

def reference(x, L0_tok_coeff_weight, L0_tok_base_embed_weight, L0_tok_lang_bias, L0_attn_Wv, L0_attn_bv, L0_attn_Wo, L0_attn_bo, L0_ffn_moe_router, L0_ffn_moe_w13, L0_ffn_moe_w2):
    import jax
    import jax.numpy as jnp

    def _L0_tok_ref(x, lang_id, coeff_weight, base_embed_weight, lang_bias):
        import jax, jax.numpy as jnp
        import numpy as np
        VOCAB = 50257
        D_MODEL = 256
        N_BASES = 4
        B, S = (8, 2048)
        coeff = jax.nn.softmax(coeff_weight[x], axis=-1)
        bases = base_embed_weight + lang_bias
        scale = jnp.sqrt(jnp.asarray(bases.shape[1], dtype=bases.dtype))
        out = jnp.einsum('bsn,nd->bsd', coeff, bases) * scale
        out = out + lang_bias[lang_id] * 0.1
        return out

    def _L0_attn_ref(x, Wv, bv, Wo, bo):
        import jax, jax.numpy as jnp
        import numpy as np
        import math
        B, S, D, H = (4, 512, 256, 16)
        DK = D // H
        b, s, d = x.shape
        h, dk = (H, DK)
        p = jnp.einsum('bsd,ed->bse', x, Wv) + bv
        p = p.reshape(b, s, h, dk).transpose(0, 2, 1, 3)
        q = k = v = p
        scores = jnp.einsum('bhqd,bhkd->bhqk', q, k) / math.sqrt(dk)
        attn = jax.nn.softmax(scores, axis=-1)
        out = jnp.einsum('bhqk,bhkd->bhqd', attn, v)
        out = out.reshape(b, s, h * dk)
        return jnp.einsum('bsd,ed->bse', out, Wo) + bo

    def _L0_ffn_ref(x, moe_router, moe_w13, moe_w2):
        import jax, jax.numpy as jnp
        import numpy as np
        NUM_EXPERTS = 8
        TOP_K = 2
        MOE_DIM = 512

        def _moe_forward(x, moe_router, moe_w13, moe_w2):
            b, s, d = x.shape
            x_flat = x.reshape(b * s, d)
            router_logits = jnp.einsum('td,de->te', x_flat, moe_router)
            topk_logits, topk_idx = jax.lax.top_k(router_logits, TOP_K)
            topk_weights = jax.nn.softmax(topk_logits, axis=-1).astype(x.dtype)
            tokens = x_flat.shape[0]
            expert_ids = topk_idx.reshape(tokens * TOP_K)
            dispatch_weights = topk_weights.reshape(tokens * TOP_K)
            sort_idx = jnp.argsort(expert_ids, axis=0)
            token_ids = jnp.arange(tokens * TOP_K, dtype=jnp.int32) // TOP_K
            token_ids_sort = token_ids[sort_idx]
            x_sort = x_flat[token_ids_sort]
            w_sort = dispatch_weights[sort_idx].astype(x_flat.dtype)
            group_sizes = jnp.bincount(expert_ids, length=NUM_EXPERTS).astype(jnp.int32)
            w13_out = jax.lax.ragged_dot(x_sort, moe_w13, group_sizes)
            gate, up = jnp.split(w13_out, [MOE_DIM], axis=-1)
            hidden = jax.nn.silu(gate) * up
            out_dispatch = jax.lax.ragged_dot(hidden, moe_w2, group_sizes)
            out_flat = jnp.zeros_like(x_flat).at[token_ids_sort].add(out_dispatch * w_sort[:, None], mode='drop')
            return out_flat.reshape(b, s, d)
        return _moe_forward(x, moe_router, moe_w13, moe_w2)
    h = _L0_tok_ref(x, 2, L0_tok_coeff_weight, L0_tok_base_embed_weight, L0_tok_lang_bias)
    h = h + _L0_attn_ref(_layernorm(h, axis=-1), L0_attn_Wv, L0_attn_bv, L0_attn_Wo, L0_attn_bo)
    h = h + _L0_ffn_ref(_layernorm(h, axis=-1), L0_ffn_moe_router, L0_ffn_moe_w13, L0_ffn_moe_w2)
    return h

_drawn_inputs = setup_inputs


def setup_inputs(seed=0):
    import zlib

    import numpy as np

    out = dict(_drawn_inputs(seed))
    spreads = {}
    factors = {'L0_attn_bv': 8.0,
     'L0_attn_bo': 8.0,
     'L0_ffn_moe_router': 8.0,
     'L0_ffn_moe_w13': 8.0,
     'L0_ffn_moe_w2': 8.0}
    for name, (base, spread) in spreads.items():
        noise = np.random.default_rng([zlib.crc32(name.encode()), seed]).standard_normal(out[name].shape)
        drawn = base * np.exp(spread * noise) if base else spread * noise
        out[name] = jnp.asarray(drawn.astype(out[name].dtype))
    for name, factor in factors.items():
        out[name] = (out[name] * factor).astype(out[name].dtype)
    return out
```

```python
from contextlib import ExitStack

import concourse.bass as bass
from concourse import mybir

F32 = mybir.dt.float32
BF16 = mybir.dt.bfloat16
I32 = mybir.dt.int32
U32 = mybir.dt.uint32
ALU = mybir.AluOpType
ACT = mybir.ActivationFunctionType
X = mybir.AxisListType.X
ds = bass.ds

P = 128
NBATCH, S, D = 4, 1024, 256
T = NBATCH * S
NT = T // P
KT = S // P
H = 16
DK = D // H
NB = 4
NA = NB + 1
E, FF = 8, 512
PART = 32
NSPLIT = 6
HG = H // 4
XR0 = 64
XC0 = XR0 + NA
XROWS = XC0 + NB
NJ = D // DK
NR = S // NJ
ETILES = 2 * T // P + E
SAFE = 40.0
FREE = 1
UN = 4 * KT
EPS = 1e-5




class Parts:
    pass


class Chain:

    def __init__(self, eng, sem):
        self.eng, self.sem, self.n = eng, sem, 0

    def __call__(self, instruction):
        self.n += 1
        instruction.then_inc(self.sem, 1)
        self.eng.wait_ge(self.sem, self.n)


def newton(dve, link, out, var, t1):
    link(dve.tensor_tensor(t1, out, out, ALU.mult))
    link(dve.tensor_tensor(t1, t1, var, ALU.mult))
    link(dve.tensor_scalar(t1, t1, -0.5, 1.5, ALU.mult, ALU.add))
    link(dve.tensor_tensor(out, out, t1, ALU.mult))


def weights_phase(nc, g, ins, sem, tmp):
    PS = g.PS
    base_s, lb_s, cst_s = tmp("base_s", [NB, D]), tmp("lb_s", [NB, D]), tmp("cst_s", [NB, D])
    bt, bc, msum = tmp("bt", [NB, D]), tmp("bc", [NB, D]), tmp("msum", [NB, 2])
    wvT_s, woT_s = tmp("wvT_s", [P, 2, D]), tmp("woT_s", [P, 2, D])
    bcT, bcT_wide = tmp("bcT", [P, 2, NB]), tmp("bcT_wide", [P, 2, NB, P])
    m5T, bv_s = tmp("m5T", [P, 2, NA]), tmp("bv_s", [P, 2])
    rep, kmov = tmp("rep", [P, 2, PART]), tmp("kmov", [P, 2, H, PART])
    head_mask, mmask = tmp("head_mask", [P, 2, H]), tmp("mmask", [P, 2, H, NA])
    mod_i, mod_sel = tmp("mod_i", [P, P], I32), tmp("mod_sel", [P, P])
    m_rep, m_blk, bias_wide = tmp("m_rep", [P, H, NA]), tmp("m_blk", [P, 2, H, NJ, NB]), tmp("bias_wide", [P, H, NR])

    pool_step, const_ready, const_dve = sem("pool_step"), sem("const_ready"), sem("const_dve")
    small_in, wv_in, wo_in, ex_in = sem("small_in"), sem("wv_in"), sem("wo_in"), sem("ex_in")
    dve_step, pe_step = sem("w_dve_step"), sem("w_pe_step")
    gathered, x_in, ready = g.gathered, g.x_in, g.weights_ready

    BC, BCT, M5T, KMOV, MMASK, MREP = range(1, 7)
    copied = sem("w_copied")
    dve_out = sem("w_dve_out")

    with nc.Block() as block:
        @block.sync
        def _(sp):
            sp.dma_start(g.xi[:], ins["x_t"]).then_inc(x_in, 16)
            sp.dma_start(base_s[:], ins["bases"]).then_inc(small_in, 16)
            sp.dma_start(lb_s[:], ins["lbias"]).then_inc(small_in, 16)
            for n in range(NB):
                sp.dma_start(cst_s[n:n + 1, :], ins["lbias"][2:3, :]).then_inc(small_in, 16)
            sp.dma_start(bv_s[:], ins["bv_col"]).then_inc(small_in, 16)
            sp.dma_start(g.mg[XR0 + NB:XC0, :], ins["bv_row"]).then_inc(small_in, 16)
            sp.dma_start(wvT_s[:], ins["wvT"].rearrange("(c p) e -> p c e", p=P)).then_inc(wv_in, 16)
            sp.dma_start(woT_s[:], ins["woT"].rearrange("(c p) e -> p c e", p=P)).then_inc(wo_in, 16)
            sp.wait_ge(const_ready, 1)
            sp.dma_start(g.resid[XC0 - 1:XC0, :], ins["bo"]).then_inc(ex_in, 16)
            sp.wait_ge(dve_out, BC)
            sp.dma_start(g.resid[XC0:XROWS, :], bt[:]).then_inc(ex_in, 16)
            sp.wait_ge(ex_in, 32)

        @block.gpsimd
        def _(pool):
            step = Chain(pool, pool_step)
            pool.wait_ge(x_in, 16)
            for t in range(NT):
                pool.indirect_dma_start(g.cw[:, t, :], None, ins["coeff"],
                                        bass.IndirectOffsetOnAxis(g.xi[:, t:t + 1].bitcast(U32), 0)).then_inc(gathered, 16)
                if t == 0:
                    step(pool.memset(g.ident[:], 0.0))
                    step(pool.affine_select(g.ident[:], g.ident[:], [[-1, P]], ALU.not_equal, 1.0, 0, 1))
                    step(pool.tensor_copy(g.identb[:], g.ident[:]))
                    step(pool.memset(head_mask[:], 1.0))
                    step(pool.affine_select(head_mask[:], head_mask[:], [[P, 2], [-DK, H]], ALU.is_ge, 0.0, 0, 1))
                    step(pool.affine_select(head_mask[:], head_mask[:], [[-P, 2], [DK, H]], ALU.is_ge, 0.0, DK - 1, -1))
                    step(pool.iota(mod_i[:], [[1, P]], P, -1))
                    step(pool.memset(g.resid[:], 0.0))
                    step(pool.memset(g.kr[:], 0.0))
                    ones_at = g.kr[0:H].rearrange("p (h r) -> p h r", h=H)[:, :, 0:NSPLIT * NA]
                    ones_at = ones_at.rearrange("p h (s n) -> p h s n", n=NA)[:, :, :, NB]
                    step(pool.affine_select(ones_at, ones_at, [[-1, H], [0, NSPLIT]], ALU.not_equal, 1.0, 0, 1))
                    pool.iota(g.iota_p[:], [[0, 1]], 0, 1).then_inc(const_ready, 1)
            step(pool.memset(g.fold_sel[:], 0.0))
            for k in range(4):
                step(pool.affine_select(g.fold_sel[:, k % 2, :], g.fold_sel[:, k % 2, :], [[-1, 32]],
                                        ALU.not_equal, 1.0, -32 * k, 1))
            step(pool.memset(g.ones[:], 1.0))
            step(pool.affine_select(g.tri[:], g.ones[:], [[1, P]], ALU.is_gt, 0.0, 0, -1))
            step(pool.iota(g.iota_i[:], [[1, P]], 0, 0))
            step(pool.tensor_copy(g.iota_r[:], g.iota_i[:]))
            step(pool.iota(g.iota_i[:, 0:2], [[1, 2]], 1, 2))
            step(pool.tensor_copy(g.iota_pk[:], g.iota_i[:, 0:2]))
            pool.memset(g.akz[:], 0.0)
            pool.memset(g.va[:], 0.0).then_inc(ready, 1)

        @block.vector
        def _(dve):
            link = Chain(dve, dve_step)

            def give(instruction):
                instruction.then_inc(dve_out, 1)

            dve.wait_ge(small_in, 16 * 8)
            link(dve.tensor_tensor(base_s[:], base_s[:], lb_s[:], ALU.add))
            link(dve.tensor_scalar(cst_s[:], cst_s[:], 0.1, None, ALU.mult))
            link(dve.scalar_tensor_tensor(bt[:], base_s[:], float(D) ** 0.5, cst_s[:], ALU.mult, ALU.add))
            link(dve.reduce_sum(msum[:, 0:1], bt[:], X))
            link(dve.tensor_scalar(msum[:, 1:2], msum[:, 0:1], -1.0 / D, None, ALU.mult))
            give(dve.tensor_scalar(bc[:], bt[:], msum[:, 1:2], None, ALU.add))
            dve.wait_ge(pe_step, 1)
            give(dve.tensor_copy(bcT[:], PS[:, 0, 0:2 * NB].rearrange("p (c n) -> p c n", c=2)))
            dve.wait_ge(dve_out, BCT)
            link(dve.tensor_copy(bcT_wide[:], bcT[:].unsqueeze(3).to_broadcast([P, 2, NB, P])))
            dve.wait_ge(pe_step, 2)
            dve.tensor_copy(m5T[:, :, NB:NA], bv_s[:].unsqueeze(2))
            give(dve.tensor_copy(m5T[:, :, 0:NB], PS[:, 1, 0:2 * NB].rearrange("p (c n) -> p c n", c=2)))
            dve.wait_ge(dve_out, M5T)
            link(dve.memset(rep[:], 0.0))
            link(dve.tensor_scalar(rep[:, :, 0:NSPLIT * NA].rearrange("p c (s n) -> p c s n", n=NA),
                                   m5T[:].unsqueeze(2).to_broadcast([P, 2, NSPLIT, NA]), 1.0 / DK ** 0.5, None, ALU.mult))
            dve.wait_ge(const_ready, 1)
            for c in range(2):
                last = dve.tensor_tensor(kmov[:, c], rep[:, c].unsqueeze(1).to_broadcast([P, H, PART]),
                                         head_mask[:, c].unsqueeze(2).to_broadcast([P, H, PART]), ALU.mult)
            give(last)
            for c in range(2):
                last = dve.tensor_tensor(mmask[:, c], m5T[:, c].unsqueeze(1).to_broadcast([P, H, NA]),
                                         head_mask[:, c].unsqueeze(2).to_broadcast([P, H, NA]), ALU.mult)
            link(dve.tensor_scalar(mod_i[:], mod_i[:], DK - 1, None, ALU.bitwise_and))
            give(dve.tensor_scalar(mod_sel[:], mod_i[:], 0.0, None, ALU.is_equal))
            link(dve.tensor_scalar(g.iota_p[:], g.iota_p[:], PART - 1, None, ALU.bitwise_and))
            link(dve.tensor_copy(g.part_r[:], g.iota_p[:]))
            for col, first in ((0, 3 * NA), (1, 5 * NA)):
                dve.tensor_scalar(g.part_c[:, col:col + 1], g.part_r[:], float(first), -1.0, ALU.is_ge, ALU.mult)
            dve.wait_ge(pe_step, 3)
            dve.tensor_copy(g.mg[XR0:XR0 + NB, :], PS[XR0:XR0 + NB, 2, 0:D])
            dve.tensor_scalar(g.vb[:], PS[:, 3, 0:NB * NB], 1.0 / D, None, ALU.mult)
            dve.wait_ge(pe_step, 4)
            dve.tensor_copy(g.kr[XR0:XC0, :], PS[XR0:XC0, 4, :])
            dve.wait_ge(pe_step, 5)
            link(dve.tensor_copy(m_rep[:].rearrange("p h n -> p (h n)"), PS[:, 5, 0:H * NA]))
            for c in range(2):
                dve.tensor_tensor(m_blk[:, c], m_rep[:, :, 0:NB].unsqueeze(2).to_broadcast([P, H, NJ, NB]),
                                  head_mask[:, c].unsqueeze(1).unsqueeze(3).to_broadcast([P, H, NJ, NB]), ALU.mult)
            give(dve.tensor_copy(bias_wide[:], m_rep[:, :, NB:NA].to_broadcast([P, H, NR])))
            for k in range(KT):
                dve.wait_ge(pe_step, 6 + k)
                dve.tensor_copy(g.g_pair[:, k, :], PS[:, k % 4, 0:D])
                dve.tensor_copy(g.h_bias[:, k, :], PS[:, k % 4, D:2 * D]).then_inc(copied, 1)

        @block.tensor
        def _(pe):
            pe.wait_ge(const_ready, 1)
            pe.wait_ge(dve_out, BC)
            for c in range(2):
                last = pe.transpose(PS[:, 0, NB * c:NB * c + NB], bc[:, P * c:P * c + P], g.ident[0:NB, 0:NB])
            last.then_inc(pe_step, 1)
            pe.wait_ge(dve_out, BCT)
            pe.wait_ge(wv_in, 16)
            for c in range(2):
                for k in range(2):
                    last = pe.matmul(PS[:, 1, NB * c:NB * c + NB], wvT_s[:, k, P * c:P * c + P], bcT[:, k, :],
                                     start=k == 0, stop=k == 1)
            last.then_inc(pe_step, 1)
            for k in range(2):
                pe.matmul(PS[XR0:XR0 + NB, 2, 0:D], bcT[:, k, :], wvT_s[:, k, :], start=k == 0, stop=k == 1)
            pe.wait_ge(dve_step, 6)
            for m in range(NB):
                for k in range(2):
                    last = pe.matmul(PS[:, 3, NB * m:NB * m + NB], bcT_wide[:, k, m, :], bcT[:, k, :],
                                     start=k == 0, stop=k == 1)
            last.then_inc(pe_step, 1)
            pe.wait_ge(dve_out, KMOV)
            for k in range(2):
                last = pe.matmul(PS[XR0:XC0, 4, :], m5T[:, k, :], kmov[:, k].rearrange("p h r -> p (h r)"),
                                 start=k == 0, stop=k == 1)
            last.then_inc(pe_step, 1)
            pe.wait_ge(dve_out, MMASK)
            for k in range(2):
                last = pe.matmul(PS[:, 5, 0:H * NA], mod_sel[:], mmask[:, k].rearrange("p h n -> p (h n)"),
                                 start=k == 0, stop=k == 1)
            last.then_inc(pe_step, 1)
            pe.wait_ge(dve_out, MREP)
            pe.wait_ge(wo_in, 16)
            for n in range(KT):
                if n >= 4:
                    pe.wait_ge(copied, n - 3)
                for c in range(2):
                    pe.matmul(PS[:, n % 4, 0:D], m_blk[:, c, 2 * n:2 * n + 2].rearrange("p h j n -> p (h j n)"),
                              woT_s[:, c, :], start=c == 0, stop=c == 1)
                for c in range(2):
                    last = pe.matmul(PS[:, n % 4, D:2 * D], bias_wide[:, 2 * n:2 * n + 2].rearrange("p h r -> p (h r)"),
                                     woT_s[:, c, :], start=c == 0, stop=c == 1)
                last.then_inc(pe_step, 1)


def tokens_phase(nc, g, sem, tmp):
    PS = g.PS
    tmax, csum, quad = tmp("tmax", [P, NT]), tmp("csum", [P, NT]), tmp("quad", [P, NT, NB, NB])
    var, t1, rstd = tmp("var", [P, NT]), tmp("t1", [P, NT]), tmp("rstd", [P, NT])
    a_part, a_res = tmp("a_part", [P, 3, NT, NA], BF16), tmp("a_res", [P, 2, NT, NA])
    ak_one, ak_rep = tmp("ak_one", [P, NT, PART], BF16), tmp("ak_rep", [P, NT, 4, PART], BF16)
    p_sq, diag, dmax = tmp("p_sq", [P, 2, 2 * D]), tmp("diag", [P, NT, H]), tmp("dmax", [P, H])
    gmax, gall = tmp("gmax", [H, 2]), tmp("gall", [1, 2])
    dve_step, dve_out, act_step, pe_step = sem("t_dve_step"), sem("t_dve_out"), sem("t_act_step"), sem("t_pe_step")
    xT_mm, xT_copied = sem("xT_mm"), [sem("xT_copied_dve"), sem("xT_copied_act")]
    ak_mm, ak_copied = sem("ak_mm"), [sem("ak_copied_dve"), sem("ak_copied_act")]
    p_mm, p_squared, p_summed = sem("p_mm"), sem("p_squared"), sem("p_summed")
    z_c = g.xtok[:, :, XC0:XROWS]
    SUBMAX, VAR, XTOK, AKREP, DMAX, GMAX, SHIFT = range(1, 8)

    with nc.Block() as block:
        @block.vector
        def _(dve):
            link = Chain(dve, dve_step)

            def give(instruction):
                instruction.then_inc(dve_out, 1)

            dve.wait_ge(g.gathered, 16 * NT)
            dve.wait_ge(g.weights_ready, 1)
            link(dve.tensor_reduce(tmax[:], g.cw[:], X, ALU.max))
            give(dve.tensor_tensor(g.cw[:], g.cw[:], tmax[:].unsqueeze(2).to_broadcast([P, NT, NB]), ALU.subtract))
            dve.wait_ge(act_step, 1)
            link(dve.reduce_sum(csum[:], g.cw[:], X))
            link(dve.reciprocal(csum[:], csum[:]))
            link(dve.tensor_tensor(z_c, g.cw[:], csum[:].unsqueeze(2).to_broadcast([P, NT, NB]), ALU.mult))
            for m in range(NB):
                last = dve.tensor_tensor(quad[:, :, m, :], z_c, z_c[:, :, m:m + 1].to_broadcast([P, NT, NB]), ALU.mult)
            link(last)
            qv = quad[:].rearrange("p t m n -> p t (m n)")
            link(dve.tensor_tensor(qv, qv, g.vb[:].unsqueeze(1).to_broadcast([P, NT, NB * NB]), ALU.mult))
            link(dve.reduce_sum(var[:], qv, X))
            give(dve.tensor_scalar(var[:], var[:], 0.0, EPS, ALU.max, ALU.add))
            dve.wait_ge(act_step, 2)
            link(dve.reciprocal(rstd[:], rstd[:]))
            newton(dve, link, rstd[:], var[:], t1[:])
            dve.memset(g.xtok[:, :, 0:XR0], 0.0)
            dve.memset(g.xtok[:, :, XR0 + NB:XC0], 1.0)
            link(dve.tensor_tensor(g.xtok[:, :, XR0:XR0 + NB], z_c, rstd[:].unsqueeze(2).to_broadcast([P, NT, NB]), ALU.mult))
            give(dve.memset(g.xT[:, T:T + S], 0.0))
            xa = g.xtok[:, :, XR0:XC0]
            link(dve.tensor_copy(a_part[:, 0], xa))
            link(dve.tensor_tensor(a_res[:, 0], xa, a_part[:, 0], ALU.subtract))
            link(dve.tensor_copy(a_part[:, 1], a_res[:, 0]))
            link(dve.tensor_tensor(a_res[:, 1], a_res[:, 0], a_part[:, 1], ALU.subtract))
            link(dve.tensor_copy(a_part[:, 2], a_res[:, 1]))
            dve.memset(ak_one[:, :, NSPLIT * NA:PART], 0.0)
            for s, part in enumerate((0, 1, 2, 0, 1, 0)):
                last = dve.tensor_copy(ak_one[:, :, NA * s:NA * s + NA], a_part[:, part])
            link(last)
            give(dve.tensor_copy(ak_rep[:], ak_one[:].unsqueeze(2).to_broadcast([P, NT, 4, PART])))
            for n in range(0, 8, 2):
                dve.wait_ge(xT_mm, n + 1)
                dve.tensor_copy(g.xT[:, 512 * n:512 * n + 512], PS[0:XROWS, n, :]).then_inc(xT_copied[0], 1)
            for n in range(0, 16, 2):
                b, k = n // 4, n % 4
                dve.wait_ge(ak_mm, b + 1)
                dve.tensor_copy(g.akz[32 * k:32 * k + 32, k, S * b:S * b + S],
                                PS[32 * k:32 * k + 32, b, :].bitcast(BF16)).then_inc(ak_copied[0], 1)
            for n in range(NT // 2):
                dve.wait_ge(p_squared, n + 1)
                dve.reduce_sum(diag[:, 2 * n:2 * n + 2, :].rearrange("p t h -> p (t h)"),
                               p_sq[:, n % 2].rearrange("p (g d) -> p g d", d=DK), X).then_inc(p_summed, 1)
            dve.wait_ge(p_summed, NT // 2)
            give(dve.tensor_reduce(dmax[:], diag[:].rearrange("p t h -> p h t"), X, ALU.max))
            dve.wait_ge(pe_step, 1)
            link(dve.tensor_reduce(gmax[:, 0:1], PS[0:H, 0, 0:P], X, ALU.max))
            give(dve.tensor_scalar(gmax[:, 1:2], gmax[:, 0:1], -1.0 / DK ** 0.5, None, ALU.mult))
            dve.wait_ge(dve_out, GMAX)
            dve.tensor_scalar(g.xT[0:H, 0:T], g.xT[0:H, 0:T], gmax[:, 1:2], None, ALU.add)
            dve.wait_ge(pe_step, 2)
            link(dve.tensor_reduce(gall[:, 0:1], PS[0:1, 1, 0:H], X, ALU.max))
            link(dve.tensor_scalar(gall[:, 1:2], gall[:, 0:1], SAFE * DK ** 0.5, None, ALU.is_le))
            link(dve.tensor_scalar(gall[:, 0:1], gall[:, 1:2], -1.0, 1.0, ALU.mult, ALU.add))
            give(dve.tensor_copy(g.flag[:], gall[:, 0:1]))

        @block.scalar
        def _(act):
            act.wait_ge(dve_out, SUBMAX)
            act.activation(g.cw[:], g.cw[:], ACT.Exp).then_inc(act_step, 1)
            act.wait_ge(dve_out, VAR)
            act.activation(rstd[:], var[:], ACT.Sqrt).then_inc(act_step, 1)
            for n in range(1, 8, 2):
                act.wait_ge(xT_mm, n + 1)
                act.copy(g.xT[:, 512 * n:512 * n + 512], PS[0:XROWS, n, :]).then_inc(xT_copied[1], 1)
            for n in range(1, 16, 2):
                b, k = n // 4, n % 4
                act.wait_ge(ak_mm, b + 1)
                act.copy(g.akz[32 * k:32 * k + 32, k, S * b:S * b + S],
                         PS[32 * k:32 * k + 32, b, :].bitcast(BF16)).then_inc(ak_copied[1], 1)
            for n in range(NT // 2):
                act.wait_ge(p_mm, n + 1)
                if n >= 2:
                    act.wait_ge(p_summed, n - 1)
                act.activation(p_sq[:, n % 2], PS[:, 4 + n % 4, :], ACT.Square).then_inc(p_squared, 1)

        @block.tensor
        def _(pe):
            pe.wait_ge(dve_out, XTOK)
            for t in range(NT):
                last = pe.transpose(PS[0:XROWS, t // 4, P * (t % 4):P * (t % 4) + P], g.xtok[:, t, :], g.ident[:])
                if t % 4 == 3:
                    last.then_inc(xT_mm, 1)
            pe.wait_ge(dve_out, AKREP)
            for b in range(NBATCH):
                pe.wait_ge(xT_copied[b % 2], b // 2 + 1)
                for t in range(KT):
                    last = pe.transpose(PS[:, b, :].bitcast(BF16)[:, P * t:P * t + P],
                                        ak_rep[:, KT * b + t].rearrange("p k r -> p (k r)"), g.identb[:])
                last.then_inc(ak_mm, 1)
            pe.wait_ge(xT_copied[0], 4)
            pe.wait_ge(xT_copied[1], 4)
            for n in range(NT // 2):
                if n >= 4:
                    pe.wait_ge(p_squared, n - 3)
                for i in range(2):
                    t = 2 * n + i
                    last = pe.matmul(PS[:, 4 + n % 4, D * i:D * i + D], g.xT[XR0:XC0, P * t:P * t + P],
                                     g.mg[XR0:XC0, :], start=True, stop=True)
                last.then_inc(p_mm, 1)
            pe.wait_ge(dve_out, DMAX)
            pe.wait_ge(ak_copied[0], 8)
            pe.wait_ge(ak_copied[1], 8)
            pe.transpose(PS[0:H, 0, 0:P], dmax[:], g.ident[:]).then_inc(pe_step, 1)
            pe.wait_ge(dve_out, GMAX)
            pe.transpose(PS[0:1, 1, 0:H], gmax[:, 0:1], g.ident[0:H, 0:H]).then_inc(pe_step, 1)


def row_maxima_phase(nc, g, sem, tmp):
    PS = g.PS
    xTr, xtile = tmp("xTr", [P, T]), tmp("xtile", [XROWS, 2, P])
    u_s, rmax = tmp("u_s", [P, HG, 4, P]), tmp("rmax", [P, NT, H])
    zeroed, replicated, u_mm, u_copied = sem("rm_zeroed"), sem("rm_replicated"), sem("rm_u_mm"), sem("rm_u_copied")
    tile_in, scored, maxed, negated = sem("rm_tile_in"), sem("rm_scored"), sem("rm_maxed"), sem("rm_negated")
    turned, taken = sem("rm_turned"), sem("rm_taken")

    with nc.Block() as block:
        @block.sync
        def _(sp):
            needed = sp.value_load(g.flag[0:1, 0:1], min_val=0, max_val=1)
            with sp.If(needed > 0):
                sp.wait_ge(zeroed, 3)
                for k in range(4):
                    sp.dma_start(xTr[32 * k:32 * k + NA, :], g.xT[XR0:XC0, 0:T]).then_inc(replicated, 16)
                sp.wait_ge(replicated, 64)

        @block.vector
        def _(dve):
            needed = dve.value_load(g.flag[0:1, 0:1], min_val=0, max_val=1)
            with dve.If(needed > 0):
                dve.sem_inc(u_copied, FREE)
                dve.sem_inc(maxed, FREE)
                dve.memset(g.xT[0:H, 0:T], 0.0).then_inc(zeroed, 1)
                dve.memset(xTr[:], 0.0).then_inc(zeroed, 1)
                dve.memset(u_s[:], 0.0).then_inc(zeroed, 1)
                dve.wait_ge(zeroed, 3)
                with dve.Fori(0, NBATCH) as b:
                    with dve.Fori(0, KT) as q:
                        t = b * KT + q
                        dve.wait_ge(u_mm, t + FREE)
                        dve.tensor_copy(xtile[:, 0, :], g.xT[:, ds(t * P, P)]).then_inc(tile_in, 1)
                        dve.wait_ge(u_mm, t + 1 + FREE)
                        dve.wait_ge(scored, t * H + FREE)
                        for k in range(4):
                            r = slice(32 * k, 32 * k + 32)
                            last = dve.tensor_copy(u_s[r, :, k, :], PS[r, 0, :].rearrange("p (h q) -> p h q", h=HG))
                        last.then_inc(u_copied, 1)
                        for h in range(H):
                            dve.wait_ge(scored, t * H + h + 1 + FREE)
                            m = 2 + 2 * (h % 2)
                            dve.tensor_reduce(rmax[:, ds(t, 1), h], PS[:, m:m + 2, :].rearrange("p b k -> p (b k)").unsqueeze(1), X, ALU.max).then_inc(maxed, 1)
                dve.wait_ge(maxed, NT * H + FREE)
                dve.tensor_scalar(g.xtok[:, :, 0:H], rmax[:], -1.0, None, ALU.mult).then_inc(negated, 1)
                for n in range(8):
                    dve.wait_ge(turned, n + 1)
                    dve.tensor_copy(g.xT[0:H, 512 * n:512 * n + 512], PS[0:H, n, :]).then_inc(taken, 1)
                dve.wait_ge(taken, 8)

        @block.tensor
        def _(pe):
            needed = pe.value_load(g.flag[0:1, 0:1], min_val=0, max_val=1)
            with pe.If(needed > 0):
                pe.sem_inc(u_mm, FREE)
                pe.sem_inc(scored, FREE)
                pe.wait_ge(replicated, 64)
                with pe.Fori(0, NBATCH) as b:
                    with pe.Fori(0, KT) as q:
                        t = b * KT + q
                        pe.wait_ge(tile_in, t + 1)
                        pe.wait_ge(u_copied, t + FREE)
                        for k in range(HG):
                            last = pe.matmul(PS[:, 0, P * k:P * k + P], g.kr[:, P * k:P * k + P], xtile[:, 0, :],
                                             start=True, stop=True)
                        last.then_inc(u_mm, 1)
                        pe.wait_ge(u_copied, t + 1 + FREE)
                        for h in range(H):
                            m = 2 + 2 * (h % 2)
                            pe.wait_ge(maxed, t * H + max(h - 1, 0) + FREE)
                            for c in range(2):
                                last = pe.matmul(PS[:, m + c, :], u_s[:, h // 4, h % 4, :],
                                                 xTr[:, ds(b * S + c * 512, 512)], start=True, stop=True)
                            last.then_inc(scored, 1)
                pe.wait_ge(negated, 1)
                for n in range(8):
                    for i in range(4):
                        last = pe.transpose(PS[0:H, n, P * i:P * i + P], g.xtok[:, 4 * n + i, 0:H], g.ident[:])
                    last.then_inc(turned, 1)


def attention_phase(nc, g, sem, tmp):
    PS = g.PS
    u1, u2 = tmp("u1", [P, 512], BF16), tmp("u2", [P, 512], BF16)
    ures = tmp("ures", [P, 512])
    qf, prob = tmp("qf", [P, HG, S], BF16), tmp("prob", [P, 4, S])
    acc_s, rden = tmp("acc_s", [P, HG, 512]), tmp("rden", [NR, HG, 8, 8])
    u_mm, u_read, u_step = sem("u_mm"), sem("u_read"), sem("u_step")
    scores_ready, exp_done, prob_used = sem("scores_ready"), sem("exp_done"), sem("prob_used")
    acc_copied, va_ready = sem("acc_copied"), sem("va_ready")
    folded, fold_read, rden_step = sem("folded"), sem("fold_read"), sem("rden_step")
    BU = HG * UN
    ACC, UB = 6, 7

    with nc.Block() as block:
        @block.tensor
        def _(pe):
            pe.sem_inc(prob_used, FREE)
            pe.sem_inc(folded, FREE)

            def query_product(b, hg, half, n):
                if not (isinstance(n, int) and n == 0):
                    pe.wait_ge(u_read, n)
                pe.matmul(PS[:, UB, :], g.kr[:, P * hg:P * hg + P], g.xT[:, ds(b * S, S)].rearrange("p (r j) -> p j r", j=NJ)[:, 8 * half:8 * half + 8, :],
                          start=True, stop=True).then_inc(u_mm, 1)

            def scores(b, n):
                hg, slot, kt, buf = n // UN, n // KT % 4, n % KT, n % 3
                if n % UN == 0:
                    pe.wait_ge(u_step, 3 * (b * (2 * HG) + 2 * hg + 2))
                if n < 3:
                    pe.wait_ge(exp_done, b * BU + FREE)
                    pe.wait_ge(fold_read, b + FREE)
                else:
                    pe.wait_ge(exp_done, b * BU + n - 2 + FREE)
                for c in range(2):
                    last = pe.matmul(PS[:, 2 * buf + c, :], g.akz[:, slot, ds(b * S + P * kt, P)],
                                     qf[:, hg, 512 * c:512 * c + 512], start=True, stop=True)
                last.then_inc(scores_ready, 1)

            def sums(b, pair):
                hg, slot = pair // (UN // 2), pair // (KT // 2) % 4
                if pair == 0:
                    pe.wait_ge(va_ready, b + 1)
                if pair % (UN // 2) == 0:
                    pe.wait_ge(acc_copied, b * HG + hg + FREE)
                pe.wait_ge(exp_done, b * BU + 2 * pair + 2 + FREE)
                for n in (2 * pair, 2 * pair + 1):
                    kt = n % KT
                    for c in range(2):
                        r = 32 * (2 * (kt % 2) + c)
                        last = pe.matmul(PS[r:r + 32, ACC, :], g.va[:, kt, slot, :], prob[:, n % 4, 512 * c:512 * c + 512],
                                         start=slot == 0 and kt < 2, stop=slot == 3 and kt >= KT - 2)
                last.then_inc(prob_used, 1)

            query_product(0, 0, 0, 0)
            query_product(0, 0, 1, 1)
            with pe.Fori(0, NBATCH) as b:
                scores(b, 0)
                scores(b, 1)
                for pair in range(BU // 2):
                    for n in (2 * pair + 2, 2 * pair + 3):
                        if n < BU:
                            scores(b, n)
                    sums(b, pair)
                    hg, at = pair // (UN // 2), pair % (UN // 2)
                    if at in (2, 8):
                        half = int(at == 8)
                        nb, nh = (b, hg + 1) if hg + 1 < HG else (b + 1, 0)
                        query_product(nb, nh, half, b * (2 * HG) + 2 * hg + 2 + half)
                pe.wait_ge(acc_copied, b * HG + HG + FREE)
                pe.wait_ge(exp_done, b * BU + BU + FREE)
                for hg in range(HG):
                    for j in range(8):
                        last = pe.matmul(PS[0:NR, hg, 64 * j:64 * j + 64], acc_s[:, hg, NR * j:NR * j + NR],
                                         g.fold_sel[:].rearrange("p c r -> p (c r)"), start=True, stop=True)
                last.then_inc(folded, 1)

        @block.scalar
        def _(act):
            act.sem_inc(exp_done, FREE)
            with act.Fori(0, NBATCH) as b:
                for n in range(BU):
                    act.wait_ge(scores_ready, b * BU + n + 1)
                    if n >= 4:
                        act.wait_ge(prob_used, b * (BU // 2) + (n - 4) // 2 + 1 + FREE)
                    else:
                        act.wait_ge(prob_used, b * (BU // 2) + FREE)
                    buf = n % 3
                    act.activation(prob[:, n % 4, :], PS[:, 2 * buf:2 * buf + 2, :].rearrange("p c q -> p (c q)"),
                                   ACT.Exp).then_inc(exp_done, 1)

        @block.vector
        def _(dve):
            dve.sem_inc(acc_copied, FREE)
            dve.sem_inc(fold_read, FREE)

            def query_features(b, hg, half, n):
                dve.wait_ge(u_mm, n + 1)
                dve.tensor_copy(u1[:], PS[:, UB, :]).then_inc(u_step, 1)
                dve.wait_ge(u_step, 3 * n + 1)
                dve.scalar_tensor_tensor(ures[:], u1[:], g.part_c[:, 0:1], PS[:, UB, :], ALU.mult, ALU.add).then_inc(u_read, 1)
                dve.wait_ge(u_read, n + 1)
                dve.tensor_copy(u2[:], ures[:]).then_inc(u_step, 1)
                dve.wait_ge(u_step, 3 * n + 2)
                dve.scalar_tensor_tensor(qf[:, hg, 512 * half:512 * half + 512], u2[:], g.part_c[:, 1:2], ures[:],
                                         ALU.mult, ALU.add).then_inc(u_step, 1)
                dve.wait_ge(u_step, 3 * n + 3)

            query_features(0, 0, 0, 0)
            query_features(0, 0, 1, 1)
            with dve.Fori(0, NBATCH) as b:
                for slot in range(4):
                    last = dve.tensor_copy(g.va[:, :, slot, 8 * slot:8 * slot + NA], g.xtok[:, ds(b * KT, KT), XR0:XC0])
                last.then_inc(va_ready, 1)
                for hg in range(HG):
                    for half in range(2):
                        nb, nh = (b, hg + 1) if hg + 1 < HG else (b + 1, 0)
                        if half == 0:
                            dve.wait_ge(scores_ready, b * BU + UN * hg + 1)
                        query_features(nb, nh, half, b * (2 * HG) + 2 * hg + 2 + half)
                    if hg == 0:
                        dve.wait_ge(folded, b + FREE)
                    dve.wait_ge(prob_used, b * (BU // 2) + (hg + 1) * (UN // 2) + FREE)
                    dve.tensor_copy(acc_s[:, hg, :], PS[:, ACC, :]).then_inc(acc_copied, 1)
                dve.wait_ge(folded, b + 1 + FREE)
                for hg in range(HG):
                    sums = PS[0:NR, hg, :].rearrange("p (j s r) -> p j s r", j=8, s=8)
                    last = dve.reciprocal(rden[:, hg], sums[:, :, :, NB])
                last.then_inc(rden_step, 1)
                dve.wait_ge(rden_step, b + 1)
                for hg in range(HG):
                    for c in range(2):
                        sums = PS[0:NR, hg, :].rearrange("p (j c s r) -> p c s j r", j=8, c=2, s=4)
                        out = g.z[:, ds(b, 1), 4 * hg:4 * hg + 4, 8 * c:8 * c + 8, :].rearrange("p b s j n -> p (b s) j n")
                        last = dve.tensor_tensor(out, sums[:, c, :, :, 0:NB],
                                                 rden[:, hg].rearrange("p j (c s) -> p c s j", c=2)[:, c].unsqueeze(3).to_broadcast([NR, 4, 8, NB]),
                                                 ALU.mult)
                last.then_inc(fold_read, 1)
                dve.wait_ge(fold_read, b + 1 + FREE)


def routing_phase(nc, g, router, w13, sem, tmp):
    PS = g.PS
    zT, xnT = tmp("zT", [P, NT, NR]), tmp("xnT", [P, 2, 2, P])
    stats = tmp("stats", [P, NT, 6])
    mean_d, var, t1, rstd = tmp("mean_d", [P, NT]), tmp("var2", [P, NT]), tmp("t1_2", [P, NT]), tmp("rstd2", [P, NT])
    logits, top, top_i = tmp("logits", [P, NT, E]), tmp("top", [P, NT, 8]), tmp("top_i", [P, NT, 8], U32)
    top_f, wgt = tmp("top_f", [P, 2, NT]), tmp("wgt", [P, 2, NT])
    picked, count = tmp("picked", [P, 2, NT, E]), [tmp("count0", [P, E, NT]), tmp("count1", [P, E, NT])]
    chosen, place, prod = tmp("chosen", [P, E, NT]), tmp("place", [P, E, NT]), tmp("prod", [P, NT, E])
    tiles_i, tiles = tmp("tiles_i", [P, E], I32), tmp("tiles", [P, E])
    first, shift = [tmp(f"first{i}", [P, E]) for i in range(4)], tmp("shift", [P, E])
    pos, pos_i, pos_r, pos_j = (tmp("pos", [P, 2, NT]), tmp("pos_i", [P, 2, 2, NT], I32), tmp("pos_r", [P, 2, NT]),
                                tmp("pos_j", [P, 2, NT]))
    hot_r, hot_j = tmp("hot_r", [P, 4, P]), tmp("hot_j", [P, 4, 2, ETILES])
    xn, mean, rt_s = tmp("xn", [P, 2, 8, D]), tmp("mean", [P, NT]), tmp("rt_s", [P, 2, E])
    pair_no = tmp("pair_no", [P, NT, 2])
    idx_f, te_f = tmp("idx_f", [P, 2, ETILES]), tmp("te_f", [P, 2, ETILES])
    zT_mm, zT_copied = sem("zT_mm"), sem("zT_copied")
    h_mm, h_copied, h_stats = sem("h_mm"), sem("h_copied"), sem("h_stats")
    xn_ready, xn_turned, xnT_copied, l_mm, l_taken = sem("xn_ready"), sem("xn_turned"), sem("xnT_copied"), sem("l_mm"), sem("l_taken")
    rt_in = sem("rt_in")
    dve_step, dve_out, act_step, pe_step = sem("r_dve_step"), sem("r_dve_out"), sem("r_act_step"), sem("r_pe_step")
    hot_ready, hot_used, xn_stored = sem("hot_ready"), sem("hot_used"), [sem("xn_stored0"), sem("xn_stored1")]
    VAR, TOPDIFF, ROWTOT = range(1, 4)

    with nc.Block() as block:
        @block.tensor
        def _(pe):
            for t in range(NT):
                b, k = t // KT, t % KT
                last = pe.transpose(PS[:, b, NR * k:NR * k + NR],
                                    g.z[:, b, 2 * k:2 * k + 2].rearrange("p h j n -> p (h j n)"), g.ident[0:NR, 0:NR])
                if k == KT - 1:
                    last.then_inc(zT_mm, 1)
            for t in range(NT):
                k, bank = t % KT, 4 + t % 4
                pe.wait_ge(zT_copied, t // KT + 1)
                if t >= 4:
                    pe.wait_ge(h_copied, t - 3)
                pe.matmul(PS[:, bank, 0:D], g.xT[XR0:XROWS, P * t:P * t + P], g.resid[XR0:XROWS, :], start=True, stop=False)
                for i in range(2):
                    r = slice(NR * i, NR * i + NR)
                    last = pe.matmul(PS[r, bank, 0:D], zT[r, t, :], g.g_pair[r, k, :], start=False, stop=True)
                last.then_inc(h_mm, 1)
            pe.wait_ge(rt_in, 16)
            for t in range(NT):
                pe.wait_ge(xn_ready, t + 1)
                if t >= 2:
                    pe.wait_ge(xnT_copied, t - 1)
                for c in range(2):
                    last = pe.transpose(PS[:, t % 2, P * c:P * c + P], xn[:, t // 8 % 2, t % 8, P * c:P * c + P], g.ident[:])
                last.then_inc(xn_turned, 1)
                pe.wait_ge(xnT_copied, t + 1)
                for c in range(2):
                    last = pe.matmul(PS[:, 3, E * t:E * t + E], xnT[:, t % 2, c, :], rt_s[:, c, :], start=c == 0, stop=c == 1)
                last.then_inc(l_mm, 1)
            pe.wait_ge(dve_out, ROWTOT)
            pe.matmul(PS[:, 0, 0:E], g.tri[:], tiles[:], start=True, stop=True)
            pe.matmul(PS[:, 1, 0:E], g.ones[:], tiles[:], start=True, stop=True).then_inc(pe_step, 1)
            for n in range(2 * NT):
                pe.wait_ge(hot_ready, n + 1)
                pe.matmul(PS[:, 2, 0:2 * ETILES], hot_r[:, n % 4, :], hot_j[:, n % 4].rearrange("p c j -> p (c j)"),
                          start=n == 0, stop=n == 2 * NT - 1).then_inc(hot_used, 1)

        @block.scalar
        def _(act):
            act.wait_ge(dve_out, VAR)
            act.activation(rstd[:], var[:], ACT.Sqrt).then_inc(act_step, 1)
            for t in range(NT):
                act.wait_ge(xn_turned, t + 1)
                if t >= 2:
                    act.wait_ge(l_mm, t - 1)
                act.copy(xnT[:, t % 2].rearrange("p c q -> p (c q)"), PS[:, t % 2, 0:2 * P]).then_inc(xnT_copied, 1)
            act.wait_ge(dve_out, TOPDIFF)
            act.activation(wgt[:, 1, :], wgt[:, 0, :], ACT.Exp).then_inc(act_step, 1)

        @block.vector
        def _(dve):
            link = Chain(dve, dve_step)

            def give(instruction):
                instruction.then_inc(dve_out, 1)

            for b in range(NBATCH):
                dve.wait_ge(zT_mm, b + 1)
                dve.tensor_copy(zT[:, KT * b:KT * b + KT, :].rearrange("p t r -> p (t r)"), PS[:, b, :]).then_inc(zT_copied, 1)
            for t in range(NT):
                dve.wait_ge(h_mm, t + 1)
                dve.tensor_tensor(g.h1[:, t, :], PS[:, 4 + t % 4, 0:D], g.h_bias[:, t % KT, :], ALU.add).then_inc(h_copied, 1)
                dve.wait_ge(h_copied, t + 1)
                dve.bn_stats(stats[:, t, :], g.h1[:, t, :]).then_inc(h_stats, 1)
            dve.wait_ge(h_stats, NT)
            link(dve.tensor_tensor(mean[:], stats[:, :, 1], stats[:, :, 4], ALU.add))
            link(dve.tensor_scalar(mean[:], mean[:], -0.5, None, ALU.mult))
            link(dve.tensor_tensor(mean_d[:], stats[:, :, 1], stats[:, :, 4], ALU.subtract))
            link(dve.tensor_tensor(mean_d[:], mean_d[:], mean_d[:], ALU.mult))
            link(dve.tensor_scalar(mean_d[:], mean_d[:], 0.25, EPS, ALU.mult, ALU.add))
            link(dve.tensor_tensor(var[:], stats[:, :, 2], stats[:, :, 5], ALU.add))
            link(dve.tensor_scalar(var[:], var[:], 1.0 / D, None, ALU.mult))
            give(dve.tensor_tensor(var[:], var[:], mean_d[:], ALU.add))
            dve.wait_ge(act_step, 1)
            link(dve.reciprocal(rstd[:], rstd[:]))
            newton(dve, link, rstd[:], var[:], t1[:])
            link(dve.tensor_tensor(mean[:], mean[:], rstd[:], ALU.mult))
            for t in range(NT):
                if t >= 16 and t % 8 == 0:
                    dve.wait_ge(xn_stored[(t // 8) % 2], 16)
                    dve.wait_ge(xn_turned, t - 8)
                dve.tensor_scalar(xn[:, t // 8 % 2, t % 8, :], g.h1[:, t, :], rstd[:, t:t + 1], mean[:, t:t + 1], ALU.mult, ALU.add).then_inc(xn_ready, 1)
            dve.wait_ge(l_mm, NT)
            link(dve.tensor_copy(logits[:].rearrange("p t e -> p (t e)"), PS[:, 3, 0:NT * E]))
            for t in range(NT):
                last = dve.max(top[:, t, :], logits[:, t, :])
            link(last)
            for t in range(NT):
                last = dve.max_index(top_i[:, t, :], top[:, t, :], logits[:, t, :])
            link(last)
            give(dve.tensor_tensor(wgt[:, 0, :], top[:, :, 1], top[:, :, 0], ALU.subtract))
            link(dve.tensor_copy(top_f[:], top_i[:, :, 0:2].rearrange("p t k -> p k t")))
            dve.wait_ge(act_step, 2)
            link(dve.tensor_scalar(wgt[:, 0, :], wgt[:, 1, :], 1.0, None, ALU.add))
            link(dve.reciprocal(wgt[:, 0, :], wgt[:, 0, :]))
            link(dve.tensor_tensor(wgt[:, 1, :], wgt[:, 1, :], wgt[:, 0, :], ALU.mult))
            for k in range(2):
                last = dve.tensor_tensor(picked[:, k], g.iota_e.unsqueeze(1).to_broadcast([P, NT, E]),
                                         top_f[:, k].unsqueeze(2).to_broadcast([P, NT, E]), ALU.is_equal)
            link(last)
            link(dve.tensor_tensor(chosen[:], picked[:, 0].rearrange("p t e -> p e t"),
                                   picked[:, 1].rearrange("p t e -> p e t"), ALU.add))
            src, step = chosen, 1
            while step < NT:
                dst = count[(step.bit_length() - 1) % 2]
                dve.tensor_copy(dst[:, :, 0:step], src[:, :, 0:step])
                link(dve.tensor_tensor(dst[:, :, step:], src[:, :, step:], src[:, :, 0:NT - step], ALU.add))
                src, step = dst, 2 * step
            give(dve.tensor_copy(tiles[:], src[:, :, NT - 1]))
            link(dve.tensor_tensor(place[:], src[:], chosen[:], ALU.subtract))
            dve.wait_ge(pe_step, 1)
            link(dve.tensor_scalar(shift[:], PS[:, 1, 0:E], float(P - 1), None, ALU.add))
            link(dve.tensor_copy(tiles_i[:], shift[:]))
            link(dve.tensor_scalar(tiles_i[:], tiles_i[:], 7, None, ALU.logical_shift_right))
            link(dve.tensor_copy(tiles[:], tiles_i[:]))
            src = tiles
            for i, step in enumerate((1, 2, 4)):
                dve.tensor_copy(first[i][:, 0:step], src[:, 0:step])
                link(dve.tensor_tensor(first[i][:, step:], src[:, step:], src[:, 0:E - step], ALU.add))
                src = first[i]
            link(dve.tensor_tensor(first[3][:], src[:], tiles[:], ALU.subtract))
            link(dve.scalar_tensor_tensor(shift[:], first[3][:], float(P), PS[:, 0, 0:E], ALU.mult, ALU.add))
            link(dve.tensor_tensor(place[:], place[:], shift[:].unsqueeze(2).to_broadcast([P, E, NT]), ALU.add))
            for k in range(2):
                link(dve.tensor_tensor(prod[:], picked[:, k], place[:].rearrange("p e t -> p t e"), ALU.mult))
                link(dve.reduce_sum(pos[:, k, :], prod[:], X))
            link(dve.tensor_copy(pos_i[:, 0], pos[:]))
            link(dve.tensor_scalar(pos_i[:, 1], pos_i[:, 0], 7, None, ALU.logical_shift_right))
            link(dve.tensor_copy(pos_j[:], pos_i[:, 1]))
            link(dve.scalar_tensor_tensor(pos_r[:], pos_j[:], -float(P), pos[:], ALU.mult, ALU.add))
            link(dve.memset(te_f[:, 0, :], 0.0))
            for e in range(1, E):
                link(dve.scalar_tensor_tensor(te_f[:, e % 2, :], g.iota_r[:, 0:ETILES], first[3][:, e:e + 1],
                                              te_f[:, (e + 1) % 2, :], ALU.is_ge, ALU.add))
            dve.tensor_copy(g.tile_expert[:], te_f[0:1, (E - 1) % 2, :])
            for t in range(NT):
                last = dve.tensor_scalar(pair_no[:, t, :], g.iota_pk[:], float(2 * P * t), None, ALU.add)
            link(last)
            for n in range(2 * NT):
                t, k = n // 2, n % 2
                if n >= 4:
                    dve.wait_ge(hot_used, n - 3)
                dve.tensor_scalar(hot_r[:, n % 4, :], g.iota_r[:], pos_r[:, k, t:t + 1], None, ALU.is_equal)
                dve.tensor_scalar(hot_j[:, n % 4, 0, :], g.iota_r[:, 0:ETILES], pos_j[:, k, t:t + 1],
                                  pair_no[:, t, k:k + 1], ALU.is_equal, ALU.mult)
                dve.tensor_scalar(hot_j[:, n % 4, 1, :], g.iota_r[:, 0:ETILES], pos_j[:, k, t:t + 1],
                                  wgt[:, k, t:t + 1], ALU.is_equal, ALU.mult).then_inc(hot_ready, 1)
            dve.wait_ge(hot_used, 2 * NT)
            link(dve.tensor_copy(te_f[:], PS[:, 2, 0:2 * ETILES].rearrange("p (c j) -> p c j", c=2)))
            link(dve.tensor_scalar(idx_f[:, 1, :], te_f[:, 0, :], 0.0, float(4 * T), ALU.is_equal, ALU.mult))
            link(dve.tensor_tensor(idx_f[:, 0, :], te_f[:, 0, :], idx_f[:, 1, :], ALU.add))
            link(dve.tensor_scalar(idx_f[:, 0, :], idx_f[:, 0, :], -1.0, None, ALU.add))
            dve.tensor_copy(g.slot_w[:], te_f[:, 1, :])
            link(dve.tensor_copy(g.idx[:], idx_f[:, 0, :]))
            link(dve.tensor_scalar(g.idx_tok[:], g.idx[:], 1, None, ALU.logical_shift_right))

        @block.sync
        def _(sp):
            sp.dma_start(rt_s[:], router.rearrange("(c p) e -> p c e", p=P)).then_inc(rt_in, 16)
            for e in range(E):
                sp.dma_start(g.w13_s[:, :, e, :], w13[e].rearrange("(c p) f -> p c f", p=P)).then_inc(g.w_in, 16)
            for q in range(4):
                sp.wait_ge(xn_ready, 8 * q + 8)
                sp.dma_start(g.xrows.rearrange("(t p) d -> p t d", p=P)[:, 8 * q:8 * q + 8],
                             xn[:, q % 2]).then_inc(xn_stored[q % 2], 16)
            sp.wait_ge(xn_stored[0], 32)
            sp.wait_ge(xn_stored[1], 32)
            sp.wait_ge(g.w_in, 16 * E)


def experts_phase(nc, g, w2, sem, tmp):
    PS = g.PS
    xs, xsT = tmp("xs", [P, 2, D]), tmp("xsT", [P, 2, 2, P])
    act_s, hid, hidT = tmp("act_s", [P, 2, FF]), tmp("hid", [P, 2, FF]), tmp("hidT", [P, 2, FF])
    y_s, w2_s = tmp("y_s", [P, 2, D]), tmp("w2_s", [P, 4, E, D])
    w2_in, y_free = sem("w2_in"), sem("y_free")
    xs_in, y_out = [sem("xs_in0"), sem("xs_in1")], [sem("y_out0"), sem("y_out1")]
    zeroed, x_turned, x_copied, up_mm = sem("zeroed"), sem("x_turned"), sem("x_copied"), sem("up_mm")
    silu_done, hid_ready, hid_turned = sem("silu_done"), sem("hid_ready"), sem("hid_turned")
    hidT_ready, y_mm, y_copied = sem("hidT_ready"), sem("y_mm"), sem("y_copied")

    with nc.Block() as block:
        @block.sync
        def _(sp):
            for e in range(E):
                sp.dma_start(w2_s[:, :, e, :], w2[e].rearrange("(c p) d -> p c d", p=P)).then_inc(w2_in, 16)
            sp.sem_inc(y_free, FREE)
            with sp.Fori(0, ETILES // 2) as i:
                for k in range(2):
                    sp.wait_ge(y_out[k], i * 16 + 16)
                    sp.sem_inc(y_free, 1)

        @block.gpsimd
        def _(pool):
            def gather(j):
                pool.indirect_dma_start(xs[:, j % 2, :], None, g.xrows,
                                        bass.IndirectOffsetOnAxis(g.idx_tok[:, j:j + 1].bitcast(U32), 0),
                                        bounds_check=T - 1, oob_is_err=False).then_inc(xs_in[j % 2], 16)

            pool.memset(xs[:], 0.0).then_inc(zeroed, 1)
            pool.wait_ge(zeroed, 1)
            gather(0)
            gather(1)
            for j in range(ETILES):
                if j + 2 < ETILES:
                    pool.wait_ge(x_turned, j + 1)
                    gather(j + 2)
                pool.wait_ge(y_copied, j + 1 + FREE)
                pool.indirect_dma_start(g.ypair, bass.IndirectOffsetOnAxis(g.idx[:, j:j + 1].bitcast(U32), 0),
                                        y_s[:, j % 2, :], None,
                                        bounds_check=2 * T - 1, oob_is_err=False).then_inc(y_out[j % 2], 16)
            for k in range(2):
                pool.wait_ge(y_out[k], 16 * (ETILES // 2))

        @block.tensor
        def _(pe):
            pe.sem_inc(up_mm, FREE)
            pe.sem_inc(hid_turned, FREE)
            pe.sem_inc(y_mm, FREE)
            pe.wait_ge(w2_in, 16 * E)
            with pe.Fori(0, ETILES // 2) as i:
                for k in range(2):
                    j = i * 2 + k
                    e = pe.value_load(g.tile_expert[0:1, ds(j, 1)], min_val=0, max_val=E - 1)
                    pe.wait_ge(xs_in[k], i * 16 + 16)
                    pe.wait_ge(x_copied, j + FREE)
                    for c in range(2):
                        last = pe.transpose(PS[:, 0, P * c:P * c + P], xs[:, k, P * c:P * c + P], g.ident[:])
                    last.then_inc(x_turned, 1)
                    pe.wait_ge(x_copied, j + 1 + FREE)
                    if k == 0:
                        pe.wait_ge(hid_ready, i * 2 + FREE)
                    for c in range(2):
                        for q in range(2):
                            last = pe.matmul(PS[:, 1 + 2 * k + c, :], xsT[:, k, q, :],
                                             g.w13_s[:, q, ds(e, 1), FF * c:FF * c + FF].rearrange("p e f -> p (e f)"),
                                             start=q == 0, stop=q == 1)
                    last.then_inc(up_mm, 1)
                for k in range(2):
                    j = i * 2 + k
                    e = pe.value_load(g.tile_expert[0:1, ds(j, 1)], min_val=0, max_val=E - 1)
                    pe.wait_ge(hid_ready, j + 1 + FREE)
                    pe.wait_ge(hidT_ready, j + FREE)
                    for c in range(4):
                        last = pe.transpose(PS[:, 5, P * c:P * c + P], hid[:, k, P * c:P * c + P], g.ident[:])
                    last.then_inc(hid_turned, 1)
                    pe.wait_ge(hidT_ready, j + 1 + FREE)
                    if k == 0:
                        pe.wait_ge(y_copied, i * 2 + FREE)
                    for c in range(4):
                        last = pe.matmul(PS[:, 6 + k, 0:D], hidT[:, k, P * c:P * c + P],
                                         w2_s[:, c, ds(e, 1), :].rearrange("p e d -> p (e d)"),
                                         start=c == 0, stop=c == 3)
                    last.then_inc(y_mm, 1)

        @block.scalar
        def _(act):
            act.sem_inc(x_copied, FREE)
            act.sem_inc(y_copied, FREE)
            with act.Fori(0, ETILES // 2) as i:
                for k in range(2):
                    j = i * 2 + k
                    act.wait_ge(x_turned, j + 1)
                    if k == 0:
                        act.wait_ge(up_mm, i * 2 + FREE)
                    act.copy(xsT[:, k].rearrange("p c q -> p (c q)"), PS[:, 0, 0:2 * P]).then_inc(x_copied, 1)
                    act.wait_ge(up_mm, j + 1 + FREE)
                    if k == 0:
                        act.wait_ge(hid_ready, i * 2 + FREE)
                    act.activation(act_s[:, k, :], PS[:, 1 + 2 * k, :], ACT.Silu).then_inc(silu_done, 1)
                for k in range(2):
                    j = i * 2 + k
                    act.wait_ge(y_mm, j + 1 + FREE)
                    if k == 0:
                        act.wait_ge(y_free, i * 2 + FREE)
                    act.copy(y_s[:, k, :], PS[:, 6 + k, 0:D]).then_inc(y_copied, 1)

        @block.vector
        def _(dve):
            dve.sem_inc(hid_ready, FREE)
            dve.sem_inc(hidT_ready, FREE)
            with dve.Fori(0, ETILES // 2) as i:
                for k in range(2):
                    j = i * 2 + k
                    dve.wait_ge(silu_done, j + 1)
                    if k == 0:
                        dve.wait_ge(hid_turned, i * 2 + FREE)
                    dve.scalar_tensor_tensor(hid[:, k, :], act_s[:, k, :], g.slot_w[:, ds(j, 1)], PS[:, 2 + 2 * k, :],
                                             ALU.mult, ALU.mult).then_inc(hid_ready, 1)
                for k in range(2):
                    j = i * 2 + k
                    dve.wait_ge(hid_turned, j + 1 + FREE)
                    if k == 0:
                        dve.wait_ge(y_mm, i * 2 + FREE)
                    dve.tensor_copy(hidT[:, k, :], PS[:, 5, :]).then_inc(hidT_ready, 1)


def output_phase(nc, g, out, sem, tmp):
    CH = 4
    y = tmp("y_in", [P, 2, CH, 2, D])
    y_in = [sem("y_in0"), sem("y_in1")]
    added, summed, stored = sem("added"), sem("summed"), sem("stored")
    rows = g.ypair.rearrange("(t p k) d -> p t (k d)", p=P, k=2)
    out_rows = out.rearrange("b (t p) d -> p (b t) d", p=P)

    with nc.Block() as block:
        @block.sync
        def _(sp):
            for n in range(NT // CH):
                if n >= 2:
                    sp.wait_ge(summed, n - 1)
                sp.dma_start(y[:, n % 2].rearrange("p t k d -> p t (k d)"), rows[:, CH * n:CH * n + CH]).then_inc(y_in[n % 2], 16)

        @block.vector
        def _(dve):
            for n in range(NT // CH):
                dve.wait_ge(y_in[n % 2], 16 * (n // 2 + 1))
                part = g.h1[:, CH * n:CH * n + CH, :]
                dve.tensor_tensor(part, part, y[:, n % 2, :, 0, :], ALU.add).then_inc(added, 1)
                dve.wait_ge(added, n + 1)
                dve.tensor_tensor(part, part, y[:, n % 2, :, 1, :], ALU.add).then_inc(summed, 1)

        @block.scalar
        def _(act):
            for n in range(NT // CH):
                act.wait_ge(summed, n + 1)
                act.dma_start(out_rows[:, CH * n:CH * n + CH], g.h1[:, CH * n:CH * n + CH, :]).then_inc(stored, 16)
            act.wait_ge(stored, 16 * (NT // CH))


def tower(nc, ins, out):
    with ExitStack() as whole:
        def held(name, shape, dt=F32):
            return whole.enter_context(nc.sbuf_tensor(name, shape, dt))

        def sem(name):
            return whole.enter_context(nc.semaphore(name))

        g = Parts()
        g.PS = whole.enter_context(nc.psum_tensor("PS", [P, 8, 512], F32))
        g.xrows = nc.dram_tensor("xrows", (T, D), F32, kind="Internal").ap()
        g.ypair = nc.dram_tensor("ypair", (2 * T, D), F32, kind="Internal").ap()
        g.ident = held("ident", [P, P])
        g.identb = held("identb", [P, P], BF16)
        g.fold_sel = held("fold_sel", [P, 2, 32])
        g.tri = held("tri", [P, P])
        g.ones = held("ones", [P, P])
        g.iota_i = held("iota_i", [P, P], I32)
        g.iota_r = held("iota_r", [P, P])
        g.iota_pk = held("iota_pk", [P, 2])
        g.iota_p = held("iota_p", [P, 1], I32)
        g.part_r = held("part_r", [P, 1])
        g.part_c = held("part_c", [P, 2])
        g.g_pair = held("g_pair", [P, KT, D])
        g.h_bias = held("h_bias", [P, KT, D])
        g.resid = held("resid", [XROWS, D])
        g.z = held("z", [NR, NBATCH, H, NJ, NB])
        g.xT = held("xT", [XROWS, T + S])
        g.idx = held("idx", [P, ETILES], I32)
        g.idx_tok = held("idx_tok", [P, ETILES], I32)
        g.slot_w = held("slot_w", [P, ETILES])
        g.tile_expert = held("tile_expert", [1, ETILES], I32)
        g.flag = held("flag", [1, 1], I32)
        g.iota_e = g.iota_r[:, 0:E]
        g.x_in, g.gathered, g.w_in, g.weights_ready = sem("x_in"), sem("gathered"), sem("w_in"), sem("weights_ready")

        def phase(run, *args):
            with ExitStack() as own:
                run(*args, sem, lambda name, shape, dt=F32: own.enter_context(nc.sbuf_tensor(name, shape, dt)))

        with ExitStack() as attending:
            def here(name, shape, dt=F32):
                return attending.enter_context(nc.sbuf_tensor(name, shape, dt))

            g.xi = here("xi", [P, NT], I32)
            g.cw = here("cw", [P, NT, NB])
            g.mg = here("mg", [XROWS, D])
            g.vb = here("vb", [P, NB * NB])
            g.kr = here("kr", [XROWS, H * PART])
            g.xtok = here("xtok", [P, NT, XROWS])
            g.akz = here("akz", [P, 4, T], BF16)
            g.va = here("va", [P, KT, 4, PART])
            phase(weights_phase, nc, g, ins)
            phase(tokens_phase, nc, g)
            phase(row_maxima_phase, nc, g)
            phase(attention_phase, nc, g)
        g.h1 = held("h1", [P, NT, D])
        g.w13_s = held("w13_s", [P, 2, E, 2 * FF])
        phase(routing_phase, nc, g, ins["router"], ins["w13"])
        phase(experts_phase, nc, g, ins["w2"])
        phase(output_phase, nc, g, out)


def kernel(**inputs):
    import numpy as np
    import concourse.bacc as bacc
    from concourse import mybir as mb
    from concourse.bass_utils import run_bass_kernel_spmd as run

    given = {k: np.asarray(v) for k, v in inputs.items()}
    bv, bo = given["L0_attn_bv"], given["L0_attn_bo"]
    arrays = {
        "x_t": np.ascontiguousarray(given["x"].reshape(NT, P).T),
        "coeff": np.ascontiguousarray(given["L0_tok_coeff_weight"]),
        "bases": np.ascontiguousarray(given["L0_tok_base_embed_weight"]),
        "lbias": np.ascontiguousarray(given["L0_tok_lang_bias"]),
        "wvT": np.ascontiguousarray(given["L0_attn_Wv"].T),
        "bv_row": np.ascontiguousarray(bv.reshape(1, D)),
        "bv_col": np.ascontiguousarray(bv.reshape(2, P).T),
        "woT": np.ascontiguousarray(given["L0_attn_Wo"].T),
        "bo": np.ascontiguousarray(bo.reshape(1, D)),
        "router": np.ascontiguousarray(given["L0_ffn_moe_router"]),
        "w13": np.ascontiguousarray(given["L0_ffn_moe_w13"]),
        "w2": np.ascontiguousarray(given["L0_ffn_moe_w2"]),
    }
    nc = bacc.Bacc("TRN2", target_bir_lowering=False, num_devices=1)
    ins = {name: nc.dram_tensor(name, a.shape, mb.dt.from_np(a.dtype), kind="ExternalInput").ap()
           for name, a in arrays.items()}
    out = nc.dram_tensor("out", (NBATCH, S, D), F32, kind="ExternalOutput").ap()
    tower(nc, ins, out)
    r = run(nc, [arrays], core_ids=[0])
    return r.results[0]["out"]
```

```python
from contextlib import ExitStack

import concourse.bass as bass
from concourse import mybir

F32 = mybir.dt.float32
BF16 = mybir.dt.bfloat16
F16 = mybir.dt.float16
I32 = mybir.dt.int32
U32 = mybir.dt.uint32
ALU = mybir.AluOpType
ACT = mybir.ActivationFunctionType
X = mybir.AxisListType.X
ds = bass.ds

P = 128
NBATCH, S, D = 4, 1024, 256
T = NBATCH * S
NT = T // P
KT = S // P
H = 16
DK = D // H
NB = 4
NA = NB + 1
E, FF = 8, 512
PART = 32
NSPLIT = 6
HG = H // 4
XR0 = 64
XC0 = XR0 + NA
XROWS = XC0 + NB
NJ = D // DK
NR = S // NJ
ETILES = 2 * T // P + E
ECOLS = ETILES + 2
SAFE = 40.0
FREE = 2
UN = 4 * KT
EPS = 1e-5




class Parts:
    pass


class Chain:

    def __init__(self, eng, sem):
        self.eng, self.sem, self.n = eng, sem, 0

    def __call__(self, instruction):
        self.n += 1
        instruction.then_inc(self.sem, 1)
        self.eng.wait_ge(self.sem, self.n)


def newton(dve, link, out, var, t1):
    link(dve.tensor_tensor(t1, out, out, ALU.mult))
    link(dve.tensor_tensor(t1, t1, var, ALU.mult))
    link(dve.tensor_scalar(t1, t1, -0.5, 1.5, ALU.mult, ALU.add))
    link(dve.tensor_tensor(out, out, t1, ALU.mult))


def weights_phase(nc, g, ins, sem, tmp):
    PS = g.PS
    base_s, lb_s, cst_s = tmp("base_s", [NB, D]), tmp("lb_s", [NB, D]), tmp("cst_s", [NB, D])
    bt, bc, msum = tmp("bt", [NB, D]), tmp("bc", [NB, D]), tmp("msum", [NB, 2])
    wvT_s, woT_s = tmp("wvT_s", [P, 2, D]), tmp("woT_s", [P, 2, D])
    bcT, bcT_wide = tmp("bcT", [P, 2, NB]), tmp("bcT_wide", [P, 2, NB, P])
    m5T, bv_s = tmp("m5T", [P, 2, NA]), tmp("bv_s", [P, 2])
    rep, kmov = tmp("rep", [P, 2, PART]), tmp("kmov", [P, 2, H, PART])
    head_mask, mmask = tmp("head_mask", [P, 2, H]), tmp("mmask", [P, 2, H, NA])
    mod_i, mod_sel = tmp("mod_i", [P, P], I32), tmp("mod_sel", [P, P])
    m_rep, m_blk, bias_wide = tmp("m_rep", [P, H, NA]), tmp("m_blk", [P, 2, H, NJ, NB]), tmp("bias_wide", [P, H, NR])

    pool_step, const_ready, const_dve = sem("pool_step"), sem("const_ready"), sem("const_dve")
    small_in, wv_in, wo_in, ex_in = sem("small_in"), sem("wv_in"), sem("wo_in"), sem("ex_in")
    dve_step, pe_step = sem("w_dve_step"), sem("w_pe_step")
    gathered, x_in, ready = g.gathered, g.x_in, g.weights_ready

    BC, BCT, M5T, KMOV, MMASK, MREP = range(1, 7)
    copied = sem("w_copied")
    dve_out = sem("w_dve_out")

    with nc.Block() as block:
        @block.sync
        def _(sp):
            sp.dma_start(g.xi[:], ins["x_t"]).then_inc(x_in, 16)
            sp.dma_start(base_s[:], ins["bases"]).then_inc(small_in, 16)
            sp.dma_start(lb_s[:], ins["lbias"]).then_inc(small_in, 16)
            for n in range(NB):
                sp.dma_start(cst_s[n:n + 1, :], ins["lbias"][2:3, :]).then_inc(small_in, 16)
            sp.dma_start(bv_s[:], ins["bv_col"]).then_inc(small_in, 16)
            sp.dma_start(g.mg[XR0 + NB:XC0, :], ins["bv_row"]).then_inc(small_in, 16)
            sp.dma_start(wvT_s[:], ins["wvT"].rearrange("(c p) e -> p c e", p=P)).then_inc(wv_in, 16)
            sp.dma_start(woT_s[:], ins["woT"].rearrange("(c p) e -> p c e", p=P)).then_inc(wo_in, 16)
            sp.wait_ge(const_ready, 1)
            sp.dma_start(g.resid[XC0 - 1:XC0, :], ins["bo"]).then_inc(ex_in, 16)
            sp.wait_ge(dve_out, BC)
            sp.dma_start(g.resid[XC0:XROWS, :], bt[:]).then_inc(ex_in, 16)
            sp.wait_ge(ex_in, 32)

        @block.gpsimd
        def _(pool):
            step = Chain(pool, pool_step)
            pool.wait_ge(x_in, 16)
            for t in range(NT):
                pool.indirect_dma_start(g.cw[:, t, :], None, ins["coeff"],
                                        bass.IndirectOffsetOnAxis(g.xi[:, t:t + 1].bitcast(U32), 0)).then_inc(gathered, 16)
                if t == 0:
                    step(pool.memset(g.ident[:], 0.0))
                    step(pool.affine_select(g.ident[:], g.ident[:], [[-1, P]], ALU.not_equal, 1.0, 0, 1))
                    step(pool.tensor_copy(g.identb[:], g.ident[:]))
                    step(pool.tensor_copy(g.identh[:], g.ident[:]))
                    step(pool.memset(head_mask[:], 1.0))
                    step(pool.affine_select(head_mask[:], head_mask[:], [[P, 2], [-DK, H]], ALU.is_ge, 0.0, 0, 1))
                    step(pool.affine_select(head_mask[:], head_mask[:], [[-P, 2], [DK, H]], ALU.is_ge, 0.0, DK - 1, -1))
                    step(pool.iota(mod_i[:], [[1, P]], P, -1))
                    step(pool.memset(g.resid[:], 0.0))
                    step(pool.memset(g.kr[:], 0.0))
                    ones_at = g.kr[0:H].rearrange("p (h r) -> p h r", h=H)[:, :, 0:NSPLIT * NA]
                    ones_at = ones_at.rearrange("p h (s n) -> p h s n", n=NA)[:, :, :, NB]
                    step(pool.affine_select(ones_at, ones_at, [[-1, H], [0, NSPLIT]], ALU.not_equal, 1.0, 0, 1))
                    pool.iota(g.iota_p[:], [[0, 1]], 0, 1).then_inc(const_ready, 1)
            step(pool.memset(g.fold_sel[:], 0.0))
            for k in range(4):
                step(pool.affine_select(g.fold_sel[:, k % 2, :], g.fold_sel[:, k % 2, :], [[-1, 32]],
                                        ALU.not_equal, 1.0, -32 * k, 1))
            step(pool.memset(g.ones[:], 1.0))
            step(pool.affine_select(g.tri[:], g.ones[:], [[1, P]], ALU.is_gt, 0.0, 0, -1))
            step(pool.iota(g.iota_i[:], [[1, P]], 0, 0))
            step(pool.tensor_copy(g.iota_r[:], g.iota_i[:]))
            step(pool.tensor_copy(g.iota_b[:], g.iota_i[:]))
            step(pool.iota(g.iota_i[:, 0:2], [[1, 2]], 1, 2))
            step(pool.tensor_copy(g.iota_pk[:], g.iota_i[:, 0:2]))
            pool.memset(g.akz[:], 0.0)
            pool.memset(g.va[:], 0.0).then_inc(ready, 1)

        @block.vector
        def _(dve):
            link = Chain(dve, dve_step)

            def give(instruction):
                instruction.then_inc(dve_out, 1)

            dve.wait_ge(small_in, 16 * 8)
            link(dve.tensor_tensor(base_s[:], base_s[:], lb_s[:], ALU.add))
            link(dve.tensor_scalar(cst_s[:], cst_s[:], 0.1, None, ALU.mult))
            link(dve.scalar_tensor_tensor(bt[:], base_s[:], float(D) ** 0.5, cst_s[:], ALU.mult, ALU.add))
            link(dve.reduce_sum(msum[:, 0:1], bt[:], X))
            link(dve.tensor_scalar(msum[:, 1:2], msum[:, 0:1], -1.0 / D, None, ALU.mult))
            give(dve.tensor_scalar(bc[:], bt[:], msum[:, 1:2], None, ALU.add))
            dve.wait_ge(pe_step, 1)
            give(dve.tensor_copy(bcT[:], PS[:, 0, 0:2 * NB].rearrange("p (c n) -> p c n", c=2)))
            dve.wait_ge(dve_out, BCT)
            link(dve.tensor_copy(bcT_wide[:], bcT[:].unsqueeze(3).to_broadcast([P, 2, NB, P])))
            dve.wait_ge(pe_step, 2)
            dve.tensor_copy(m5T[:, :, NB:NA], bv_s[:].unsqueeze(2))
            give(dve.tensor_copy(m5T[:, :, 0:NB], PS[:, 1, 0:2 * NB].rearrange("p (c n) -> p c n", c=2)))
            dve.wait_ge(dve_out, M5T)
            link(dve.memset(rep[:], 0.0))
            link(dve.tensor_scalar(rep[:, :, 0:NSPLIT * NA].rearrange("p c (s n) -> p c s n", n=NA),
                                   m5T[:].unsqueeze(2).to_broadcast([P, 2, NSPLIT, NA]), 1.0 / DK ** 0.5, None, ALU.mult))
            dve.wait_ge(const_ready, 1)
            for c in range(2):
                last = dve.tensor_tensor(kmov[:, c], rep[:, c].unsqueeze(1).to_broadcast([P, H, PART]),
                                         head_mask[:, c].unsqueeze(2).to_broadcast([P, H, PART]), ALU.mult)
            give(last)
            for c in range(2):
                last = dve.tensor_tensor(mmask[:, c], m5T[:, c].unsqueeze(1).to_broadcast([P, H, NA]),
                                         head_mask[:, c].unsqueeze(2).to_broadcast([P, H, NA]), ALU.mult)
            link(dve.tensor_scalar(mod_i[:], mod_i[:], DK - 1, None, ALU.bitwise_and))
            give(dve.tensor_scalar(mod_sel[:], mod_i[:], 0.0, None, ALU.is_equal))
            link(dve.tensor_scalar(g.iota_p[:], g.iota_p[:], PART - 1, None, ALU.bitwise_and))
            link(dve.tensor_copy(g.part_r[:], g.iota_p[:]))
            for col, first in ((0, 3 * NA), (1, 5 * NA)):
                dve.tensor_scalar(g.part_c[:, col:col + 1], g.part_r[:], float(first), -1.0, ALU.is_ge, ALU.mult)
            dve.wait_ge(pe_step, 3)
            dve.tensor_copy(g.mg[XR0:XR0 + NB, :], PS[XR0:XR0 + NB, 2, 0:D])
            dve.tensor_scalar(g.vb[:], PS[:, 3, 0:NB * NB], 1.0 / D, None, ALU.mult)
            dve.wait_ge(pe_step, 4)
            dve.tensor_copy(g.kr[XR0:XC0, :], PS[XR0:XC0, 4, :])
            dve.wait_ge(pe_step, 5)
            link(dve.tensor_copy(m_rep[:].rearrange("p h n -> p (h n)"), PS[:, 5, 0:H * NA]))
            for c in range(2):
                dve.tensor_tensor(m_blk[:, c], m_rep[:, :, 0:NB].unsqueeze(2).to_broadcast([P, H, NJ, NB]),
                                  head_mask[:, c].unsqueeze(1).unsqueeze(3).to_broadcast([P, H, NJ, NB]), ALU.mult)
            give(dve.tensor_copy(bias_wide[:], m_rep[:, :, NB:NA].to_broadcast([P, H, NR])))
            for k in range(KT):
                dve.wait_ge(pe_step, 6 + k)
                dve.tensor_copy(g.g_pair[:, k, :], PS[:, k % 4, 0:D])
                dve.tensor_copy(g.h_bias[:, k, :], PS[:, k % 4, D:2 * D]).then_inc(copied, 1)

        @block.tensor
        def _(pe):
            pe.wait_ge(const_ready, 1)
            pe.wait_ge(dve_out, BC)
            for c in range(2):
                last = pe.transpose(PS[:, 0, NB * c:NB * c + NB], bc[:, P * c:P * c + P], g.ident[0:NB, 0:NB])
            last.then_inc(pe_step, 1)
            pe.wait_ge(dve_out, BCT)
            pe.wait_ge(wv_in, 16)
            for c in range(2):
                for k in range(2):
                    last = pe.matmul(PS[:, 1, NB * c:NB * c + NB], wvT_s[:, k, P * c:P * c + P], bcT[:, k, :],
                                     start=k == 0, stop=k == 1)
            last.then_inc(pe_step, 1)
            for k in range(2):
                pe.matmul(PS[XR0:XR0 + NB, 2, 0:D], bcT[:, k, :], wvT_s[:, k, :], start=k == 0, stop=k == 1)
            pe.wait_ge(dve_step, 6)
            for m in range(NB):
                for k in range(2):
                    last = pe.matmul(PS[:, 3, NB * m:NB * m + NB], bcT_wide[:, k, m, :], bcT[:, k, :],
                                     start=k == 0, stop=k == 1)
            last.then_inc(pe_step, 1)
            pe.wait_ge(dve_out, KMOV)
            for k in range(2):
                last = pe.matmul(PS[XR0:XC0, 4, :], m5T[:, k, :], kmov[:, k].rearrange("p h r -> p (h r)"),
                                 start=k == 0, stop=k == 1)
            last.then_inc(pe_step, 1)
            pe.wait_ge(dve_out, MMASK)
            for k in range(2):
                last = pe.matmul(PS[:, 5, 0:H * NA], mod_sel[:], mmask[:, k].rearrange("p h n -> p (h n)"),
                                 start=k == 0, stop=k == 1)
            last.then_inc(pe_step, 1)
            pe.wait_ge(dve_out, MREP)
            pe.wait_ge(wo_in, 16)
            for n in range(KT):
                if n >= 4:
                    pe.wait_ge(copied, n - 3)
                for c in range(2):
                    pe.matmul(PS[:, n % 4, 0:D], m_blk[:, c, 2 * n:2 * n + 2].rearrange("p h j n -> p (h j n)"),
                              woT_s[:, c, :], start=c == 0, stop=c == 1)
                for c in range(2):
                    last = pe.matmul(PS[:, n % 4, D:2 * D], bias_wide[:, 2 * n:2 * n + 2].rearrange("p h r -> p (h r)"),
                                     woT_s[:, c, :], start=c == 0, stop=c == 1)
                last.then_inc(pe_step, 1)


def tokens_phase(nc, g, sem, tmp):
    PS = g.PS
    tmax, csum, quad = tmp("tmax", [P, NT]), tmp("csum", [P, NT]), tmp("quad", [P, NT, NB, NB])
    var, t1, rstd = tmp("var", [P, NT]), tmp("t1", [P, NT]), tmp("rstd", [P, NT])
    a_part, a_res = tmp("a_part", [P, 3, NT, NA], BF16), tmp("a_res", [P, 2, NT, NA])
    ak_one, ak_rep = tmp("ak_one", [P, NT, PART], BF16), tmp("ak_rep", [P, NT, 4, PART], BF16)
    p_sq, diag, dmax = tmp("p_sq", [P, 2, 2 * D]), tmp("diag", [P, NT, H]), tmp("dmax", [P, H])
    gmax, gall = tmp("gmax", [H, 2]), tmp("gall", [1, 2])
    dve_step, dve_out, act_step, pe_step = sem("t_dve_step"), sem("t_dve_out"), sem("t_act_step"), sem("t_pe_step")
    xT_mm, xT_copied = sem("xT_mm"), [sem("xT_copied_dve"), sem("xT_copied_act")]
    ak_mm, ak_copied = sem("ak_mm"), [sem("ak_copied_dve"), sem("ak_copied_act")]
    p_mm, p_squared, p_summed = sem("p_mm"), sem("p_squared"), sem("p_summed")
    z_c = g.xtok[:, :, XC0:XROWS]
    SUBMAX, VAR, XTOK, AKREP, DMAX, GMAX, SHIFT = range(1, 8)

    with nc.Block() as block:
        @block.vector
        def _(dve):
            link = Chain(dve, dve_step)

            def give(instruction):
                instruction.then_inc(dve_out, 1)

            dve.wait_ge(g.gathered, 16 * NT)
            dve.wait_ge(g.weights_ready, 1)
            link(dve.tensor_reduce(tmax[:], g.cw[:], X, ALU.max))
            give(dve.tensor_tensor(g.cw[:], g.cw[:], tmax[:].unsqueeze(2).to_broadcast([P, NT, NB]), ALU.subtract))
            dve.wait_ge(act_step, 1)
            link(dve.reduce_sum(csum[:], g.cw[:], X))
            link(dve.reciprocal(csum[:], csum[:]))
            link(dve.tensor_tensor(z_c, g.cw[:], csum[:].unsqueeze(2).to_broadcast([P, NT, NB]), ALU.mult))
            for m in range(NB):
                last = dve.tensor_tensor(quad[:, :, m, :], z_c, z_c[:, :, m:m + 1].to_broadcast([P, NT, NB]), ALU.mult)
            link(last)
            qv = quad[:].rearrange("p t m n -> p t (m n)")
            link(dve.tensor_tensor(qv, qv, g.vb[:].unsqueeze(1).to_broadcast([P, NT, NB * NB]), ALU.mult))
            link(dve.reduce_sum(var[:], qv, X))
            give(dve.tensor_scalar(var[:], var[:], 0.0, EPS, ALU.max, ALU.add))
            dve.wait_ge(act_step, 2)
            link(dve.reciprocal(rstd[:], rstd[:]))
            newton(dve, link, rstd[:], var[:], t1[:])
            dve.memset(g.xtok[:, :, 0:XR0], 0.0)
            dve.memset(g.xtok[:, :, XR0 + NB:XC0], 1.0)
            link(dve.tensor_tensor(g.xtok[:, :, XR0:XR0 + NB], z_c, rstd[:].unsqueeze(2).to_broadcast([P, NT, NB]), ALU.mult))
            give(dve.memset(g.xT[:, T:T + S], 0.0))
            xa = g.xtok[:, :, XR0:XC0]
            link(dve.tensor_copy(a_part[:, 0], xa))
            link(dve.tensor_tensor(a_res[:, 0], xa, a_part[:, 0], ALU.subtract))
            link(dve.tensor_copy(a_part[:, 1], a_res[:, 0]))
            link(dve.tensor_tensor(a_res[:, 1], a_res[:, 0], a_part[:, 1], ALU.subtract))
            link(dve.tensor_copy(a_part[:, 2], a_res[:, 1]))
            dve.memset(ak_one[:, :, NSPLIT * NA:PART], 0.0)
            for s, part in enumerate((0, 1, 2, 0, 1, 0)):
                last = dve.tensor_copy(ak_one[:, :, NA * s:NA * s + NA], a_part[:, part])
            link(last)
            give(dve.tensor_copy(ak_rep[:], ak_one[:].unsqueeze(2).to_broadcast([P, NT, 4, PART])))
            for n in range(0, 8, 2):
                dve.wait_ge(xT_mm, n + 1)
                dve.tensor_copy(g.xT[:, 512 * n:512 * n + 512], PS[0:XROWS, n, :]).then_inc(xT_copied[0], 1)
            for n in range(0, 16, 2):
                b, k = n // 4, n % 4
                dve.wait_ge(ak_mm, b + 1)
                dve.tensor_copy(g.akz[32 * k:32 * k + 32, k, S * b:S * b + S],
                                PS[32 * k:32 * k + 32, b, :].bitcast(BF16)).then_inc(ak_copied[0], 1)
            for n in range(NT // 2):
                dve.wait_ge(p_squared, n + 1)
                dve.reduce_sum(diag[:, 2 * n:2 * n + 2, :].rearrange("p t h -> p (t h)"),
                               p_sq[:, n % 2].rearrange("p (g d) -> p g d", d=DK), X).then_inc(p_summed, 1)
            dve.wait_ge(p_summed, NT // 2)
            give(dve.tensor_reduce(dmax[:], diag[:].rearrange("p t h -> p h t"), X, ALU.max))
            dve.wait_ge(pe_step, 1)
            link(dve.tensor_reduce(gmax[:, 0:1], PS[0:H, 0, 0:P], X, ALU.max))
            give(dve.tensor_scalar(gmax[:, 1:2], gmax[:, 0:1], -1.0 / DK ** 0.5, None, ALU.mult))
            dve.wait_ge(dve_out, GMAX)
            dve.tensor_scalar(g.xT[0:H, 0:T], g.xT[0:H, 0:T], gmax[:, 1:2], None, ALU.add)
            dve.wait_ge(pe_step, 2)
            link(dve.tensor_reduce(gall[:, 0:1], PS[0:1, 1, 0:H], X, ALU.max))
            link(dve.tensor_scalar(gall[:, 1:2], gall[:, 0:1], SAFE * DK ** 0.5, None, ALU.is_le))
            link(dve.tensor_scalar(gall[:, 0:1], gall[:, 1:2], -1.0, 1.0, ALU.mult, ALU.add))
            give(dve.tensor_copy(g.flag[:], gall[:, 0:1]))

        @block.scalar
        def _(act):
            act.wait_ge(dve_out, SUBMAX)
            act.activation(g.cw[:], g.cw[:], ACT.Exp).then_inc(act_step, 1)
            act.wait_ge(dve_out, VAR)
            act.activation(rstd[:], var[:], ACT.Sqrt).then_inc(act_step, 1)
            for n in range(1, 8, 2):
                act.wait_ge(xT_mm, n + 1)
                act.copy(g.xT[:, 512 * n:512 * n + 512], PS[0:XROWS, n, :]).then_inc(xT_copied[1], 1)
            for n in range(1, 16, 2):
                b, k = n // 4, n % 4
                act.wait_ge(ak_mm, b + 1)
                act.copy(g.akz[32 * k:32 * k + 32, k, S * b:S * b + S],
                         PS[32 * k:32 * k + 32, b, :].bitcast(BF16)).then_inc(ak_copied[1], 1)
            for n in range(NT // 2):
                act.wait_ge(p_mm, n + 1)
                if n >= 2:
                    act.wait_ge(p_summed, n - 1)
                act.activation(p_sq[:, n % 2], PS[:, 4 + n % 4, :], ACT.Square).then_inc(p_squared, 1)

        @block.tensor
        def _(pe):
            pe.wait_ge(dve_out, XTOK)
            for t in range(NT):
                last = pe.transpose(PS[0:XROWS, t // 4, P * (t % 4):P * (t % 4) + P], g.xtok[:, t, :], g.ident[:])
                if t % 4 == 3:
                    last.then_inc(xT_mm, 1)
            pe.wait_ge(dve_out, AKREP)
            for b in range(NBATCH):
                pe.wait_ge(xT_copied[b % 2], b // 2 + 1)
                for t in range(KT):
                    last = pe.transpose(PS[:, b, :].bitcast(BF16)[:, P * t:P * t + P],
                                        ak_rep[:, KT * b + t].rearrange("p k r -> p (k r)"), g.identb[:])
                last.then_inc(ak_mm, 1)
            pe.wait_ge(xT_copied[0], 4)
            pe.wait_ge(xT_copied[1], 4)
            for n in range(NT // 2):
                if n >= 4:
                    pe.wait_ge(p_squared, n - 3)
                for i in range(2):
                    t = 2 * n + i
                    last = pe.matmul(PS[:, 4 + n % 4, D * i:D * i + D], g.xT[XR0:XC0, P * t:P * t + P],
                                     g.mg[XR0:XC0, :], start=True, stop=True)
                last.then_inc(p_mm, 1)
            pe.wait_ge(dve_out, DMAX)
            pe.wait_ge(ak_copied[0], 8)
            pe.wait_ge(ak_copied[1], 8)
            pe.transpose(PS[0:H, 0, 0:P], dmax[:], g.ident[:]).then_inc(pe_step, 1)
            pe.wait_ge(dve_out, GMAX)
            pe.transpose(PS[0:1, 1, 0:H], gmax[:, 0:1], g.ident[0:H, 0:H]).then_inc(pe_step, 1)


def row_maxima_phase(nc, g, sem, tmp):
    PS = g.PS
    xTr, xtile = tmp("xTr", [P, T]), tmp("xtile", [XROWS, 2, P])
    u_s, rmax = tmp("u_s", [P, HG, 4, P]), tmp("rmax", [P, NT, H])
    zeroed, replicated, u_mm, u_copied = sem("rm_zeroed"), sem("rm_replicated"), sem("rm_u_mm"), sem("rm_u_copied")
    tile_in, scored, maxed, negated = sem("rm_tile_in"), sem("rm_scored"), sem("rm_maxed"), sem("rm_negated")
    turned, taken = sem("rm_turned"), sem("rm_taken")

    with nc.Block() as block:
        @block.sync
        def _(sp):
            needed = sp.value_load(g.flag[0:1, 0:1], min_val=0, max_val=1)
            with sp.If(needed > 0):
                sp.wait_ge(zeroed, 3)
                for k in range(4):
                    sp.dma_start(xTr[32 * k:32 * k + NA, :], g.xT[XR0:XC0, 0:T]).then_inc(replicated, 16)
                sp.wait_ge(replicated, 64)

        @block.vector
        def _(dve):
            needed = dve.value_load(g.flag[0:1, 0:1], min_val=0, max_val=1)
            with dve.If(needed > 0):
                dve.sem_inc(u_copied, FREE)
                dve.sem_inc(maxed, FREE)
                dve.memset(g.xT[0:H, 0:T], 0.0).then_inc(zeroed, 1)
                dve.memset(xTr[:], 0.0).then_inc(zeroed, 1)
                dve.memset(u_s[:], 0.0).then_inc(zeroed, 1)
                dve.wait_ge(zeroed, 3)
                with dve.Fori(0, NBATCH) as b:
                    with dve.Fori(0, KT) as q:
                        t = b * KT + q
                        dve.wait_ge(u_mm, t + FREE)
                        dve.tensor_copy(xtile[:, 0, :], g.xT[:, ds(t * P, P)]).then_inc(tile_in, 1)
                        dve.wait_ge(u_mm, t + 1 + FREE)
                        dve.wait_ge(scored, t * H + FREE)
                        for k in range(4):
                            r = slice(32 * k, 32 * k + 32)
                            last = dve.tensor_copy(u_s[r, :, k, :], PS[r, 0, :].rearrange("p (h q) -> p h q", h=HG))
                        last.then_inc(u_copied, 1)
                        for h in range(H):
                            dve.wait_ge(scored, t * H + h + 1 + FREE)
                            m = 2 + 2 * (h % 2)
                            dve.tensor_reduce(rmax[:, ds(t, 1), h], PS[:, m:m + 2, :].rearrange("p b k -> p (b k)").unsqueeze(1), X, ALU.max).then_inc(maxed, 1)
                dve.wait_ge(maxed, NT * H + FREE)
                dve.tensor_scalar(g.xtok[:, :, 0:H], rmax[:], -1.0, None, ALU.mult).then_inc(negated, 1)
                for n in range(8):
                    dve.wait_ge(turned, n + 1)
                    dve.tensor_copy(g.xT[0:H, 512 * n:512 * n + 512], PS[0:H, n, :]).then_inc(taken, 1)
                dve.wait_ge(taken, 8)

        @block.tensor
        def _(pe):
            needed = pe.value_load(g.flag[0:1, 0:1], min_val=0, max_val=1)
            with pe.If(needed > 0):
                pe.sem_inc(u_mm, FREE)
                pe.sem_inc(scored, FREE)
                pe.wait_ge(replicated, 64)
                with pe.Fori(0, NBATCH) as b:
                    with pe.Fori(0, KT) as q:
                        t = b * KT + q
                        pe.wait_ge(tile_in, t + 1)
                        pe.wait_ge(u_copied, t + FREE)
                        for k in range(HG):
                            last = pe.matmul(PS[:, 0, P * k:P * k + P], g.kr[:, P * k:P * k + P], xtile[:, 0, :],
                                             start=True, stop=True)
                        last.then_inc(u_mm, 1)
                        pe.wait_ge(u_copied, t + 1 + FREE)
                        for h in range(H):
                            m = 2 + 2 * (h % 2)
                            pe.wait_ge(maxed, t * H + max(h - 1, 0) + FREE)
                            for c in range(2):
                                last = pe.matmul(PS[:, m + c, :], u_s[:, h // 4, h % 4, :],
                                                 xTr[:, ds(b * S + c * 512, 512)], start=True, stop=True)
                            last.then_inc(scored, 1)
                pe.wait_ge(negated, 1)
                for n in range(8):
                    for i in range(4):
                        last = pe.transpose(PS[0:H, n, P * i:P * i + P], g.xtok[:, 4 * n + i, 0:H], g.ident[:])
                    last.then_inc(turned, 1)


def attention_phase(nc, g, sem, tmp):
    PS = g.PS
    u1, u2 = tmp("u1", [P, 512], BF16), tmp("u2", [P, 512], BF16)
    ures = tmp("ures", [P, 512])
    qf, prob = tmp("qf", [P, HG, S], BF16), tmp("prob", [P, 4, S])
    acc_s, rden = tmp("acc_s", [P, HG, 512]), tmp("rden", [NR, HG, 8, 8])
    u_mm, u_read, u_step = sem("u_mm"), sem("u_read"), sem("u_step")
    scores_ready, exp_done, prob_used = sem("scores_ready"), sem("exp_done"), sem("prob_used")
    acc_copied, va_ready = sem("acc_copied"), sem("va_ready")
    folded, fold_read, rden_step = sem("folded"), sem("fold_read"), sem("rden_step")
    BU = HG * UN
    ACC, UB = 6, 7

    with nc.Block() as block:
        @block.tensor
        def _(pe):
            pe.sem_inc(prob_used, FREE)
            pe.sem_inc(folded, FREE)

            def query_product(b, hg, half, n):
                if not (isinstance(n, int) and n == 0):
                    pe.wait_ge(u_read, n)
                pe.matmul(PS[:, UB, :], g.kr[:, P * hg:P * hg + P], g.xT[:, ds(b * S, S)].rearrange("p (r j) -> p j r", j=NJ)[:, 8 * half:8 * half + 8, :],
                          start=True, stop=True).then_inc(u_mm, 1)

            def scores(b, n):
                hg, slot, kt, buf = n // UN, n // KT % 4, n % KT, n % 3
                if n % UN == 0:
                    pe.wait_ge(u_step, 3 * (b * (2 * HG) + 2 * hg + 2))
                if n < 3:
                    pe.wait_ge(exp_done, b * BU + FREE)
                    pe.wait_ge(fold_read, b + FREE)
                else:
                    pe.wait_ge(exp_done, b * BU + n - 2 + FREE)
                for c in range(2):
                    last = pe.matmul(PS[:, 2 * buf + c, :], g.akz[:, slot, ds(b * S + P * kt, P)],
                                     qf[:, hg, 512 * c:512 * c + 512], start=True, stop=True)
                last.then_inc(scores_ready, 1)

            def sums(b, pair):
                hg, slot = pair // (UN // 2), pair // (KT // 2) % 4
                if pair == 0:
                    pe.wait_ge(va_ready, b + 1)
                if pair % (UN // 2) == 0:
                    pe.wait_ge(acc_copied, b * HG + hg + FREE)
                pe.wait_ge(exp_done, b * BU + 2 * pair + 2 + FREE)
                for n in (2 * pair, 2 * pair + 1):
                    kt = n % KT
                    for c in range(2):
                        r = 32 * (2 * (kt % 2) + c)
                        last = pe.matmul(PS[r:r + 32, ACC, :], g.va[:, kt, slot, :], prob[:, n % 4, 512 * c:512 * c + 512],
                                         start=slot == 0 and kt < 2, stop=slot == 3 and kt >= KT - 2)
                last.then_inc(prob_used, 1)

            query_product(0, 0, 0, 0)
            query_product(0, 0, 1, 1)
            with pe.Fori(0, NBATCH) as b:
                scores(b, 0)
                scores(b, 1)
                for pair in range(BU // 2):
                    for n in (2 * pair + 2, 2 * pair + 3):
                        if n < BU:
                            scores(b, n)
                    sums(b, pair)
                    hg, at = pair // (UN // 2), pair % (UN // 2)
                    if at in (2, 8):
                        half = int(at == 8)
                        nb, nh = (b, hg + 1) if hg + 1 < HG else (b + 1, 0)
                        query_product(nb, nh, half, b * (2 * HG) + 2 * hg + 2 + half)
                pe.wait_ge(acc_copied, b * HG + HG + FREE)
                pe.wait_ge(exp_done, b * BU + BU + FREE)
                for hg in range(HG):
                    for j in range(8):
                        last = pe.matmul(PS[0:NR, hg, 64 * j:64 * j + 64], acc_s[:, hg, NR * j:NR * j + NR],
                                         g.fold_sel[:].rearrange("p c r -> p (c r)"), start=True, stop=True)
                last.then_inc(folded, 1)

        @block.scalar
        def _(act):
            act.sem_inc(exp_done, FREE)
            with act.Fori(0, NBATCH) as b:
                for n in range(BU):
                    act.wait_ge(scores_ready, b * BU + n + 1)
                    if n >= 4:
                        act.wait_ge(prob_used, b * (BU // 2) + (n - 4) // 2 + 1 + FREE)
                    else:
                        act.wait_ge(prob_used, b * (BU // 2) + FREE)
                    buf = n % 3
                    act.activation(prob[:, n % 4, :], PS[:, 2 * buf:2 * buf + 2, :].rearrange("p c q -> p (c q)"),
                                   ACT.Exp).then_inc(exp_done, 1)

        @block.vector
        def _(dve):
            dve.sem_inc(acc_copied, FREE)
            dve.sem_inc(fold_read, FREE)

            def query_features(b, hg, half, n):
                dve.wait_ge(u_mm, n + 1)
                dve.tensor_copy(u1[:], PS[:, UB, :]).then_inc(u_step, 1)
                dve.wait_ge(u_step, 3 * n + 1)
                dve.scalar_tensor_tensor(ures[:], u1[:], g.part_c[:, 0:1], PS[:, UB, :], ALU.mult, ALU.add).then_inc(u_read, 1)
                dve.wait_ge(u_read, n + 1)
                dve.tensor_copy(u2[:], ures[:]).then_inc(u_step, 1)
                dve.wait_ge(u_step, 3 * n + 2)
                dve.scalar_tensor_tensor(qf[:, hg, 512 * half:512 * half + 512], u2[:], g.part_c[:, 1:2], ures[:],
                                         ALU.mult, ALU.add).then_inc(u_step, 1)
                dve.wait_ge(u_step, 3 * n + 3)

            query_features(0, 0, 0, 0)
            query_features(0, 0, 1, 1)
            with dve.Fori(0, NBATCH) as b:
                for slot in range(4):
                    last = dve.tensor_copy(g.va[:, :, slot, 8 * slot:8 * slot + NA], g.xtok[:, ds(b * KT, KT), XR0:XC0])
                last.then_inc(va_ready, 1)
                for hg in range(HG):
                    for half in range(2):
                        nb, nh = (b, hg + 1) if hg + 1 < HG else (b + 1, 0)
                        if half == 0:
                            dve.wait_ge(scores_ready, b * BU + UN * hg + 1)
                        query_features(nb, nh, half, b * (2 * HG) + 2 * hg + 2 + half)
                    if hg == 0:
                        dve.wait_ge(folded, b + FREE)
                    dve.wait_ge(prob_used, b * (BU // 2) + (hg + 1) * (UN // 2) + FREE)
                    dve.tensor_copy(acc_s[:, hg, :], PS[:, ACC, :]).then_inc(acc_copied, 1)
                dve.wait_ge(folded, b + 1 + FREE)
                for hg in range(HG):
                    sums = PS[0:NR, hg, :].rearrange("p (j s r) -> p j s r", j=8, s=8)
                    last = dve.reciprocal(rden[:, hg], sums[:, :, :, NB])
                last.then_inc(rden_step, 1)
                dve.wait_ge(rden_step, b + 1)
                for hg in range(HG):
                    for c in range(2):
                        sums = PS[0:NR, hg, :].rearrange("p (j c s r) -> p c s j r", j=8, c=2, s=4)
                        out = g.z[:, ds(b, 1), 4 * hg:4 * hg + 4, 8 * c:8 * c + 8, :].rearrange("p b s j n -> p (b s) j n")
                        last = dve.tensor_tensor(out, sums[:, c, :, :, 0:NB],
                                                 rden[:, hg].rearrange("p j (c s) -> p c s j", c=2)[:, c].unsqueeze(3).to_broadcast([NR, 4, 8, NB]),
                                                 ALU.mult)
                last.then_inc(fold_read, 1)
                dve.wait_ge(fold_read, b + 1 + FREE)


def residual_phase(nc, g, sem, tmp):
    PS = g.PS
    zT = tmp("zT", [P, NT, NR])
    stats, mean_d = tmp("stats", [P, NT, 6]), tmp("mean_d", [P, NT])
    zT_mm, zT_copied = sem("zT_mm"), sem("zT_copied")
    h_mm, h_copied, h_stats, dve_step = sem("h_mm"), sem("h_copied"), sem("h_stats"), sem("h_dve_step")

    with nc.Block() as block:
        @block.tensor
        def _(pe):
            for t in range(NT):
                b, k = t // KT, t % KT
                last = pe.transpose(PS[:, b, NR * k:NR * k + NR],
                                    g.z[:, b, 2 * k:2 * k + 2].rearrange("p h j n -> p (h j n)"), g.ident[0:NR, 0:NR])
                if k == KT - 1:
                    last.then_inc(zT_mm, 1)
            for t in range(NT):
                k, bank = t % KT, 4 + t % 4
                pe.wait_ge(zT_copied, t // KT + 1)
                if t >= 4:
                    pe.wait_ge(h_copied, t - 3)
                pe.matmul(PS[:, bank, 0:D], g.xT[XR0:XROWS, P * t:P * t + P], g.resid[XR0:XROWS, :], start=True, stop=False)
                for i in range(2):
                    r = slice(NR * i, NR * i + NR)
                    last = pe.matmul(PS[r, bank, 0:D], zT[r, t, :], g.g_pair[r, k, :], start=False, stop=True)
                last.then_inc(h_mm, 1)

        @block.scalar
        def _(act):
            for b in range(NBATCH):
                act.wait_ge(zT_mm, b + 1)
                act.copy(zT[:, KT * b:KT * b + KT, :].rearrange("p t r -> p (t r)"), PS[:, b, :]).then_inc(zT_copied, 1)

        @block.vector
        def _(dve):
            link = Chain(dve, dve_step)
            for t in range(NT):
                dve.wait_ge(h_mm, t + 1)
                dve.tensor_tensor(g.h1[:, t, :], PS[:, 4 + t % 4, 0:D], g.h_bias[:, t % KT, :], ALU.add).then_inc(h_copied, 1)
                if t >= 1:
                    dve.wait_ge(h_copied, t)
                    dve.bn_stats(stats[:, t - 1, :], g.h1[:, t - 1, :]).then_inc(h_stats, 1)
            dve.wait_ge(h_copied, NT)
            dve.bn_stats(stats[:, NT - 1, :], g.h1[:, NT - 1, :]).then_inc(h_stats, 1)
            dve.wait_ge(h_stats, NT)
            dve.tensor_tensor(g.mean[:], stats[:, :, 1], stats[:, :, 4], ALU.add)
            dve.tensor_tensor(g.var[:], stats[:, :, 2], stats[:, :, 5], ALU.add)
            link(dve.tensor_tensor(mean_d[:], stats[:, :, 1], stats[:, :, 4], ALU.subtract))
            dve.tensor_scalar(g.mean[:], g.mean[:], -0.5, None, ALU.mult)
            dve.tensor_scalar(g.var[:], g.var[:], 1.0 / D, None, ALU.mult)
            link(dve.tensor_tensor(mean_d[:], mean_d[:], mean_d[:], ALU.mult))
            link(dve.tensor_scalar(mean_d[:], mean_d[:], 0.25, EPS, ALU.mult, ALU.add))
            dve.tensor_tensor(g.var[:], g.var[:], mean_d[:], ALU.add)


def routing_phase(nc, g, router, w13, w2, sem, tmp):
    PS = g.PS
    XB, WB = 4, 4
    xn, x_parts, xnT = tmp("xn", [P, XB, D]), tmp("x_parts", [P, 2, XB, 2, D], F16), tmp("xnT", [P, 2, 2, P])
    w_raw = tmp("w_raw", [P, WB, 2 * FF])
    t1, rstd, rt_s = tmp("t1_2", [P, NT]), tmp("rstd2", [P, NT]), tmp("rt_s", [P, 2, E])
    logits, top, top_i = tmp("logits", [P, NT, E]), tmp("top", [P, NT, 8]), tmp("top_i", [P, NT, 8], U32)
    top_f = tmp("top_f", [P, 2, NT])
    picked, count = tmp("picked", [P, 2, NT, E]), [tmp("count0", [P, E, NT]), tmp("count1", [P, E, NT])]
    chosen, place, prod = tmp("chosen", [P, E, NT]), tmp("place", [P, E, NT]), tmp("prod", [P, 2, NT, E])
    tiles_i, tiles = tmp("tiles_i", [P, E], I32), tmp("tiles", [P, E])
    first, shift = [tmp(f"first{i}", [P, E]) for i in range(4)], tmp("shift", [P, E])
    pos, pos_i, pos_r, pos_j = (tmp("pos", [P, 2, NT]), tmp("pos_i", [P, 2, 2, NT], I32), tmp("pos_r", [P, 2, NT]),
                                tmp("pos_j", [P, 2, NT]))
    HB = 8
    hot_r, hot_j = tmp("hot_r", [P, HB, P], BF16), tmp("hot_j", [P, HB, 2, ECOLS], BF16)
    idx_f, te_f = tmp("idx_f", [P, 2, ECOLS]), tmp("te_f", [P, 2, ECOLS])
    xn_ready, hi_ready, lo_ready = sem("xn_ready"), sem("hi_ready"), sem("lo_ready")
    xn_turned, xnT_copied, l_mm, rt_in = sem("xn_turned"), sem("xnT_copied"), sem("l_mm"), sem("rt_in")
    w_in, w_hi, w_lo = [sem(f"w_in{k}") for k in range(WB)], sem("w_hi"), sem("w_lo")
    x_stored = [sem("x_stored0"), sem("x_stored1")]
    dve_step, dve_out, act_step, pe_step = sem("r_dve_step"), sem("r_dve_out"), sem("r_act_step"), sem("r_pe_step")
    hot_ready, hot_used = sem("hot_ready"), sem("hot_used")
    TOPDIFF, ROWTOT = range(1, 3)

    pieces = []
    for e in range(E):
        for c in range(2):
            pieces.append((w13[e, P * c:P * c + P, :], g.w13_p[:, 0, c, e, :], g.w13_p[:, 1, c, e, :], None))
        pieces.append((w2[e].rearrange("(c p) d -> p c d", p=P), g.w2_p[:, 0, :, e, :], g.w2_p[:, 1, :, e, :], 4))

    def raw(n):
        piece = w_raw[:, n % WB, :]
        return piece.rearrange("p (c d) -> p c d", c=4) if pieces[n][3] else piece

    with nc.Block() as block:
        @block.sync
        def _(sp):
            sp.dma_start(rt_s[:], router.rearrange("(c p) e -> p c e", p=P)).then_inc(rt_in, 16)
            for n in range(len(pieces)):
                if n >= WB:
                    sp.wait_ge(w_lo, n - WB + 1)
                sp.dma_start(raw(n), pieces[n][0]).then_inc(w_in[n % WB], 16)
            for k in range(2):
                sp.wait_ge(x_stored[k], 16 * (NT // XB // 2))

        @block.gpsimd
        def _(pool):
            for n in range(len(pieces)):
                pool.wait_ge(w_hi, n + 1)
                pool.tensor_tensor(pieces[n][2], raw(n), pieces[n][1], ALU.subtract).then_inc(w_lo, 1)

        @block.scalar
        def _(act):
            def weights(n):
                act.wait_ge(w_in[n % WB], 16 * (n // WB + 1))
                act.copy(pieces[n][1], raw(n)).then_inc(w_hi, 1)

            def turned_copy(t):
                act.wait_ge(xn_turned, t + 1)
                if t >= 2:
                    act.wait_ge(l_mm, t - 1)
                act.copy(xnT[:, t % 2].rearrange("p c q -> p (c q)"), PS[:, t % 2, 0:2 * P]).then_inc(xnT_copied, 1)

            act.activation(rstd[:], g.var[:], ACT.Sqrt).then_inc(act_step, 1)
            for t in range(NT):
                act.wait_ge(xn_ready, t + 1)
                q = t // XB
                if t % XB == 0 and q >= 2:
                    act.wait_ge(x_stored[q % 2], 16 * (q // 2))
                act.copy(x_parts[:, q % 2, t % XB, 0, :], xn[:, t % XB, :]).then_inc(hi_ready, 1)
                if t >= 1:
                    turned_copy(t - 1)
                if t < len(pieces):
                    weights(t)
                if t % XB == XB - 1:
                    act.wait_ge(lo_ready, t + 1)
                    act.dma_start(g.xrows.rearrange("(t p) d -> p t d", p=P)[:, XB * q:XB * q + XB],
                                  x_parts[:, q % 2].rearrange("p t c d -> p t (c d)")).then_inc(x_stored[q % 2], 16)
            turned_copy(NT - 1)
            act.wait_ge(dve_out, TOPDIFF)
            act.activation(g.wgt[:, 1, :], g.wgt[:, 0, :], ACT.Exp).then_inc(act_step, 1)

        @block.tensor
        def _(pe):
            def logit(t):
                pe.wait_ge(xnT_copied, t + 1)
                for c in range(2):
                    last = pe.matmul(PS[:, 3, E * t:E * t + E], xnT[:, t % 2, c, :], rt_s[:, c, :], start=c == 0, stop=c == 1)
                last.then_inc(l_mm, 1)

            pe.wait_ge(rt_in, 16)
            for t in range(NT):
                pe.wait_ge(xn_ready, t + 1)
                if t >= 2:
                    pe.wait_ge(xnT_copied, t - 1)
                for c in range(2):
                    last = pe.transpose(PS[:, t % 2, P * c:P * c + P], xn[:, t % XB, P * c:P * c + P], g.ident[:])
                last.then_inc(xn_turned, 1)
                if t >= 1:
                    logit(t - 1)
            logit(NT - 1)
            pe.wait_ge(dve_out, ROWTOT)
            pe.matmul(PS[:, 0, 0:E], g.tri[:], tiles[:], start=True, stop=True)
            pe.matmul(PS[:, 1, 0:E], g.ones[:], tiles[:], start=True, stop=True).then_inc(pe_step, 1)
            for n in range(2 * NT):
                pe.wait_ge(hot_ready, n + 1)
                pe.matmul(PS[:, 2, 0:2 * ECOLS], hot_r[:, n % HB, :], hot_j[:, n % HB].rearrange("p c j -> p (c j)"),
                          start=n == 0, stop=n == 2 * NT - 1).then_inc(hot_used, 1)

        @block.vector
        def _(dve):
            link = Chain(dve, dve_step)

            def give(instruction):
                instruction.then_inc(dve_out, 1)

            def low_part(t):
                dve.wait_ge(hi_ready, t + 1)
                parts = x_parts[:, t // XB % 2, t % XB]
                dve.tensor_tensor(parts[:, 1, :], xn[:, t % XB, :], parts[:, 0, :], ALU.subtract).then_inc(lo_ready, 1)

            dve.wait_ge(act_step, 1)
            link(dve.reciprocal(rstd[:], rstd[:]))
            newton(dve, link, rstd[:], g.var[:], t1[:])
            link(dve.tensor_tensor(g.mean[:], g.mean[:], rstd[:], ALU.mult))
            for t in range(NT):
                if t >= XB:
                    dve.wait_ge(xn_turned, t - XB + 1)
                    dve.wait_ge(lo_ready, t - XB + 1)
                dve.tensor_scalar(xn[:, t % XB, :], g.h1[:, t, :], rstd[:, t:t + 1], g.mean[:, t:t + 1],
                                  ALU.mult, ALU.add).then_inc(xn_ready, 1)
                if t >= 1:
                    low_part(t - 1)
            low_part(NT - 1)
            dve.wait_ge(l_mm, NT)
            link(dve.tensor_copy(logits[:].rearrange("p t e -> p (t e)"), PS[:, 3, 0:NT * E]))
            for t in range(NT):
                last = dve.max(top[:, t, :], logits[:, t, :])
            link(last)
            give(dve.tensor_tensor(g.wgt[:, 0, :], top[:, :, 1], top[:, :, 0], ALU.subtract))
            for t in range(NT):
                last = dve.max_index(top_i[:, t, :], top[:, t, :], logits[:, t, :])
            link(last)
            link(dve.tensor_copy(top_f[:], top_i[:, :, 0:2].rearrange("p t k -> p k t")))
            for k in range(2):
                last = dve.tensor_tensor(picked[:, k], g.iota_e.unsqueeze(1).to_broadcast([P, NT, E]),
                                         top_f[:, k].unsqueeze(2).to_broadcast([P, NT, E]), ALU.is_equal)
            link(last)
            link(dve.tensor_tensor(chosen[:], picked[:, 0].rearrange("p t e -> p e t"),
                                   picked[:, 1].rearrange("p t e -> p e t"), ALU.add))
            src, step = chosen, 1
            while step < NT:
                dst = count[(step.bit_length() - 1) % 2]
                dve.tensor_copy(dst[:, :, 0:step], src[:, :, 0:step])
                link(dve.tensor_tensor(dst[:, :, step:], src[:, :, step:], src[:, :, 0:NT - step], ALU.add))
                src, step = dst, 2 * step
            give(dve.tensor_copy(tiles[:], src[:, :, NT - 1]))
            dve.tensor_tensor(place[:], src[:], chosen[:], ALU.subtract)
            dve.wait_ge(act_step, 2)
            link(dve.tensor_scalar(g.wgt[:, 0, :], g.wgt[:, 1, :], 1.0, None, ALU.add))
            link(dve.reciprocal(g.wgt[:, 0, :], g.wgt[:, 0, :]))
            dve.tensor_tensor(g.wgt[:, 1, :], g.wgt[:, 1, :], g.wgt[:, 0, :], ALU.mult)
            dve.wait_ge(pe_step, 1)
            link(dve.tensor_scalar(shift[:], PS[:, 1, 0:E], float(P - 1), None, ALU.add))
            link(dve.tensor_copy(tiles_i[:], shift[:]))
            link(dve.tensor_scalar(tiles_i[:], tiles_i[:], 7, None, ALU.logical_shift_right))
            link(dve.tensor_copy(tiles[:], tiles_i[:]))
            src = tiles
            for i, step in enumerate((1, 2, 4)):
                dve.tensor_copy(first[i][:, 0:step], src[:, 0:step])
                link(dve.tensor_tensor(first[i][:, step:], src[:, step:], src[:, 0:E - step], ALU.add))
                src = first[i]
            link(dve.tensor_tensor(first[3][:], src[:], tiles[:], ALU.subtract))
            link(dve.scalar_tensor_tensor(shift[:], first[3][:], float(P), PS[:, 0, 0:E], ALU.mult, ALU.add))
            link(dve.tensor_tensor(place[:], place[:], shift[:].unsqueeze(2).to_broadcast([P, E, NT]), ALU.add))
            for k in range(2):
                last = dve.tensor_tensor(prod[:, k], picked[:, k], place[:].rearrange("p e t -> p t e"), ALU.mult)
            link(last)
            link(dve.reduce_sum(pos[:], prod[:], X))
            link(dve.tensor_copy(pos_i[:, 0], pos[:]))
            link(dve.tensor_scalar(pos_i[:, 1], pos_i[:, 0], 7, None, ALU.logical_shift_right))
            link(dve.tensor_copy(pos_j[:], pos_i[:, 1]))
            link(dve.scalar_tensor_tensor(pos_r[:], pos_j[:], -float(P), pos[:], ALU.mult, ALU.add))
            for n in range(2 * NT):
                t, k = n // 2, n % 2
                if n >= HB:
                    dve.wait_ge(hot_used, n - HB + 1)
                dve.tensor_scalar(hot_r[:, n % HB, :], g.iota_b[:], pos_r[:, k, t:t + 1], None, ALU.is_equal)
                dve.tensor_scalar(hot_j[:, n % HB, 0, :], g.iota_b[:, 0:ECOLS], pos_j[:, k, t:t + 1], float(2 * P * t),
                                  ALU.is_equal, ALU.mult)
                dve.tensor_scalar(hot_j[:, n % HB, 1, :], g.iota_b[:, 0:ECOLS], pos_j[:, k, t:t + 1],
                                  g.iota_pk[:, k:k + 1], ALU.is_equal, ALU.mult).then_inc(hot_ready, 1)
            link(dve.memset(te_f[:, 0, :], 0.0))
            for e in range(1, E):
                link(dve.scalar_tensor_tensor(te_f[:, e % 2, :], g.iota_r[:, 0:ECOLS], first[3][:, e:e + 1],
                                              te_f[:, (e + 1) % 2, :], ALU.is_ge, ALU.add))
            link(dve.tensor_copy(g.tile_expert[:, 1:ECOLS + 1], te_f[0:1, (E - 1) % 2, :]))
            dve.tensor_copy(g.tile_expert[:, 0:1], g.tile_expert[:, 1:2])
            dve.wait_ge(hot_used, 2 * NT)
            link(dve.tensor_copy(te_f[:], PS[:, 2, 0:2 * ECOLS].rearrange("p (c j) -> p c j", c=2)))
            link(dve.tensor_scalar(idx_f[:, 1, :], te_f[:, 1, :], 0.0, float(4 * T), ALU.is_equal, ALU.mult))
            link(dve.tensor_tensor(idx_f[:, 0, :], te_f[:, 0, :], te_f[:, 1, :], ALU.add))
            link(dve.tensor_tensor(idx_f[:, 0, :], idx_f[:, 0, :], idx_f[:, 1, :], ALU.add))
            link(dve.tensor_scalar(idx_f[:, 0, :], idx_f[:, 0, :], -1.0, None, ALU.add))
            link(dve.tensor_copy(g.idx[:], idx_f[:, 0, :]))
            link(dve.tensor_scalar(g.idx_tok[:], g.idx[:], 1, None, ALU.logical_shift_right))


def experts_phase(nc, g, sem, tmp):
    PS = g.PS
    xs, xsT = tmp("xs", [P, 2, 2 * D], F16), tmp("xsT", [P, 2, 4, P], F16)
    act_s, hid = tmp("act_s", [P, 2, FF]), tmp("hid", [P, FF])
    hid_p, hidT = tmp("hid_p", [P, 2, 2, FF], BF16), tmp("hidT", [P, 2, 8, P], BF16)
    y_s = tmp("y_s", [P, 2, D])
    xs_in, y_out = [sem("xs_in0"), sem("xs_in1")], [sem("y_out0"), sem("y_out1")]
    zeroed, x_turned, x_copied, up_mm = sem("zeroed"), sem("x_turned"), sem("x_copied"), sem("up_mm")
    silu_done, hid_ready, hid_turned = sem("silu_done"), sem("hid_ready"), sem("hid_turned")
    hidT_ready, y_mm, y_copied, y_free = sem("hidT_ready"), sem("y_mm"), sem("y_copied"), sem("y_free")
    hid_step = sem("hid_step")
    XB, HTB, YB = 0, 5, (6, 7)
    STEPS = ETILES

    def up_bank(k):
        return 1 + 2 * k

    with nc.Block() as block:
        @block.sync
        def _(sp):
            sp.sem_inc(y_free, FREE + 1)
            with sp.Fori(0, STEPS // 2) as i:
                for k in range(2):
                    sp.wait_ge(y_out[k], i * 16 + 16)
                    sp.sem_inc(y_free, 1)

        @block.gpsimd
        def _(pool):
            def gather(j):
                pool.indirect_dma_start(xs[:, j % 2, :], None, g.xrows,
                                        bass.IndirectOffsetOnAxis(g.idx_tok[:, j:j + 1].bitcast(U32), 0),
                                        bounds_check=T - 1, oob_is_err=False).then_inc(xs_in[j % 2], 16)

            pool.memset(xs[:], 0.0).then_inc(zeroed, 1)
            pool.memset(hidT[:], 0.0).then_inc(zeroed, 1)
            pool.wait_ge(zeroed, 2)
            gather(0)
            gather(1)
            for s in range(STEPS + 3):
                if s + 2 < ECOLS:
                    pool.wait_ge(x_turned, s + 1)
                    gather(s + 2)
                m = s - 3
                if m >= 0:
                    pool.wait_ge(y_copied, m + 2 + FREE)
                    pool.indirect_dma_start(g.ypair, bass.IndirectOffsetOnAxis(g.idx[:, m:m + 1].bitcast(U32), 0),
                                            y_s[:, m % 2, :], None,
                                            bounds_check=2 * T - 1, oob_is_err=False).then_inc(y_out[m % 2], 16)
            for k in range(2):
                pool.wait_ge(y_out[k], 16 * (ETILES // 2))

        @block.tensor
        def _(pe):
            def turn_x(k, arrived, copied):
                pe.wait_ge(xs_in[k], arrived)
                if copied is not None:
                    pe.wait_ge(x_copied, copied)
                for c in range(4):
                    last = pe.transpose(PS[:, XB, :].bitcast(F16)[:, P * c:P * c + P], xs[:, k, P * c:P * c + P], g.identh[:])
                last.then_inc(x_turned, 1)

            def up(k, e, copied, free):
                pe.wait_ge(x_copied, copied)
                pe.wait_ge(hid_ready, free)
                for half in range(2):
                    terms = [(c, a, w) for c in range(2) for a, w in ((0, 0), (0, 1), (1, 0))]
                    for n, (c, a, w) in enumerate(terms):
                        last = pe.matmul(PS[:, up_bank(k) + half, :], xsT[:, k, 2 * a + c, :],
                                         g.w13_p[:, w, c, ds(e, 1), FF * half:FF * half + FF].rearrange("p e f -> p (e f)"),
                                         start=n == 0, stop=n == len(terms) - 1)
                last.then_inc(up_mm, 1)

            def turn_hidden(k, ready, free):
                pe.wait_ge(hid_ready, ready)
                pe.wait_ge(hidT_ready, free)
                for a in range(2):
                    for c in range(4):
                        n = 4 * a + c
                        last = pe.transpose(PS[:, HTB, :].bitcast(BF16)[:, P * n:P * n + P],
                                            hid_p[:, k, a, P * c:P * c + P], g.identb[:])
                last.then_inc(hid_turned, 1)

            def down(k, e, ready, free):
                pe.wait_ge(hidT_ready, ready)
                pe.wait_ge(y_copied, free)
                terms = [(c, a, w) for c in range(4) for a, w in ((0, 0), (0, 1), (1, 0))]
                for n, (c, a, w) in enumerate(terms):
                    last = pe.matmul(PS[:, YB[k], 0:D], hidT[:, k, 4 * a + c, :],
                                     g.w2_p[:, w, c, ds(e, 1), :].rearrange("p e d -> p (e d)"),
                                     start=n == 0, stop=n == len(terms) - 1)
                last.then_inc(y_mm, 1)

            def expert(col):
                return pe.value_load(g.tile_expert[0:1, ds(col, 1) if not isinstance(col, int) else slice(col, col + 1)],
                                     min_val=0, max_val=E - 1)

            pe.sem_inc(hid_turned, FREE)
            pe.sem_inc(y_mm, FREE)
            pe.wait_ge(zeroed, 2)
            turn_x(0, 16, None)
            turn_x(1, 16, 1)
            up(0, expert(1), 1, FREE)
            with pe.Fori(0, STEPS // 2) as i:
                for k in range(2):
                    j = i * 2 + k
                    up(1 - k, expert(j + 2), j + 2, j + FREE)
                    turn_x(k, i * 16 + 32, j + 2)
                    turn_hidden(k, j + 1 + FREE, j + FREE)
                    down(1 - k, expert(j), j + FREE, j - 1 + FREE)
            down(1, expert(STEPS), STEPS + FREE, STEPS - 1 + FREE)

        @block.scalar
        def _(act):
            def copy_x(k, turned, used):
                act.wait_ge(x_turned, turned)
                if used is not None:
                    act.wait_ge(up_mm, used)
                act.copy(xsT[:, k].rearrange("p c q -> p (c q)"), PS[:, XB, :].bitcast(F16)[:, 0:4 * P]).then_inc(x_copied, 1)

            def silu(k, up_done, free):
                act.wait_ge(up_mm, up_done)
                act.wait_ge(hid_ready, free)
                act.activation(act_s[:, k, :], PS[:, up_bank(k), :], ACT.Silu).then_inc(silu_done, 1)

            def copy_y(k, ready, free):
                act.wait_ge(y_mm, ready)
                act.wait_ge(y_free, free)
                act.copy(y_s[:, k, :], PS[:, YB[k], 0:D]).then_inc(y_copied, 1)

            act.sem_inc(y_copied, FREE)
            copy_x(0, 1, None)
            copy_x(1, 2, None)
            silu(0, 1, FREE)
            with act.Fori(0, STEPS // 2) as i:
                for k in range(2):
                    j = i * 2 + k
                    silu(1 - k, j + 2, j + FREE)
                    copy_x(k, j + 3, j + 1)
                    copy_y(1 - k, j + 1 + FREE, j - 2 + FREE + 1)
            copy_y(1, STEPS + 1 + FREE, STEPS - 2 + FREE + 1)

        @block.vector
        def _(dve):
            def hidden(k, n, free):
                dve.wait_ge(silu_done, n + 1)
                dve.wait_ge(hid_turned, free)
                dve.tensor_tensor(hid[:], act_s[:, k, :], PS[:, up_bank(k) + 1, :], ALU.mult).then_inc(hid_step, 1)
                dve.wait_ge(hid_step, n * 2 + 1)
                dve.tensor_copy(hid_p[:, k, 0, :], hid[:]).then_inc(hid_step, 1)
                dve.wait_ge(hid_step, n * 2 + 2)
                dve.tensor_tensor(hid_p[:, k, 1, :], hid[:], hid_p[:, k, 0, :], ALU.subtract).then_inc(hid_ready, 1)
                dve.wait_ge(hid_ready, n + 1 + FREE)

            dve.sem_inc(hid_ready, FREE)
            dve.sem_inc(hidT_ready, FREE)
            hidden(0, 0, FREE)
            with dve.Fori(0, STEPS // 2) as i:
                for k in range(2):
                    j = i * 2 + k
                    dve.wait_ge(hid_turned, j + 1 + FREE)
                    dve.wait_ge(y_mm, j + FREE)
                    dve.tensor_copy(hidT[:, k].rearrange("p c q -> p (c q)"), PS[:, HTB, :].bitcast(BF16)).then_inc(hidT_ready, 1)
                    hidden(1 - k, j + 1, j + FREE)


def output_phase(nc, g, out, sem, tmp):
    CH, RING = 2, 4
    y = tmp("y_in", [P, RING, CH, 2, D])
    y_in = [sem(f"y_in{k}") for k in range(RING)]
    added, summed, stored = sem("added"), sem("summed"), sem("stored")
    rows = g.ypair.rearrange("(t p k) d -> p t (k d)", p=P, k=2)
    out_rows = out.rearrange("b (t p) d -> p (b t) d", p=P)

    with nc.Block() as block:
        @block.sync
        def _(sp):
            for n in range(NT // CH):
                if n >= RING:
                    sp.wait_ge(summed, n - RING + 1)
                sp.dma_start(y[:, n % RING].rearrange("p t k d -> p t (k d)"), rows[:, CH * n:CH * n + CH]).then_inc(y_in[n % RING], 16)

        @block.vector
        def _(dve):
            for n in range(NT // CH):
                dve.wait_ge(y_in[n % RING], 16 * (n // RING + 1))
                for k in range(2):
                    if k:
                        dve.wait_ge(added, n + 1)
                    for i in range(CH):
                        t = CH * n + i
                        last = dve.scalar_tensor_tensor(g.h1[:, t, :], y[:, n % RING, i, k, :], g.wgt[:, k, t:t + 1],
                                                        g.h1[:, t, :], ALU.mult, ALU.add)
                    last.then_inc(summed if k else added, 1)

        @block.scalar
        def _(act):
            for n in range(NT // CH):
                act.wait_ge(summed, n + 1)
                act.dma_start(out_rows[:, CH * n:CH * n + CH], g.h1[:, CH * n:CH * n + CH, :]).then_inc(stored, 16)
            act.wait_ge(stored, 16 * (NT // CH))


def tower(nc, ins, out):
    with ExitStack() as whole:
        def held(name, shape, dt=F32):
            return whole.enter_context(nc.sbuf_tensor(name, shape, dt))

        def sem(name):
            return whole.enter_context(nc.semaphore(name))

        g = Parts()
        g.PS = whole.enter_context(nc.psum_tensor("PS", [P, 8, 512], F32))
        g.xrows = nc.dram_tensor("xrows", (T, 2 * D), F16, kind="Internal").ap()
        g.ypair = nc.dram_tensor("ypair", (2 * T, D), F32, kind="Internal").ap()
        g.ident = held("ident", [P, P])
        g.identb = held("identb", [P, P], BF16)
        g.identh = held("identh", [P, P], F16)
        g.fold_sel = held("fold_sel", [P, 2, 32])
        g.tri = held("tri", [P, P])
        g.ones = held("ones", [P, P])
        g.iota_i = held("iota_i", [P, P], I32)
        g.iota_r = held("iota_r", [P, P])
        g.iota_pk = held("iota_pk", [P, 2])
        g.iota_p = held("iota_p", [P, 1], I32)
        g.part_r = held("part_r", [P, 1])
        g.part_c = held("part_c", [P, 2])
        g.flag = held("flag", [1, 1], I32)
        g.iota_b = held("iota_b", [P, P], BF16)
        g.idx, g.idx_tok = held("idx", [P, ECOLS], I32), held("idx_tok", [P, ECOLS], I32)
        g.tile_expert = held("tile_expert", [1, ECOLS + 1], I32)
        g.wgt, g.mean, g.var = held("wgt", [P, 2, NT]), held("mean", [P, NT]), held("var2", [P, NT])
        g.iota_e = g.iota_r[:, 0:E]
        g.x_in, g.gathered, g.w_in, g.weights_ready = sem("x_in"), sem("gathered"), sem("w_in"), sem("weights_ready")

        def phase(run, *args):
            with ExitStack() as own:
                run(*args, sem, lambda name, shape, dt=F32: own.enter_context(nc.sbuf_tensor(name, shape, dt)))

        g.h1 = held("h1", [P, NT, D])

        with ExitStack() as to_residual:
            def kept(name, shape, dt=F32):
                return to_residual.enter_context(nc.sbuf_tensor(name, shape, dt))

            g.g_pair, g.h_bias, g.resid = kept("g_pair", [P, KT, D]), kept("h_bias", [P, KT, D]), kept("resid", [XROWS, D])
            g.z, g.xT = kept("z", [NR, NBATCH, H, NJ, NB]), kept("xT", [XROWS, T + S])
            with ExitStack() as attending:
                def here(name, shape, dt=F32):
                    return attending.enter_context(nc.sbuf_tensor(name, shape, dt))

                g.xi = here("xi", [P, NT], I32)
                g.cw = here("cw", [P, NT, NB])
                g.mg = here("mg", [XROWS, D])
                g.vb = here("vb", [P, NB * NB])
                g.kr = here("kr", [XROWS, H * PART])
                g.xtok = here("xtok", [P, NT, XROWS])
                g.akz = here("akz", [P, 4, T], BF16)
                g.va = here("va", [P, KT, 4, PART])
                phase(weights_phase, nc, g, ins)
                phase(tokens_phase, nc, g)
                phase(row_maxima_phase, nc, g)
                phase(attention_phase, nc, g)
            phase(residual_phase, nc, g)
        g.w13_p, g.w2_p = held("w13_p", [P, 2, 2, E, 2 * FF], BF16), held("w2_p", [P, 2, 4, E, D], BF16)
        phase(routing_phase, nc, g, ins["router"], ins["w13"], ins["w2"])
        phase(experts_phase, nc, g)
        phase(output_phase, nc, g, out)


def kernel(**inputs):
    import numpy as np
    import concourse.bacc as bacc
    from concourse import mybir as mb
    from concourse.bass_utils import run_bass_kernel_spmd as run

    given = {k: np.asarray(v) for k, v in inputs.items()}
    bv, bo = given["L0_attn_bv"], given["L0_attn_bo"]
    arrays = {
        "x_t": np.ascontiguousarray(given["x"].reshape(NT, P).T),
        "coeff": np.ascontiguousarray(given["L0_tok_coeff_weight"]),
        "bases": np.ascontiguousarray(given["L0_tok_base_embed_weight"]),
        "lbias": np.ascontiguousarray(given["L0_tok_lang_bias"]),
        "wvT": np.ascontiguousarray(given["L0_attn_Wv"].T),
        "bv_row": np.ascontiguousarray(bv.reshape(1, D)),
        "bv_col": np.ascontiguousarray(bv.reshape(2, P).T),
        "woT": np.ascontiguousarray(given["L0_attn_Wo"].T),
        "bo": np.ascontiguousarray(bo.reshape(1, D)),
        "router": np.ascontiguousarray(given["L0_ffn_moe_router"]),
        "w13": np.ascontiguousarray(given["L0_ffn_moe_w13"]),
        "w2": np.ascontiguousarray(given["L0_ffn_moe_w2"]),
    }
    nc = bacc.Bacc("TRN2", target_bir_lowering=False, num_devices=1)
    ins = {name: nc.dram_tensor(name, a.shape, mb.dt.from_np(a.dtype), kind="ExternalInput").ap()
           for name, a in arrays.items()}
    out = nc.dram_tensor("out", (NBATCH, S, D), F32, kind="ExternalOutput").ap()
    tower(nc, ins, out)
    r = run(nc, [arrays], core_ids=[0])
    return r.results[0]["out"]
```

```python
from contextlib import ExitStack

import concourse.bass as bass
from concourse import mybir

F32 = mybir.dt.float32
BF16 = mybir.dt.bfloat16
F16 = mybir.dt.float16
I32 = mybir.dt.int32
U32 = mybir.dt.uint32
ALU = mybir.AluOpType
ACT = mybir.ActivationFunctionType
X = mybir.AxisListType.X
ds = bass.ds

P = 128
NBATCH, S, D = 4, 1024, 256
T = NBATCH * S
NT = T // P
KT = S // P
H = 16
DK = D // H
NB = 4
NA = NB + 1
E, FF = 8, 512
PART = 32
NSPLIT = 6
HG = H // 4
XR0 = 64
XC0 = XR0 + NA
XROWS = XC0 + NB
NJ = D // DK
NR = S // NJ
ETILES = 2 * T // P + E
ECOLS = ETILES + 2
USUAL = ETILES - 4
SAFE = 40.0
PAIRS_EARLY = 5
FREE = 2
UN = 4 * KT
EPS = 1e-5


class Parts:
    pass


class Chain:

    def __init__(self, eng, sem):
        self.eng, self.sem, self.n = eng, sem, 0

    def __call__(self, instruction):
        self.n += 1
        instruction.then_inc(self.sem, 1)
        self.eng.wait_ge(self.sem, self.n)


def newton(dve, link, out, var, t1):
    link(dve.tensor_tensor(t1, out, out, ALU.mult))
    link(dve.tensor_tensor(t1, t1, var, ALU.mult))
    link(dve.tensor_scalar(t1, t1, -0.5, 1.5, ALU.mult, ALU.add))
    link(dve.tensor_tensor(out, out, t1, ALU.mult))


def weights_phase(nc, g, ins, sem, tmp):
    PS = g.PS
    base_s, lb_s, cst_s = tmp("base_s", [NB, D]), tmp("lb_s", [NB, D]), tmp("cst_s", [NB, D])
    bt, bc, msum = tmp("bt", [NB, D]), tmp("bc", [NB, D]), tmp("msum", [NB, 2])
    wvT_s = tmp("wvT_s", [P, 2, D])
    bcT, bcT_wide = tmp("bcT", [P, 2, NB]), tmp("bcT_wide", [P, 2, NB, P])
    m5T, bv_s = tmp("m5T", [P, 2, NA]), tmp("bv_s", [P, 2])
    rep, kmov = tmp("rep", [P, 2, PART]), tmp("kmov", [P, 2, H, PART])
    m5_rows = tmp("m5_rows", [P, 2, PART])
    k1, k2, kres = (tmp("k1", [PART, H * PART], BF16), tmp("k2", [PART, H * PART], BF16), tmp("kres", [PART, H * PART]))
    j_mask = tmp("j_mask", [P, 2, NJ])
    head_mask, mmask = tmp("head_mask", [P, 2, H]), tmp("mmask", [P, 2, H, NA])
    mod_i, mod_sel = tmp("mod_i", [P, P], I32), tmp("mod_sel", [P, P])
    m_rep, m_blk, bias_wide = tmp("m_rep", [P, H, NA]), g.m_blk, g.bias_wide

    pool_step, const_ready, const_dve = sem("pool_step"), sem("const_ready"), sem("const_dve")
    small_in, wv_in, wo_in, ex_in = sem("small_in"), sem("wv_in"), sem("wo_in"), sem("ex_in")
    dve_step, pe_step = sem("w_dve_step"), sem("w_pe_step")
    gathered, x_in = g.gathered, g.x_in

    BC, BCT, M5T, KMOV, MMASK, MREP = range(1, 7)
    paired, pairs_copied = sem("w_paired"), sem("w_pairs_copied")
    dve_out = sem("w_dve_out")

    with nc.Block() as block:
        @block.sync
        def _(sp):
            sp.dma_start(g.xi[:], ins["x_t"]).then_inc(x_in, 16)
            sp.dma_start(base_s[:], ins["bases"]).then_inc(small_in, 16)
            sp.dma_start(lb_s[:], ins["lbias"]).then_inc(small_in, 16)
            for n in range(NB):
                sp.dma_start(cst_s[n:n + 1, :], ins["lbias"][2:3, :]).then_inc(small_in, 16)
            sp.dma_start(bv_s[:], ins["bv_col"]).then_inc(small_in, 16)
            sp.dma_start(wvT_s[:], ins["wvT"].rearrange("(c p) e -> p c e", p=P)).then_inc(wv_in, 16)
            sp.dma_start(g.woT_s[:], ins["woT"].rearrange("(c p) e -> p c e", p=P)).then_inc(wo_in, 16)
            sp.wait_ge(const_ready, 1)
            sp.dma_start(g.resid[XC0 - 1:XC0, :], ins["bo"]).then_inc(ex_in, 16)
            sp.wait_ge(dve_out, BC)
            sp.dma_start(g.resid[XC0:XROWS, :], bt[:]).then_inc(ex_in, 16)
            sp.wait_ge(ex_in, 32)

        @block.gpsimd
        def _(pool):
            step = Chain(pool, pool_step)
            pool.wait_ge(x_in, 16)
            for t in range(NT):
                pool.indirect_dma_start(g.cw[:, t, :], None, ins["coeff"],
                                        bass.IndirectOffsetOnAxis(g.xi[:, t:t + 1].bitcast(U32), 0)).then_inc(gathered, 16)
                if t == 0:
                    step(pool.memset(g.ident[:], 0.0))
                    step(pool.affine_select(g.ident[:], g.ident[:], [[-1, P]], ALU.not_equal, 1.0, 0, 1))
                    step(pool.tensor_copy(g.identb[:], g.ident[:]))
                    step(pool.tensor_copy(g.identh[:], g.ident[:]))
                    step(pool.memset(head_mask[:], 1.0))
                    step(pool.affine_select(head_mask[:], head_mask[:], [[P, 2], [-DK, H]], ALU.is_ge, 0.0, 0, 1))
                    step(pool.affine_select(head_mask[:], head_mask[:], [[-P, 2], [DK, H]], ALU.is_ge, 0.0, DK - 1, -1))
                    step(pool.iota(mod_i[:], [[1, P]], P, -1))
                    step(pool.memset(g.resid[:], 0.0))
                    step(pool.memset(g.kr[:], 0.0))
                    ones_at = g.kr[0:H].rearrange("p (h r) -> p h r", h=H)[:, :, 0:NSPLIT * NA]
                    ones_at = ones_at.rearrange("p h (s n) -> p h s n", n=NA)[:, :, :, NB]
                    step(pool.affine_select(ones_at, ones_at, [[-1, H], [0, NSPLIT]], ALU.not_equal, 1.0, 0, 1))
                    pool.iota(g.iota_p[:], [[0, 1]], 0, 1).then_inc(const_ready, 1)
            pool.wait_ge(gathered, 16 * NT)

        @block.vector
        def _(dve):
            link = Chain(dve, dve_step)

            def give(instruction):
                instruction.then_inc(dve_out, 1)

            dve.memset(g.akz[:], 0.0)
            dve.memset(g.krb[:], 0.0)
            dve.memset(g.xtok[:, :, 0:XR0], 0.0)
            dve.wait_ge(small_in, 16 * 7)
            link(dve.tensor_tensor(base_s[:], base_s[:], lb_s[:], ALU.add))
            link(dve.tensor_scalar(cst_s[:], cst_s[:], 0.1, None, ALU.mult))
            link(dve.scalar_tensor_tensor(bt[:], base_s[:], float(D) ** 0.5, cst_s[:], ALU.mult, ALU.add))
            link(dve.reduce_sum(msum[:, 0:1], bt[:], X))
            link(dve.tensor_scalar(msum[:, 1:2], msum[:, 0:1], -1.0 / D, None, ALU.mult))
            give(dve.tensor_scalar(bc[:], bt[:], msum[:, 1:2], None, ALU.add))
            dve.wait_ge(pe_step, 1)
            give(dve.tensor_copy(bcT[:], PS[:, 0, 0:2 * NB].rearrange("p (c n) -> p c n", c=2)))
            dve.wait_ge(dve_out, BCT)
            link(dve.tensor_copy(bcT_wide[:], bcT[:].unsqueeze(3).to_broadcast([P, 2, NB, P])))
            dve.wait_ge(pe_step, 2)
            dve.tensor_copy(m5T[:, :, NB:NA], bv_s[:].unsqueeze(2))
            give(dve.tensor_copy(m5T[:, :, 0:NB], PS[:, 1, 0:2 * NB].rearrange("p (c n) -> p c n", c=2)))
            dve.wait_ge(dve_out, M5T)
            link(dve.memset(rep[:], 0.0))
            link(dve.tensor_scalar(rep[:, :, 0:NSPLIT * NA].rearrange("p c (s n) -> p c s n", n=NA),
                                   m5T[:].unsqueeze(2).to_broadcast([P, 2, NSPLIT, NA]), 1.0 / DK ** 0.5, None, ALU.mult))
            link(dve.memset(m5_rows[:], 0.0))
            dve.tensor_copy(m5_rows[:, :, 0:NSPLIT * NA].rearrange("p c (s n) -> p c s n", n=NA),
                            m5T[:].unsqueeze(2).to_broadcast([P, 2, NSPLIT, NA]))
            dve.wait_ge(const_ready, 1)
            for c in range(2):
                last = dve.tensor_tensor(kmov[:, c], rep[:, c].unsqueeze(1).to_broadcast([P, H, PART]),
                                         head_mask[:, c].unsqueeze(2).to_broadcast([P, H, PART]), ALU.mult)
            give(last)
            for c in range(2):
                last = dve.tensor_tensor(mmask[:, c], m5T[:, c].unsqueeze(1).to_broadcast([P, H, NA]),
                                         head_mask[:, c].unsqueeze(2).to_broadcast([P, H, NA]), ALU.mult)
            link(dve.tensor_scalar(mod_i[:], mod_i[:], DK - 1, None, ALU.bitwise_and))
            give(dve.tensor_scalar(mod_sel[:], mod_i[:], 0.0, None, ALU.is_equal))
            link(dve.tensor_scalar(g.iota_p[:], g.iota_p[:], PART - 1, None, ALU.bitwise_and))
            link(dve.tensor_copy(g.part_r[:], g.iota_p[:]))
            for col, first in ((0, 3 * NA), (1, 5 * NA)):
                dve.tensor_scalar(g.part_c[:, col:col + 1], g.part_r[:], float(first), -1.0, ALU.is_ge, ALU.mult)
            dve.wait_ge(pe_step, 3)
            dve.tensor_scalar(g.vb[:], PS[:, 3, 0:NB * NB], 1.0 / D, None, ALU.mult)
            dve.wait_ge(pe_step, 4)
            dve.tensor_copy(g.kr[XR0:XC0, :], PS[XR0:XC0, 4, :])
            k_rows = PS[0:PART, 6, :]
            link(dve.tensor_copy(k1[:], k_rows))
            link(dve.scalar_tensor_tensor(kres[:], k1[:], g.part_c[0:PART, 0:1], k_rows, ALU.mult, ALU.add))
            link(dve.tensor_copy(k2[:], kres[:]))
            link(dve.scalar_tensor_tensor(g.krb[0:PART, :], k2[:], g.part_c[0:PART, 1:2], kres[:], ALU.mult, ALU.add))
            dve.wait_ge(pe_step, 5)
            link(dve.tensor_copy(m_rep[:].rearrange("p h n -> p (h n)"), PS[:, 5, 0:H * NA]))
            for c in range(2):
                last = dve.tensor_copy(j_mask[:, c].rearrange("p (q j) -> p q j", q=2),
                                       head_mask[:, c].rearrange("p (j q) -> p q j", q=2))
            link(last)
            for c in range(2):
                dve.tensor_tensor(m_blk[:, c], m_rep[:, :, 0:NB].unsqueeze(2).to_broadcast([P, H, NJ, NB]),
                                  j_mask[:, c].unsqueeze(1).unsqueeze(3).to_broadcast([P, H, NJ, NB]), ALU.mult)
            give(dve.tensor_copy(bias_wide[:], m_rep[:, :, NB:NA].to_broadcast([P, H, NR])))

        @block.tensor
        def _(pe):
            pe.wait_ge(const_ready, 1)
            pe.wait_ge(dve_out, BC)
            for c in range(2):
                last = pe.transpose(PS[:, 0, NB * c:NB * c + NB], bc[:, P * c:P * c + P], g.ident[0:NB, 0:NB])
            last.then_inc(pe_step, 1)
            pe.wait_ge(dve_out, BCT)
            pe.wait_ge(wv_in, 16)
            for c in range(2):
                for k in range(2):
                    last = pe.matmul(PS[:, 1, NB * c:NB * c + NB], wvT_s[:, k, P * c:P * c + P], bcT[:, k, :],
                                     start=k == 0, stop=k == 1)
            last.then_inc(pe_step, 1)
            pe.wait_ge(dve_step, 6)
            for m in range(NB):
                for k in range(2):
                    last = pe.matmul(PS[:, 3, NB * m:NB * m + NB], bcT_wide[:, k, m, :], bcT[:, k, :],
                                     start=k == 0, stop=k == 1)
            last.then_inc(pe_step, 1)
            pe.wait_ge(dve_out, KMOV)
            for k in range(2):
                pe.matmul(PS[XR0:XC0, 4, :], m5T[:, k, :], kmov[:, k].rearrange("p h r -> p (h r)"),
                          start=k == 0, stop=k == 1)
            for k in range(2):
                last = pe.matmul(PS[0:PART, 6, :], m5_rows[:, k, :], kmov[:, k].rearrange("p h r -> p (h r)"),
                                 start=k == 0, stop=k == 1)
            last.then_inc(pe_step, 1)
            pe.wait_ge(dve_out, MMASK)
            for k in range(2):
                last = pe.matmul(PS[:, 5, 0:H * NA], mod_sel[:], mmask[:, k].rearrange("p h n -> p (h n)"),
                                 start=k == 0, stop=k == 1)
            last.then_inc(pe_step, 1)
            pe.wait_ge(dve_out, MREP)
            pe.wait_ge(wo_in, 16)
            pair_products(pe, g, range(0, PAIRS_EARLY), 0, paired)

        @block.scalar
        def _(act):
            copy_pairs(act, g, range(0, PAIRS_EARLY), 0, paired, pairs_copied)


def pair_products(pe, g, ks, bank, paired):
    for i, k in enumerate(ks):
        for c in range(2):
            pe.matmul(g.PS[:, bank + i, 0:D], g.m_blk[:, c, 2 * k:2 * k + 2].rearrange("p h j n -> p (h j n)"),
                      g.woT_s[:, c, :], start=c == 0, stop=c == 1)
        for c in range(2):
            last = pe.matmul(g.PS[:, bank + i, D:2 * D], g.bias_wide[:, 2 * k:2 * k + 2].rearrange("p h r -> p (h r)"),
                             g.woT_s[:, c, :], start=c == 0, stop=c == 1)
        last.then_inc(paired, 1)


def copy_pairs(act, g, ks, bank, paired, copied):
    for i, k in enumerate(ks):
        act.wait_ge(paired, i + 1)
        act.copy(g.pair[:, k, :], g.PS[:, bank + i, :]).then_inc(copied, 1)


def tokens_phase(nc, g, sem, tmp):
    PS = g.PS
    tmax, csum, quad = tmp("tmax", [P, NT]), tmp("csum", [P, NT]), tmp("quad", [P, NT, NB, NB])
    var, t1, rstd = tmp("var", [P, NT]), tmp("t1", [P, NT]), tmp("rstd", [P, NT])
    a_part, a_res = tmp("a_part", [P, 3, NT, NA], BF16), tmp("a_res", [P, 2, NT, NA])
    ak_one, ak_rep = tmp("ak_one", [P, NT, PART], BF16), tmp("ak_rep", [P, NT, 4, PART], BF16)
    u_a = g.h1[:].rearrange("p t d -> p (t d)")[:, 0:NT * H * NA].rearrange("p (t h n) -> p t h n", t=NT, h=H)
    diag, dmax = tmp("diag", [P, NT, H]), tmp("dmax", [P, H])
    gmax, gall = tmp("gmax", [H, 2]), tmp("gall", [1, 2])
    shift_p, shift_r = tmp("shift_p", [H, 3], BF16), tmp("shift_r", [H, 2])
    dve_step, dve_out, act_step, pe_step = sem("t_dve_step"), sem("t_dve_out"), sem("t_act_step"), sem("t_pe_step")
    xT_mm, xT_copied = sem("xT_mm"), [sem("xT_copied_dve"), sem("xT_copied_act")]
    ak_mm, ak_copied = sem("ak_mm"), [sem("ak_copied_dve"), sem("ak_copied_act")]
    u_mm, u_times_a, paired, pool_step = sem("t_u_mm"), sem("u_times_a"), sem("t_paired"), sem("t_pool_step")
    pairs_copied = sem("t_pairs_copied")
    UT = NT // 8
    z_c, xq_ready = g.xtok[:, :, XC0:XROWS], sem("xq_ready")
    xq_in = sem("xq_in")
    SUBMAX, VAR, XTOK, AKREP, DMAX, GMAX = range(1, 7)

    with nc.Block() as block:
        @block.sync
        def _(sp):
            sp.wait_ge(xq_ready, 1)
            for b in range(NBATCH):
                sp.wait_ge(ak_copied[0], 2 * b + 1)
                sp.dma_start(g.xq[0:32, S * b:S * b + S], g.akz[0:32, 0, S * b:S * b + S]).then_inc(xq_in, 16)
            sp.wait_ge(xq_in, 16 * NBATCH)

        @block.vector
        def _(dve):
            link = Chain(dve, dve_step)

            def give(instruction):
                instruction.then_inc(dve_out, 1)

            link(dve.tensor_reduce(tmax[:], g.cw[:], X, ALU.max))
            give(dve.tensor_tensor(g.cw[:], g.cw[:], tmax[:].unsqueeze(2).to_broadcast([P, NT, NB]), ALU.subtract))
            def own_times_a(n):
                dve.wait_ge(u_mm, n + 1)
                tiles = slice(UT * n, UT * n + UT)
                dve.tensor_tensor(u_a[:, tiles], PS[:, 4 + n % 4, 0:UT * H * NA].rearrange("p (t h n) -> p t h n", t=UT, n=NA),
                                  g.xtok[:, tiles, XR0:XC0].unsqueeze(2).to_broadcast([P, UT, H, NA]), ALU.mult).then_inc(u_times_a, 1)

            dve.wait_ge(act_step, 1)
            link(dve.reduce_sum(csum[:], g.cw[:], X))
            link(dve.reciprocal(csum[:], csum[:]))
            link(dve.tensor_tensor(z_c, g.cw[:], csum[:].unsqueeze(2).to_broadcast([P, NT, NB]), ALU.mult))
            for m in range(NB):
                last = dve.tensor_tensor(quad[:, :, m, :], z_c, z_c[:, :, m:m + 1].to_broadcast([P, NT, NB]), ALU.mult)
            link(last)
            qv = quad[:].rearrange("p t m n -> p t (m n)")
            link(dve.tensor_tensor(qv, qv, g.vb[:].unsqueeze(1).to_broadcast([P, NT, NB * NB]), ALU.mult))
            link(dve.reduce_sum(var[:], qv, X))
            give(dve.tensor_scalar(var[:], var[:], 0.0, EPS, ALU.max, ALU.add))
            dve.wait_ge(act_step, 2)
            link(dve.reciprocal(rstd[:], rstd[:]))
            newton(dve, link, rstd[:], var[:], t1[:])
            link(dve.tensor_tensor(g.xtok[:, :, XR0:XR0 + NB], z_c, rstd[:].unsqueeze(2).to_broadcast([P, NT, NB]), ALU.mult))
            give(dve.memset(g.xtok[:, :, XR0 + NB:XC0], 1.0))
            dve.wait_ge(dve_out, XTOK)
            xa = g.xtok[:, :, XR0:XC0]
            link(dve.tensor_copy(a_part[:, 0], xa))
            link(dve.tensor_tensor(a_res[:, 0], xa, a_part[:, 0], ALU.subtract))
            link(dve.tensor_copy(a_part[:, 1], a_res[:, 0]))
            link(dve.tensor_tensor(a_res[:, 1], a_res[:, 0], a_part[:, 1], ALU.subtract))
            link(dve.tensor_copy(a_part[:, 2], a_res[:, 1]))
            dve.memset(ak_one[:, :, NSPLIT * NA:PART], 0.0)
            for s, part in enumerate((0, 1, 2, 0, 1, 0)):
                last = dve.tensor_copy(ak_one[:, :, NA * s:NA * s + NA], a_part[:, part])
            link(last)
            give(dve.tensor_copy(ak_rep[:], ak_one[:].unsqueeze(2).to_broadcast([P, NT, 4, PART])))
            for n in range(0, 8, 2):
                dve.wait_ge(xT_mm, n + 1)
                dve.tensor_copy(g.xT[:, 512 * n:512 * n + 512], PS[0:XROWS, n, :]).then_inc(xT_copied[0], 1)
            for n in range(0, 16, 2):
                b, k = n // 4, n % 4
                dve.wait_ge(ak_mm, b + 1)
                dve.tensor_copy(g.akz[32 * k:32 * k + 32, k, S * b:S * b + S],
                                PS[32 * k:32 * k + 32, b, :].bitcast(BF16)).then_inc(ak_copied[0], 1)
                own_times_a(n // 2)
            dve.wait_ge(u_times_a, NT // UT)
            link(dve.reduce_sum(diag[:].rearrange("p t h -> p (t h)"), u_a.rearrange("p t h n -> p (t h) n"), X))
            give(dve.tensor_reduce(dmax[:], diag[:].rearrange("p t h -> p h t"), X, ALU.max))
            dve.wait_ge(pe_step, 1)
            link(dve.tensor_reduce(gmax[:, 0:1], PS[0:H, 0, 0:P], X, ALU.max))
            give(dve.tensor_scalar(gmax[:, 1:2], gmax[:, 0:1], -1.0, None, ALU.mult))
            dve.wait_ge(dve_out, GMAX)
            link(dve.tensor_copy(shift_p[:, 0:1], gmax[:, 1:2]))
            link(dve.tensor_tensor(shift_r[:, 0:1], gmax[:, 1:2], shift_p[:, 0:1], ALU.subtract))
            link(dve.tensor_copy(shift_p[:, 1:2], shift_r[:, 0:1]))
            link(dve.tensor_tensor(shift_r[:, 1:2], shift_r[:, 0:1], shift_p[:, 1:2], ALU.subtract))
            link(dve.tensor_copy(shift_p[:, 2:3], shift_r[:, 1:2]))
            for k in range(3):
                dve.tensor_scalar(g.krb[32 * k + 32:32 * k + 32 + H, :], g.kr[0:H, :], shift_p[:, k:k + 1], None, ALU.mult)
            dve.wait_ge(pe_step, 2)
            link(dve.tensor_reduce(gall[:, 0:1], PS[0:1, 1, 0:H], X, ALU.max))
            link(dve.tensor_scalar(gall[:, 1:2], gall[:, 0:1], SAFE, None, ALU.is_le))
            link(dve.tensor_scalar(gall[:, 0:1], gall[:, 1:2], -1.0, 1.0, ALU.mult, ALU.add))
            give(dve.tensor_copy(g.flag[:], gall[:, 0:1]))

        @block.scalar
        def _(act):
            act.wait_ge(dve_out, SUBMAX)
            act.activation(g.cw[:], g.cw[:], ACT.Exp).then_inc(act_step, 1)
            act.activation(gall[0:1, 0:1], g.ident[0:1, 0:1], ACT.Sqrt)
            act.wait_ge(dve_out, VAR)
            act.activation(rstd[:], var[:], ACT.Sqrt).then_inc(act_step, 1)
            copy_pairs(act, g, range(PAIRS_EARLY, KT), 4, paired, pairs_copied)
            for n in range(1, 8, 2):
                act.wait_ge(xT_mm, n + 1)
                act.copy(g.xT[:, 512 * n:512 * n + 512], PS[0:XROWS, n, :]).then_inc(xT_copied[1], 1)
            for n in range(1, 16, 2):
                b, k = n // 4, n % 4
                act.wait_ge(ak_mm, b + 1)
                act.copy(g.akz[32 * k:32 * k + 32, k, S * b:S * b + S],
                         PS[32 * k:32 * k + 32, b, :].bitcast(BF16)).then_inc(ak_copied[1], 1)

        @block.gpsimd
        def _(pool):
            step = Chain(pool, pool_step)
            pool.memset(g.xq[:], 1.0).then_inc(xq_ready, 1)
            step(pool.memset(g.va[:], 0.0))
            step(pool.memset(g.fold_sel[:], 0.0))
            for k in range(4):
                step(pool.affine_select(g.fold_sel[:, k % 2, :], g.fold_sel[:, k % 2, :], [[-1, 32]],
                                        ALU.not_equal, 1.0, -32 * k, 1))
            step(pool.memset(g.ones[:], 1.0))
            step(pool.affine_select(g.tri[:], g.ones[:], [[1, P]], ALU.is_gt, 0.0, 0, -1))
            step(pool.iota(g.iota_i[:], [[1, P]], 0, 0))
            step(pool.tensor_copy(g.iota_r[:], g.iota_i[:]))
            step(pool.tensor_copy(g.iota_h[:], g.iota_i[:]))
            pairs = g.iota_i[:, 0:2 * KT].rearrange("p (k t) -> p k t", k=2)
            step(pool.iota(pairs, [[1, 2], [2 * P, KT]], 1, 2))
            step(pool.tensor_copy(g.pair_no[:], pairs))

        @block.tensor
        def _(pe):
            def own_scores(n):
                if n >= 4:
                    pe.wait_ge(u_times_a, n - 3)
                else:
                    pe.wait_ge(xT_copied[n % 2], n // 2 + 3)
                for i in range(UT):
                    t = UT * n + i
                    last = pe.matmul(PS[:, 4 + n % 4, H * NA * i:H * NA * i + H * NA], g.xT[0:XC0, P * t:P * t + P],
                                     g.kr[0:XC0, :].rearrange("p (h r) -> p h r", h=H)[:, :, 0:NA], start=True, stop=True)
                last.then_inc(u_mm, 1)

            pair_products(pe, g, range(PAIRS_EARLY, KT), 4, paired)
            pe.wait_ge(dve_out, XTOK)
            for t in range(NT):
                if t == 16:
                    pe.wait_ge(pairs_copied, KT - PAIRS_EARLY)
                last = pe.transpose(PS[0:XROWS, t // 4, P * (t % 4):P * (t % 4) + P], g.xtok[:, t, :], g.ident[:])
                if t % 4 == 3:
                    last.then_inc(xT_mm, 1)
            pe.wait_ge(dve_out, AKREP)
            for b in range(NBATCH):
                pe.wait_ge(xT_copied[b % 2], b // 2 + 1)
                for t in range(KT):
                    last = pe.transpose(PS[:, b, :].bitcast(BF16)[:, P * t:P * t + P],
                                        ak_rep[:, KT * b + t].rearrange("p k r -> p (k r)"), g.identb[:])
                last.then_inc(ak_mm, 1)
            for n in range(NT // UT):
                own_scores(n)
            pe.wait_ge(dve_out, DMAX)
            pe.wait_ge(ak_copied[0], 8)
            pe.wait_ge(ak_copied[1], 8)
            pe.transpose(PS[0:H, 0, 0:P], dmax[:], g.ident[:]).then_inc(pe_step, 1)
            pe.wait_ge(dve_out, GMAX)
            pe.transpose(PS[0:1, 1, 0:H], gmax[:, 0:1], g.ident[0:H, 0:H]).then_inc(pe_step, 1)


def row_maxima_phase(nc, g, sem, tmp):
    PS = g.PS
    xTr, xtile = tmp("xTr", [P, T]), tmp("xtile", [XROWS, 2, P])
    part, rest = tmp("rm_part", [H, 2, 512], BF16), tmp("rm_rest", [H, 2, 512])
    u_s, rmax = tmp("u_s", [P, HG, 4, P]), tmp("rmax", [P, NT, H])
    zeroed, replicated, u_mm, u_copied = sem("rm_zeroed"), sem("rm_replicated"), sem("rm_u_mm"), sem("rm_u_copied")
    tile_in, scored, maxed, negated = sem("rm_tile_in"), sem("rm_scored"), sem("rm_maxed"), sem("rm_negated")
    turned, taken = sem("rm_turned"), sem("rm_taken")

    with nc.Block() as block:
        @block.sync
        def _(sp):
            needed = sp.value_load(g.flag[0:1, 0:1], min_val=0, max_val=1)
            with sp.If(needed > 0):
                sp.wait_ge(zeroed, 2)
                for k in range(4):
                    sp.dma_start(xTr[32 * k:32 * k + NA, :], g.xT[XR0:XC0, 0:T]).then_inc(replicated, 16)
                sp.wait_ge(replicated, 64)

        @block.vector
        def _(dve):
            needed = dve.value_load(g.flag[0:1, 0:1], min_val=0, max_val=1)
            with dve.If(needed > 0):
                dve.sem_inc(u_copied, FREE)
                dve.sem_inc(maxed, FREE)
                dve.memset(xTr[:], 0.0).then_inc(zeroed, 1)
                dve.memset(u_s[:], 0.0).then_inc(zeroed, 1)
                dve.wait_ge(zeroed, 2)
                with dve.Fori(0, NBATCH) as b:
                    with dve.Fori(0, KT) as q:
                        t = b * KT + q
                        dve.wait_ge(u_mm, t + FREE)
                        dve.tensor_copy(xtile[:, 0, :], g.xT[:, ds(t * P, P)]).then_inc(tile_in, 1)
                        dve.wait_ge(u_mm, t + 1 + FREE)
                        dve.wait_ge(scored, t * H + FREE)
                        for k in range(4):
                            r = slice(32 * k, 32 * k + 32)
                            last = dve.tensor_copy(u_s[r, :, k, :], PS[r, 0, :].rearrange("p (h q) -> p h q", h=HG))
                        last.then_inc(u_copied, 1)
                        for h in range(H):
                            dve.wait_ge(scored, t * H + h + 1 + FREE)
                            m = 2 + 2 * (h % 2)
                            dve.tensor_reduce(rmax[:, ds(t, 1), h], PS[:, m:m + 2, :].rearrange("p b k -> p (b k)").unsqueeze(1), X, ALU.max).then_inc(maxed, 1)
                dve.wait_ge(maxed, NT * H + FREE)
                dve.tensor_scalar(g.xtok[:, :, 0:H], rmax[:], -1.0, None, ALU.mult).then_inc(negated, 1)
                link = Chain(dve, taken)
                for k in range(3):
                    dve.tensor_copy(g.krb[32 * k + 32:32 * k + 32 + H, :], g.kr[0:H, :])
                for n in range(8):
                    dve.wait_ge(turned, n + 1)
                    at, shift = slice(512 * n, 512 * n + 512), PS[0:H, n, :]
                    link(dve.tensor_copy(part[:, 0], shift))
                    link(dve.tensor_tensor(rest[:, 0], shift, part[:, 0], ALU.subtract))
                    link(dve.tensor_copy(part[:, 1], rest[:, 0]))
                    link(dve.tensor_tensor(rest[:, 1], rest[:, 0], part[:, 1], ALU.subtract))
                    dve.tensor_copy(g.xq[32:32 + H, at], part[:, 0])
                    dve.tensor_copy(g.xq[64:64 + H, at], part[:, 1])
                    link(dve.tensor_copy(g.xq[96:96 + H, at], rest[:, 1]))

        @block.tensor
        def _(pe):
            needed = pe.value_load(g.flag[0:1, 0:1], min_val=0, max_val=1)
            with pe.If(needed > 0):
                pe.sem_inc(u_mm, FREE)
                pe.sem_inc(scored, FREE)
                pe.wait_ge(replicated, 64)
                with pe.Fori(0, NBATCH) as b:
                    with pe.Fori(0, KT) as q:
                        t = b * KT + q
                        pe.wait_ge(tile_in, t + 1)
                        pe.wait_ge(u_copied, t + FREE)
                        for k in range(HG):
                            last = pe.matmul(PS[:, 0, P * k:P * k + P], g.kr[:, P * k:P * k + P], xtile[:, 0, :],
                                             start=True, stop=True)
                        last.then_inc(u_mm, 1)
                        pe.wait_ge(u_copied, t + 1 + FREE)
                        for h in range(H):
                            m = 2 + 2 * (h % 2)
                            pe.wait_ge(maxed, t * H + max(h - 1, 0) + FREE)
                            for c in range(2):
                                last = pe.matmul(PS[:, m + c, :], u_s[:, h // 4, h % 4, :],
                                                 xTr[:, ds(b * S + c * 512, 512)], start=True, stop=True)
                            last.then_inc(scored, 1)
                pe.wait_ge(negated, 1)
                for n in range(8):
                    for i in range(4):
                        last = pe.transpose(PS[0:H, n, P * i:P * i + P], g.xtok[:, 4 * n + i, 0:H], g.ident[:])
                    last.then_inc(turned, 1)


def attention_phase(nc, g, sem, tmp):
    PS = g.PS
    u1, u2 = tmp("u1", [P, 512], BF16), tmp("u2", [P, 512], BF16)
    ures = tmp("ures", [P, 512])
    RING = 8
    qf = tmp("qf", [P, HG, S], BF16)
    prob = g.h1[:].rearrange("p t d -> p (t d)").rearrange("p (n q) -> p n q", n=RING)
    acc_s, rden = tmp("acc_s", [P, 512]), tmp("rden", [P, 4, 8])
    u_mm, u_read, u_step = sem("u_mm"), sem("u_read"), sem("u_step")
    scores_ready, exp_done, prob_used = sem("scores_ready"), sem("exp_done"), sem("prob_used")
    acc_copied, va_ready = sem("acc_copied"), sem("va_ready")
    folded, fold_read, rden_step = sem("folded"), sem("fold_read"), sem("rden_step")
    BU = HG * UN
    GROUPS = NBATCH * HG
    ACC, UB = 6, 7

    with nc.Block() as block:
        @block.tensor
        def _(pe):
            pe.sem_inc(prob_used, RING)

            def query_product(b, hg, half, n):
                if not (isinstance(n, int) and n == 0):
                    pe.wait_ge(u_read, n)
                pe.matmul(PS[:, UB, :], g.krb[:, P * hg:P * hg + P],
                          g.xq[:, ds(b * S, S)].rearrange("p (r j) -> p j r", j=NJ)[:, 8 * half:8 * half + 8, :],
                          start=True, stop=True).then_inc(u_mm, 1)

            def scores(b, n, exps):
                hg, slot, kt, buf = n // UN, n // KT % 4, n % KT, n % 3
                if n % UN == 0:
                    pe.wait_ge(u_step, 3 * (b * (2 * HG) + 2 * hg + 2))
                if exps is not None:
                    pe.wait_ge(exp_done, exps)
                for c in range(2):
                    last = pe.matmul(PS[:, 2 * buf + c, :], g.akz[:, slot, ds(b * S + P * kt, P)],
                                     qf[:, hg, 512 * c:512 * c + 512], start=True, stop=True)
                last.then_inc(scores_ready, 1)

            def sums(b, pair):
                hg, slot = pair // (UN // 2), pair // (KT // 2) % 4
                if pair == 0:
                    pe.wait_ge(va_ready, b + 1)
                if pair % (UN // 2) == 0:
                    pe.wait_ge(acc_copied, b * HG + hg + FREE)
                pe.wait_ge(exp_done, b * BU + 2 * pair + 2 + FREE)
                for n in (2 * pair, 2 * pair + 1):
                    kt = n % KT
                    for c in range(2):
                        r = 32 * (2 * (kt % 2) + c)
                        last = pe.matmul(PS[r:r + 32, ACC, :], g.va[:, kt, slot, :], prob[:, n % RING, 512 * c:512 * c + 512],
                                         start=slot == 0 and kt < 2, stop=slot == 3 and kt >= KT - 2)
                last.then_inc(prob_used, 1)

            def fold(n, part):
                pe.wait_ge(acc_copied, n + FREE)
                pe.wait_ge(u_read, n * 2 + 4 if not isinstance(n, int) else 2 * n + 2)
                for i in (2 * part, 2 * part + 1):
                    last = pe.matmul(PS[:, UB, 64 * i:64 * i + 64], acc_s[:, P * i:P * i + P],
                                     g.fold_sel[:].rearrange("p c r -> p (c r)"), start=True, stop=True)
                if part:
                    last.then_inc(folded, 1)

            def between(b, hg, at):
                if at in (3, 8):
                    half = int(at == 8)
                    nb, nh = (b, hg + 1) if hg + 1 < HG else (b + 1, 0)
                    if half == 0:
                        pe.wait_ge(fold_read, b * HG + hg + FREE)
                    query_product(nb, nh, half, b * (2 * HG) + 2 * hg + 2 + half)
                if at in (12, 14):
                    fold(b * HG + hg, int(at == 14))

            query_product(0, 0, 0, 0)
            query_product(0, 0, 1, 1)
            scores(0, 0, None)
            scores(0, 1, None)
            with pe.Fori(0, NBATCH) as b:
                for pair in range(BU // 2):
                    for n in (2 * pair + 2, 2 * pair + 3):
                        if n == 2:
                            scores(b, n, b * BU + FREE)
                        elif n < BU:
                            scores(b, n, b * BU + n - 2 + FREE)
                        else:
                            scores(b + 1, n - BU, b * BU + n - 1 + FREE)
                        if n % 2 == 0:
                            between(b, pair // (UN // 2), pair % (UN // 2))
                    if pair:
                        sums(b, pair - 1)
                sums(b, BU // 2 - 1)
            fold(GROUPS, 0)
            fold(GROUPS, 1)

        @block.gpsimd
        def _(pool):
            pool.memset(g.z_blk[:], 0.0)

        @block.scalar
        def _(act):
            act.sem_inc(exp_done, FREE)
            with act.Fori(0, NBATCH) as b:
                for n in range(BU):
                    act.wait_ge(scores_ready, b * BU + n + 1)
                    act.wait_ge(prob_used, b * (BU // 2) + (n - RING) // 2 + 1 + RING)
                    buf = n % 3
                    act.activation(prob[:, n % RING, :], PS[:, 2 * buf:2 * buf + 2, :].rearrange("p c q -> p (c q)"),
                                   ACT.Exp).then_inc(exp_done, 1)

        @block.vector
        def _(dve):
            dve.sem_inc(fold_read, FREE)
            dve.sem_inc(acc_copied, FREE - 1)
            dve.memset(acc_s[:], 1.0).then_inc(acc_copied, 1)

            def query_features(b, hg, half, n):
                dve.wait_ge(u_mm, n + 1)
                dve.tensor_copy(u1[:], PS[:, UB, :]).then_inc(u_step, 1)
                dve.wait_ge(u_step, 3 * n + 1)
                dve.scalar_tensor_tensor(ures[:], u1[:], g.part_c[:, 0:1], PS[:, UB, :], ALU.mult, ALU.add).then_inc(u_read, 1)
                dve.wait_ge(u_read, n + 1)
                dve.tensor_copy(u2[:], ures[:]).then_inc(u_step, 1)
                dve.wait_ge(u_step, 3 * n + 2)
                dve.scalar_tensor_tensor(qf[:, hg, 512 * half:512 * half + 512], u2[:], g.part_c[:, 1:2], ures[:],
                                         ALU.mult, ALU.add).then_inc(u_step, 1)
                dve.wait_ge(u_step, 3 * n + 3)

            def fold_out(zb, heads, n):
                dve.wait_ge(folded, n + 1)
                sums = PS[:, UB, 0:256].rearrange("p (i s r) -> p i s r", i=4, s=8)
                dve.reciprocal(rden[:], sums[:, :, :, NB]).then_inc(rden_step, 1)
                dve.wait_ge(rden_step, n + 1)
                for c in range(2):
                    sums = PS[:, UB, 0:256].rearrange("p (i c s r) -> p c s i r", i=4, c=2, s=4)
                    out = g.z[:, ds(zb, 1) if not isinstance(zb, int) else slice(zb, zb + 1), heads:heads + 4, 4 * c:4 * c + 4, :]
                    last = dve.tensor_tensor(out.rearrange("p b s i n -> p (b s) i n"), sums[:, c, :, :, 0:NB],
                                             rden[:].rearrange("p i (c s) -> p c s i", c=2)[:, c].unsqueeze(3).to_broadcast([P, 4, 4, NB]),
                                             ALU.mult)
                last.then_inc(fold_read, 1)

            query_features(0, 0, 0, 0)
            query_features(0, 0, 1, 1)
            with dve.Fori(0, NBATCH) as b:
                for slot in range(4):
                    last = dve.tensor_copy(g.va[:, :, slot, 8 * slot:8 * slot + NA], g.xtok[:, ds(b * KT, KT), XR0:XC0])
                last.then_inc(va_ready, 1)
                for hg in range(HG):
                    for half in range(2):
                        nb, nh = (b, hg + 1) if hg + 1 < HG else (b + 1, 0)
                        query_features(nb, nh, half, b * (2 * HG) + 2 * hg + 2 + half)
                    fold_out(b + 1 if hg else b, 4 * (hg - 1) if hg else H - 4, b * HG + hg)
                    dve.wait_ge(prob_used, b * (BU // 2) + (hg + 1) * (UN // 2) + RING)
                    dve.tensor_copy(acc_s[:], PS[:, ACC, :]).then_inc(acc_copied, 1)
            fold_out(NBATCH, H - 4, GROUPS)
            dve.wait_ge(fold_read, GROUPS + 1 + FREE)


def residual_phase(nc, g, sem, tmp):
    PS = g.PS
    stats, mean_d = tmp("stats", [P, NT, 6]), tmp("mean_d", [P, NT])
    zT_mm, zT_copied = sem("zT_mm"), [sem("zT_copied_act"), sem("zT_copied_dve")]

    def copy_blocks(copy, eng, i):
        for b in range(NBATCH):
            eng.wait_ge(zT_mm, b + 1)
            for jp in range(2):
                r = NR * i + 32 * jp
                src = PS[32 * i:32 * i + 32, 2 * (b % 2):2 * (b % 2) + 2, :].rearrange("p c (k q r) -> p (c k) q r", k=4, q=2)
                last = copy(g.z_blk[r:r + 32, KT * b:KT * b + KT, NR * i:NR * i + NR], src[:, :, jp, :])
            last.then_inc(zT_copied[i], 1)

    h_mm, h_copied, h_stats, dve_step = sem("h_mm"), sem("h_copied"), sem("h_stats"), sem("h_dve_step")

    with nc.Block() as block:
        @block.tensor
        def _(pe):
            for t in range(NT):
                b, k = t // KT, t % KT
                if b >= 2 and k == 0:
                    pe.wait_ge(zT_copied[0], b - 1)
                    pe.wait_ge(zT_copied[1], b - 1)
                last = pe.transpose(PS[0:NR, 2 * (b % 2) + k // 4, P * (k % 4):P * (k % 4) + P],
                                    g.z[:, b + 1, 2 * k:2 * k + 2].rearrange("p h j n -> p (h j n)"), g.ident[:])
                if k == KT - 1:
                    last.then_inc(zT_mm, 1)
            for t in range(NT):
                k, bank = t % KT, 4 + t % 4
                pe.wait_ge(zT_copied[0], t // KT + 1)
                pe.wait_ge(zT_copied[1], t // KT + 1)
                if t >= 4:
                    pe.wait_ge(h_copied, t - 3)
                pe.matmul(PS[:, bank, 0:D], g.xT[:, P * t:P * t + P], g.resid[:], start=True, stop=False)
                pe.matmul(PS[:, bank, 0:D], g.z_blk[:, t, :], g.pair[:, k, 0:D], start=False, stop=True).then_inc(h_mm, 1)

        @block.scalar
        def _(act):
            copy_blocks(act.copy, act, 0)

        @block.vector
        def _(dve):
            link = Chain(dve, dve_step)
            copy_blocks(dve.tensor_copy, dve, 1)
            for t in range(NT):
                dve.wait_ge(h_mm, t + 1)
                dve.tensor_tensor(g.h1[:, t, :], PS[:, 4 + t % 4, 0:D], g.pair[:, t % KT, D:2 * D], ALU.add).then_inc(h_copied, 1)
                if t >= 1:
                    dve.wait_ge(h_copied, t)
                    dve.bn_stats(stats[:, t - 1, :], g.h1[:, t - 1, :]).then_inc(h_stats, 1)
            dve.wait_ge(h_copied, NT)
            dve.bn_stats(stats[:, NT - 1, :], g.h1[:, NT - 1, :]).then_inc(h_stats, 1)
            dve.wait_ge(h_stats, NT)
            dve.tensor_tensor(g.mean[:], stats[:, :, 1], stats[:, :, 4], ALU.add)
            dve.tensor_tensor(g.var[:], stats[:, :, 2], stats[:, :, 5], ALU.add)
            link(dve.tensor_tensor(mean_d[:], stats[:, :, 1], stats[:, :, 4], ALU.subtract))
            dve.tensor_scalar(g.mean[:], g.mean[:], -0.5, None, ALU.mult)
            dve.tensor_scalar(g.var[:], g.var[:], 1.0 / D, None, ALU.mult)
            link(dve.tensor_tensor(mean_d[:], mean_d[:], mean_d[:], ALU.mult))
            link(dve.tensor_scalar(mean_d[:], mean_d[:], 0.25, EPS, ALU.mult, ALU.add))
            dve.tensor_tensor(g.var[:], g.var[:], mean_d[:], ALU.add)


def routing_phase(nc, g, router, w13, w2, sem, tmp):
    PS = g.PS
    XB, WB = 4, 4
    xn, x_parts, xnT = tmp("xn", [P, XB, D]), tmp("x_parts", [P, 2, XB, 2, D], F16), tmp("xnT", [P, 2, 2, P])
    w_raw = tmp("w_raw", [P, WB, 2 * FF])
    t1, rstd, rt_s = tmp("t1_2", [P, NT]), tmp("rstd2", [P, NT]), tmp("rt_s", [P, 2, E])
    logits, top, top_i = tmp("logits", [P, NT, E]), tmp("top", [P, NT, 8]), tmp("top_i", [P, NT, 8], U32)
    top_f = tmp("top_f", [P, 2, NT])
    picked, count = tmp("picked", [P, 2, NT, E]), [tmp("count0", [P, E, NT]), tmp("count1", [P, E, NT])]
    chosen, place, prod = tmp("chosen", [P, E, NT]), tmp("place", [P, E, NT]), tmp("prod", [P, 2, NT, E])
    tiles_i, tiles = tmp("tiles_i", [P, E], I32), tmp("tiles", [P, E])
    first, shift = [tmp(f"first{i}", [P, E]) for i in range(4)], tmp("shift", [P, E])
    pos, pos_i, pos_r, pos_j = (tmp("pos", [P, 2, NT]), tmp("pos_i", [P, 2, 2, NT], I32), tmp("pos_r", [P, 2, NT]),
                                tmp("pos_j", [P, 2, NT]))
    HB = 8
    hot_r, hot_j = tmp("hot_r", [P, HB, P], F16), tmp("hot_j", [P, HB, ECOLS], F16)
    idx_f, filled, te_f = tmp("idx_f", [P, 2, ECOLS]), tmp("filled", [P, NBATCH, ECOLS]), tmp("te_f", [P, 2, ECOLS])
    xn_ready, hi_ready, lo_ready = sem("xn_ready"), sem("hi_ready"), sem("lo_ready")
    xn_turned, xnT_copied, l_mm, rt_in = sem("xn_turned"), sem("xnT_copied"), sem("l_mm"), sem("rt_in")
    w_in, w_hi, w_lo = [sem(f"w_in{k}") for k in range(WB)], sem("w_hi"), sem("w_lo")
    x_stored = [sem("x_stored0"), sem("x_stored1")]
    dve_step, dve_out, act_step, pe_step = sem("r_dve_step"), sem("r_dve_out"), sem("r_act_step"), sem("r_pe_step")
    hot_ready, hot_used = sem("hot_ready"), sem("hot_used")
    TOPDIFF, ROWTOT = range(1, 3)

    pieces = []
    for e in range(E):
        for c in range(2):
            pieces.append((w13[e, P * c:P * c + P, :], g.w13_p[:, 0, c, e, :], g.w13_p[:, 1, c, e, :], None))
        pieces.append((w2[e].rearrange("(c p) d -> p c d", p=P), g.w2_p[:, 0, :, e, :], g.w2_p[:, 1, :, e, :], 4))

    def raw(n):
        piece = w_raw[:, n % WB, :]
        return piece.rearrange("p (c d) -> p c d", c=4) if pieces[n][3] else piece

    with nc.Block() as block:
        @block.sync
        def _(sp):
            sp.dma_start(rt_s[:], router.rearrange("(c p) e -> p c e", p=P)).then_inc(rt_in, 16)
            loaded = 0
            for q in range(NT // XB + 1):
                last = min(len(pieces), WB + (XB * q) // 3 if q < NT // XB else len(pieces))
                for n in range(loaded, last):
                    if n >= WB:
                        sp.wait_ge(w_lo, n - WB + 1)
                    sp.dma_start(raw(n), pieces[n][0]).then_inc(w_in[n % WB], 16)
                loaded = last
                if q < NT // XB:
                    sp.wait_ge(hi_ready, XB * q + XB)
                    sp.wait_ge(lo_ready, XB * q + XB)
                    sp.dma_start(g.xrows.rearrange("(t p) d -> p t d", p=P)[:, XB * q:XB * q + XB],
                                 x_parts[:, q % 2].rearrange("p t c d -> p t (c d)")).then_inc(x_stored[q % 2], 16)
            for k in range(2):
                sp.wait_ge(x_stored[k], 16 * (NT // XB // 2))

        @block.gpsimd
        def _(pool):
            for n in range(len(pieces)):
                pool.wait_ge(w_hi, n + 1)
                pool.tensor_tensor(pieces[n][2], raw(n), pieces[n][1], ALU.subtract).then_inc(w_lo, 1)

        @block.scalar
        def _(act):
            def weights(n):
                act.wait_ge(w_in[n % WB], 16 * (n // WB + 1))
                act.copy(pieces[n][1], raw(n)).then_inc(w_hi, 1)

            def turned_copy(t):
                act.wait_ge(xn_turned, t + 1)
                if t >= 2:
                    act.wait_ge(l_mm, t - 1)
                act.copy(xnT[:, t % 2].rearrange("p c q -> p (c q)"), PS[:, t % 2, 0:2 * P]).then_inc(xnT_copied, 1)

            act.activation(rstd[:], g.var[:], ACT.Sqrt).then_inc(act_step, 1)
            for t in range(NT):
                act.wait_ge(xn_ready, t + 1)
                q = t // XB
                if t % XB == 0 and q >= 2:
                    act.wait_ge(x_stored[q % 2], 16 * (q // 2))
                act.copy(x_parts[:, q % 2, t % XB, 0, :], xn[:, t % XB, :]).then_inc(hi_ready, 1)
                if t >= 1:
                    turned_copy(t - 1)
                if t % 3 == 2:
                    weights(t // 3)
            turned_copy(NT - 1)
            act.wait_ge(dve_out, TOPDIFF)
            act.activation(g.wgt[:, 1, :], g.wgt[:, 0, :], ACT.Exp).then_inc(act_step, 1)
            for n in range(NT // 3, len(pieces)):
                weights(n)

        @block.tensor
        def _(pe):
            def logit(t):
                pe.wait_ge(xnT_copied, t + 1)
                for c in range(2):
                    last = pe.matmul(PS[:, 3, E * t:E * t + E], xnT[:, t % 2, c, :], rt_s[:, c, :], start=c == 0, stop=c == 1)
                last.then_inc(l_mm, 1)

            pe.wait_ge(rt_in, 16)
            for t in range(NT):
                pe.wait_ge(xn_ready, t + 1)
                if t >= 2:
                    pe.wait_ge(xnT_copied, t - 1)
                for c in range(2):
                    last = pe.transpose(PS[:, t % 2, P * c:P * c + P], xn[:, t % XB, P * c:P * c + P], g.ident[:])
                last.then_inc(xn_turned, 1)
                if t >= 1:
                    logit(t - 1)
            logit(NT - 1)
            pe.wait_ge(dve_out, ROWTOT)
            pe.matmul(PS[:, 0, 0:E], g.tri[:], tiles[:], start=True, stop=True)
            pe.matmul(PS[:, 1, 0:E], g.ones[:], tiles[:], start=True, stop=True).then_inc(pe_step, 1)
            for n in range(2 * NT):
                pe.wait_ge(hot_ready, n + 1)
                b = n // (2 * KT)
                pe.matmul(PS[:, 2, ECOLS * b:ECOLS * b + ECOLS], hot_r[:, n % HB, :], hot_j[:, n % HB, :],
                          start=n % (2 * KT) == 0, stop=n % (2 * KT) == 2 * KT - 1).then_inc(hot_used, 1)

        @block.vector
        def _(dve):
            link = Chain(dve, dve_step)

            def give(instruction):
                instruction.then_inc(dve_out, 1)

            def low_part(t):
                dve.wait_ge(hi_ready, t + 1)
                parts = x_parts[:, t // XB % 2, t % XB]
                dve.tensor_tensor(parts[:, 1, :], xn[:, t % XB, :], parts[:, 0, :], ALU.subtract).then_inc(lo_ready, 1)

            dve.wait_ge(act_step, 1)
            link(dve.reciprocal(rstd[:], rstd[:]))
            newton(dve, link, rstd[:], g.var[:], t1[:])
            link(dve.tensor_tensor(g.mean[:], g.mean[:], rstd[:], ALU.mult))
            for t in range(NT):
                if t >= XB:
                    dve.wait_ge(xn_turned, t - XB + 1)
                    dve.wait_ge(lo_ready, t - XB + 1)
                dve.tensor_scalar(xn[:, t % XB, :], g.h1[:, t, :], rstd[:, t:t + 1], g.mean[:, t:t + 1],
                                  ALU.mult, ALU.add).then_inc(xn_ready, 1)
                if t >= 2:
                    low_part(t - 2)
            low_part(NT - 2)
            low_part(NT - 1)
            dve.wait_ge(l_mm, NT)
            link(dve.tensor_copy(logits[:].rearrange("p t e -> p (t e)"), PS[:, 3, 0:NT * E]))
            for t in range(NT):
                last = dve.max(top[:, t, :], logits[:, t, :])
            link(last)
            give(dve.tensor_tensor(g.wgt[:, 0, :], top[:, :, 1], top[:, :, 0], ALU.subtract))
            for t in range(NT):
                last = dve.max_index(top_i[:, t, :], top[:, t, :], logits[:, t, :])
            link(last)
            link(dve.tensor_copy(top_f[:], top_i[:, :, 0:2].rearrange("p t k -> p k t")))
            for k in range(2):
                last = dve.tensor_tensor(picked[:, k], g.iota_e.unsqueeze(1).to_broadcast([P, NT, E]),
                                         top_f[:, k].unsqueeze(2).to_broadcast([P, NT, E]), ALU.is_equal)
            link(last)
            link(dve.tensor_tensor(chosen[:], picked[:, 0].rearrange("p t e -> p e t"),
                                   picked[:, 1].rearrange("p t e -> p e t"), ALU.add))
            src, step = chosen, 1
            while step < NT:
                dst = count[(step.bit_length() - 1) % 2]
                dve.tensor_copy(dst[:, :, 0:step], src[:, :, 0:step])
                link(dve.tensor_tensor(dst[:, :, step:], src[:, :, step:], src[:, :, 0:NT - step], ALU.add))
                src, step = dst, 2 * step
            give(dve.tensor_copy(tiles[:], src[:, :, NT - 1]))
            dve.tensor_tensor(place[:], src[:], chosen[:], ALU.subtract)
            dve.wait_ge(act_step, 2)
            link(dve.tensor_scalar(g.wgt[:, 0, :], g.wgt[:, 1, :], 1.0, None, ALU.add))
            link(dve.reciprocal(g.wgt[:, 0, :], g.wgt[:, 0, :]))
            dve.tensor_tensor(g.wgt[:, 1, :], g.wgt[:, 1, :], g.wgt[:, 0, :], ALU.mult)
            dve.wait_ge(pe_step, 1)
            link(dve.tensor_scalar(shift[:], PS[:, 1, 0:E], float(P - 1), None, ALU.add))
            link(dve.tensor_copy(tiles_i[:], shift[:]))
            link(dve.tensor_scalar(tiles_i[:], tiles_i[:], 7, None, ALU.logical_shift_right))
            link(dve.tensor_copy(tiles[:], tiles_i[:]))
            src = tiles
            for i, step in enumerate((1, 2, 4)):
                dve.tensor_copy(first[i][:, 0:step], src[:, 0:step])
                link(dve.tensor_tensor(first[i][:, step:], src[:, step:], src[:, 0:E - step], ALU.add))
                src = first[i]
            link(dve.tensor_tensor(first[3][:], src[:], tiles[:], ALU.subtract))
            link(dve.scalar_tensor_tensor(shift[:], first[3][:], float(P), PS[:, 0, 0:E], ALU.mult, ALU.add))
            link(dve.tensor_tensor(place[:], place[:], shift[:].unsqueeze(2).to_broadcast([P, E, NT]), ALU.add))
            for k in range(2):
                last = dve.tensor_tensor(prod[:, k], picked[:, k], place[:].rearrange("p e t -> p t e"), ALU.mult)
            link(last)
            link(dve.reduce_sum(pos[:], prod[:], X))
            link(dve.tensor_copy(pos_i[:, 0], pos[:]))
            link(dve.tensor_scalar(pos_i[:, 1], pos_i[:, 0], 7, None, ALU.logical_shift_right))
            link(dve.tensor_copy(pos_j[:], pos_i[:, 1]))
            link(dve.scalar_tensor_tensor(pos_r[:], pos_j[:], -float(P), pos[:], ALU.mult, ALU.add))
            for n in range(2 * NT):
                t, k = n // 2, n % 2
                if n >= HB:
                    dve.wait_ge(hot_used, n - HB + 1)
                dve.tensor_scalar(hot_r[:, n % HB, :], g.iota_h[:], pos_r[:, k, t:t + 1], None, ALU.is_equal)
                dve.tensor_scalar(hot_j[:, n % HB, :], g.iota_h[:, 0:ECOLS], pos_j[:, k, t:t + 1], g.pair_no[:, k, t % KT:t % KT + 1],
                                  ALU.is_equal, ALU.mult).then_inc(hot_ready, 1)
            link(dve.memset(te_f[:, 0, :], 0.0))
            for e in range(1, E):
                link(dve.scalar_tensor_tensor(te_f[:, e % 2, :], g.iota_r[:, 0:ECOLS], first[3][:, e:e + 1],
                                              te_f[:, (e + 1) % 2, :], ALU.is_ge, ALU.add))
            link(dve.tensor_scalar(shift[0:1, 0:1], first[2][0:1, E - 1:E], float(USUAL), None, ALU.is_gt))
            dve.tensor_copy(g.more[:], shift[0:1, 0:1])
            link(dve.tensor_copy(g.tile_expert[:, 1:ECOLS + 1], te_f[0:1, (E - 1) % 2, :]))
            dve.tensor_copy(g.tile_expert[:, 0:1], g.tile_expert[:, 1:2])
            dve.wait_ge(hot_used, 2 * NT)
            slot = PS[:, 2, 0:NBATCH * ECOLS].rearrange("p (b j) -> p b j", b=NBATCH)
            for b in range(NBATCH):
                last = dve.tensor_scalar(filled[:, b, :], slot[:, b, :], 0.0, float(2 * S * b - 4 * T - 1), ALU.is_gt, ALU.mult)
            link(last)
            link(dve.tensor_tensor(filled[:], filled[:], slot, ALU.add))
            link(dve.reduce_sum(idx_f[:, 0, :], filled[:].rearrange("p b j -> p j b"), X))
            link(dve.tensor_scalar(idx_f[:, 0, :], idx_f[:, 0, :], float(4 * T), None, ALU.add))
            link(dve.tensor_copy(g.idx[:], idx_f[:, 0, :]))
            link(dve.tensor_scalar(g.idx_tok[:], g.idx[:], 1, None, ALU.logical_shift_right))


def experts_phase(nc, g, sem, tmp):
    PS = g.PS
    xs, xsT = tmp("xs", [P, 2, 2 * D], F16), tmp("xsT", [P, 2, 4, P], F16)
    act_s, hid = tmp("act_s", [P, 2, FF]), tmp("hid", [P, FF])
    hid_p, hidT = tmp("hid_p", [P, 2, 2, FF], BF16), tmp("hidT", [P, 2, 8, P], BF16)
    y_s = tmp("y_s", [P, 2, D])
    xs_in, y_out = [sem("xs_in0"), sem("xs_in1")], [sem("y_out0"), sem("y_out1")]
    zeroed, x_turned, x_copied, up_mm = sem("zeroed"), sem("x_turned"), sem("x_copied"), sem("up_mm")
    silu_done, hid_ready, hid_turned = sem("silu_done"), sem("hid_ready"), sem("hid_turned")
    hidT_ready, y_mm, y_copied, y_free = sem("hidT_ready"), sem("y_mm"), sem("y_copied"), sem("y_free")
    hid_step = sem("hid_step")
    XB, HTB, YB = 0, 5, (6, 7)

    def up_bank(k):
        return 1 + 2 * k

    def steps(eng, body, end):
        more = eng.value_load(g.more[0:1, 0:1], min_val=0, max_val=1)
        with eng.Fori(0, USUAL // 2) as i:
            body(i)
        with eng.If(more > 0):
            with eng.Fori(USUAL // 2, ETILES // 2) as i:
                body(i)
            end(ETILES)
        with eng.If(more < 1):
            end(USUAL)

    with nc.Block() as block:
        @block.sync
        def _(sp):
            sp.sem_inc(y_free, FREE + 1)

            def relay(i):
                for k in range(2):
                    sp.wait_ge(y_out[k], i * 16 + 16)
                    sp.sem_inc(y_free, 1)

            def end(tiles):
                pass

            steps(sp, relay, end)

        @block.gpsimd
        def _(pool):
            def gather(j):
                pool.indirect_dma_start(xs[:, j % 2, :], None, g.xrows,
                                        bass.IndirectOffsetOnAxis(g.idx_tok[:, j:j + 1].bitcast(U32), 0),
                                        bounds_check=T - 1, oob_is_err=False).then_inc(xs_in[j % 2], 16)

            pool.wait_ge(zeroed, 1)
            gather(0)
            gather(1)

            def scatter(m):
                pool.wait_ge(y_copied, m + 2 + FREE)
                pool.indirect_dma_start(g.ypair, bass.IndirectOffsetOnAxis(g.idx[:, m:m + 1].bitcast(U32), 0),
                                        y_s[:, m % 2, :], None,
                                        bounds_check=2 * T - 1, oob_is_err=False).then_inc(y_out[m % 2], 16)

            def ahead(first, last):
                for j in range(first, last):
                    pool.wait_ge(x_turned, j - 1)
                    gather(j)
                    if j >= 5:
                        scatter(j - 5)

            def end(tiles):
                for m in range(tiles - 3, tiles):
                    scatter(m)
                for k in range(2):
                    pool.wait_ge(y_out[k], 16 * (tiles // 2))

            more = pool.value_load(g.more[0:1, 0:1], min_val=0, max_val=1)
            ahead(2, USUAL + 2)
            with pool.If(more > 0):
                ahead(USUAL + 2, ETILES + 2)
                end(ETILES)
            with pool.If(more < 1):
                end(USUAL)

        @block.tensor
        def _(pe):
            def turn_x(k, arrived, copied):
                pe.wait_ge(xs_in[k], arrived)
                if copied is not None:
                    pe.wait_ge(x_copied, copied)
                for c in range(4):
                    last = pe.transpose(PS[:, XB, :].bitcast(F16)[:, P * c:P * c + P], xs[:, k, P * c:P * c + P], g.identh[:])
                last.then_inc(x_turned, 1)

            def up(k, e, copied, free):
                pe.wait_ge(x_copied, copied)
                pe.wait_ge(hid_ready, free)
                for half in range(2):
                    terms = [(c, a, w) for c in range(2) for a, w in ((0, 0), (0, 1), (1, 0))]
                    for n, (c, a, w) in enumerate(terms):
                        last = pe.matmul(PS[:, up_bank(k) + half, :], xsT[:, k, 2 * a + c, :],
                                         g.w13_p[:, w, c, ds(e, 1), FF * half:FF * half + FF].rearrange("p e f -> p (e f)"),
                                         start=n == 0, stop=n == len(terms) - 1)
                last.then_inc(up_mm, 1)

            def turn_hidden(k, ready, free):
                pe.wait_ge(hid_ready, ready)
                pe.wait_ge(hidT_ready, free)
                for a in range(2):
                    for c in range(4):
                        n = 4 * a + c
                        last = pe.transpose(PS[:, HTB, :].bitcast(BF16)[:, P * n:P * n + P],
                                            hid_p[:, k, a, P * c:P * c + P], g.identb[:])
                last.then_inc(hid_turned, 1)

            def down(k, e, ready, free):
                pe.wait_ge(hidT_ready, ready)
                pe.wait_ge(y_copied, free)
                terms = [(c, a, w) for c in range(4) for a, w in ((0, 0), (0, 1), (1, 0))]
                for n, (c, a, w) in enumerate(terms):
                    last = pe.matmul(PS[:, YB[k], 0:D], hidT[:, k, 4 * a + c, :],
                                     g.w2_p[:, w, c, ds(e, 1), :].rearrange("p e d -> p (e d)"),
                                     start=n == 0, stop=n == len(terms) - 1)
                last.then_inc(y_mm, 1)

            def expert(col):
                return pe.value_load(g.tile_expert[0:1, ds(col, 1) if not isinstance(col, int) else slice(col, col + 1)],
                                     min_val=0, max_val=E - 1)

            pe.sem_inc(hid_turned, FREE)
            pe.sem_inc(y_mm, FREE)
            pe.wait_ge(zeroed, 2)
            turn_x(0, 16, None)
            turn_x(1, 16, 1)
            up(0, expert(1), 1, FREE)

            def body(i):
                for k in range(2):
                    j = i * 2 + k
                    up(1 - k, expert(j + 2), j + 2, j + FREE)
                    turn_x(k, i * 16 + 32, j + 2)
                    turn_hidden(k, j + 1 + FREE, j + FREE)
                    down(1 - k, expert(j), j + FREE, j - 1 + FREE)

            def end(tiles):
                down(1, expert(tiles), tiles + FREE, tiles - 1 + FREE)

            steps(pe, body, end)

        @block.scalar
        def _(act):
            def copy_x(k, turned, used):
                act.wait_ge(x_turned, turned)
                if used is not None:
                    act.wait_ge(up_mm, used)
                act.copy(xsT[:, k].rearrange("p c q -> p (c q)"), PS[:, XB, :].bitcast(F16)[:, 0:4 * P]).then_inc(x_copied, 1)

            def silu(k, up_done, free):
                act.wait_ge(up_mm, up_done)
                act.wait_ge(hid_ready, free)
                act.activation(act_s[:, k, :], PS[:, up_bank(k), :], ACT.Silu).then_inc(silu_done, 1)

            def copy_y(k, ready, free):
                act.wait_ge(y_mm, ready)
                act.wait_ge(y_free, free)
                act.copy(y_s[:, k, :], PS[:, YB[k], 0:D]).then_inc(y_copied, 1)

            act.sem_inc(y_copied, FREE)
            copy_x(0, 1, None)
            copy_x(1, 2, None)
            silu(0, 1, FREE)

            def body(i):
                for k in range(2):
                    j = i * 2 + k
                    silu(1 - k, j + 2, j + FREE)
                    copy_x(k, j + 3, j + 1)
                    copy_y(1 - k, j + 1 + FREE, j - 2 + FREE + 1)

            def end(tiles):
                copy_y(1, tiles + 1 + FREE, tiles - 2 + FREE + 1)

            steps(act, body, end)

        @block.vector
        def _(dve):
            def hidden(k, n, free):
                dve.wait_ge(silu_done, n + 1)
                dve.wait_ge(hid_turned, free)
                dve.tensor_tensor(hid[:], act_s[:, k, :], PS[:, up_bank(k) + 1, :], ALU.mult).then_inc(hid_step, 1)
                dve.wait_ge(hid_step, n * 2 + 1)
                dve.tensor_copy(hid_p[:, k, 0, :], hid[:]).then_inc(hid_step, 1)
                dve.wait_ge(hid_step, n * 2 + 2)
                dve.tensor_tensor(hid_p[:, k, 1, :], hid[:], hid_p[:, k, 0, :], ALU.subtract).then_inc(hid_ready, 1)
                dve.wait_ge(hid_ready, n + 1 + FREE)

            dve.memset(xs[:], 0.0).then_inc(zeroed, 1)
            dve.memset(hidT[:], 0.0).then_inc(zeroed, 1)
            dve.sem_inc(hid_ready, FREE)
            dve.sem_inc(hidT_ready, FREE)
            hidden(0, 0, FREE)

            def body(i):
                for k in range(2):
                    j = i * 2 + k
                    dve.wait_ge(hid_turned, j + 1 + FREE)
                    dve.wait_ge(y_mm, j + FREE)
                    dve.tensor_copy(hidT[:, k].rearrange("p c q -> p (c q)"), PS[:, HTB, :].bitcast(BF16)).then_inc(hidT_ready, 1)
                    hidden(1 - k, j + 1, j + FREE)

            def end(tiles):
                pass

            steps(dve, body, end)


def output_phase(nc, g, out, sem, tmp):
    CH, RING = 4, 4
    y = tmp("y_in", [P, RING, CH, 2, D])
    y_in = [sem(f"y_in{k}") for k in range(RING)]
    added, summed, stored = sem("added"), sem("summed"), sem("stored")
    rows = g.ypair.rearrange("(t p k) d -> p t (k d)", p=P, k=2)
    out_rows = out.rearrange("b (t p) d -> p (b t) d", p=P)

    with nc.Block() as block:
        @block.sync
        def _(sp):
            for n in range(NT // CH):
                if n >= RING:
                    sp.wait_ge(summed, n - RING + 1)
                sp.dma_start(y[:, n % RING].rearrange("p t k d -> p t (k d)"), rows[:, CH * n:CH * n + CH]).then_inc(y_in[n % RING], 16)

        @block.vector
        def _(dve):
            for n in range(NT // CH):
                dve.wait_ge(y_in[n % RING], 16 * (n // RING + 1))
                for k in range(2):
                    if k:
                        dve.wait_ge(added, n + 1)
                    for i in range(CH):
                        t = CH * n + i
                        last = dve.scalar_tensor_tensor(g.h1[:, t, :], y[:, n % RING, i, k, :], g.wgt[:, k, t:t + 1],
                                                        g.h1[:, t, :], ALU.mult, ALU.add)
                    last.then_inc(summed if k else added, 1)

        @block.scalar
        def _(act):
            for n in range(NT // CH):
                act.wait_ge(summed, n + 1)
                act.dma_start(out_rows[:, CH * n:CH * n + CH], g.h1[:, CH * n:CH * n + CH, :]).then_inc(stored, 16)
            act.wait_ge(stored, 16 * (NT // CH))


def tower(nc, ins, out):
    with ExitStack() as whole:
        def held(name, shape, dt=F32):
            return whole.enter_context(nc.sbuf_tensor(name, shape, dt))

        def sem(name):
            return whole.enter_context(nc.semaphore(name))

        g = Parts()
        g.PS = whole.enter_context(nc.psum_tensor("PS", [P, 8, 512], F32))
        g.xrows = nc.dram_tensor("xrows", (T, 2 * D), F16, kind="Internal").ap()
        g.ypair = nc.dram_tensor("ypair", (2 * T, D), F32, kind="Internal").ap()
        g.ident = held("ident", [P, P])
        g.identb = held("identb", [P, P], BF16)
        g.identh = held("identh", [P, P], F16)
        g.fold_sel = held("fold_sel", [P, 2, 32])
        g.tri = held("tri", [P, P])
        g.ones = held("ones", [P, P])
        g.iota_i = held("iota_i", [P, P], I32)
        g.iota_r, g.iota_h = held("iota_r", [P, P]), held("iota_h", [P, P], F16)
        g.pair_no = held("pair_no", [P, 2, KT])
        g.iota_p = held("iota_p", [P, 1], I32)
        g.part_r = held("part_r", [P, 1])
        g.part_c = held("part_c", [P, 2])
        g.flag, g.more = held("flag", [1, 1], I32), held("more", [1, 1], I32)
        g.idx, g.idx_tok = held("idx", [P, ECOLS], I32), held("idx_tok", [P, ECOLS], I32)
        g.tile_expert = held("tile_expert", [1, ECOLS + 1], I32)
        g.wgt, g.mean, g.var = held("wgt", [P, 2, NT]), held("mean", [P, NT]), held("var2", [P, NT])
        g.iota_e = g.iota_r[:, 0:E]
        g.x_in, g.gathered = sem("x_in"), sem("gathered")

        def phase(run, *args):
            with ExitStack() as own:
                run(*args, sem, lambda name, shape, dt=F32: own.enter_context(nc.sbuf_tensor(name, shape, dt)))

        g.h1 = held("h1", [P, NT, D])

        with ExitStack() as to_residual:
            def kept(name, shape, dt=F32):
                return to_residual.enter_context(nc.sbuf_tensor(name, shape, dt))

            g.pair, g.resid = kept("pair", [P, KT, 2 * D]), kept("resid", [XROWS, D])
            g.z, g.xT = kept("z", [P, NBATCH + 1, H, NJ // 2, NB]), kept("xT", [XROWS, T])
            g.z_blk = kept("z_blk", [P, NT, P])
            with ExitStack() as attending:
                def here(name, shape, dt=F32):
                    return attending.enter_context(nc.sbuf_tensor(name, shape, dt))

                g.xi = here("xi", [P, NT], I32)
                g.cw = here("cw", [P, NT, NB])
                g.vb = here("vb", [P, NB * NB])
                g.kr = here("kr", [XROWS, H * PART])
                g.krb, g.xq = here("krb", [P, H * PART], BF16), here("xq", [P, T + S], BF16)
                g.xtok = here("xtok", [P, NT, XROWS])
                g.akz = here("akz", [P, 4, T + 2 * P], BF16)
                g.va = here("va", [P, KT, 4, PART])
                with ExitStack() as setting_up:
                    def early(name, shape):
                        return setting_up.enter_context(nc.sbuf_tensor(name, shape, F32))

                    g.woT_s, g.m_blk = early("woT_s", [P, 2, D]), early("m_blk", [P, 2, H, NJ, NB])
                    g.bias_wide = early("bias_wide", [P, H, NR])
                    phase(weights_phase, nc, g, ins)
                    phase(tokens_phase, nc, g)
                phase(row_maxima_phase, nc, g)
                phase(attention_phase, nc, g)
            phase(residual_phase, nc, g)
        g.w13_p, g.w2_p = held("w13_p", [P, 2, 2, E, 2 * FF], BF16), held("w2_p", [P, 2, 4, E, D], BF16)
        phase(routing_phase, nc, g, ins["router"], ins["w13"], ins["w2"])
        phase(experts_phase, nc, g)
        phase(output_phase, nc, g, out)


def kernel(**inputs):
    import numpy as np
    import concourse.bacc as bacc
    from concourse import mybir as mb
    from concourse.bass_utils import run_bass_kernel_spmd as run

    given = {k: np.asarray(v) for k, v in inputs.items()}
    bv, bo = given["L0_attn_bv"], given["L0_attn_bo"]
    arrays = {
        "x_t": np.ascontiguousarray(given["x"].reshape(NT, P).T),
        "coeff": np.ascontiguousarray(given["L0_tok_coeff_weight"]),
        "bases": np.ascontiguousarray(given["L0_tok_base_embed_weight"]),
        "lbias": np.ascontiguousarray(given["L0_tok_lang_bias"]),
        "wvT": np.ascontiguousarray(given["L0_attn_Wv"].T),
        "bv_col": np.ascontiguousarray(bv.reshape(2, P).T),
        "woT": np.ascontiguousarray(given["L0_attn_Wo"].T),
        "bo": np.ascontiguousarray(bo.reshape(1, D)),
        "router": np.ascontiguousarray(given["L0_ffn_moe_router"]),
        "w13": np.ascontiguousarray(given["L0_ffn_moe_w13"]),
        "w2": np.ascontiguousarray(given["L0_ffn_moe_w2"]),
    }
    nc = bacc.Bacc("TRN2", target_bir_lowering=False, num_devices=1)
    ins = {name: nc.dram_tensor(name, a.shape, mb.dt.from_np(a.dtype), kind="ExternalInput").ap()
           for name, a in arrays.items()}
    out = nc.dram_tensor("out", (NBATCH, S, D), F32, kind="ExternalOutput").ap()
    tower(nc, ins, out)
    r = run(nc, [arrays], core_ids=[0])
    return r.results[0]["out"]
```
